# Optimizing a Trainium2 kernel written in Bass

```python
import numpy as np
import jax
import jax.numpy as jnp

def _softmax(x, axis=-1):
    return jax.nn.softmax(x, axis=axis)

def _gelu(x):
    return jax.nn.gelu(x, approximate=True)

def _silu(x):
    return jax.nn.silu(x)

def _sigmoid(x):
    return jax.nn.sigmoid(x)

def _layernorm(x, axis=-1, eps=1e-05):
    m = jnp.mean(x, axis=axis, keepdims=True)
    v = jnp.var(x, axis=axis, keepdims=True)
    return (x - m) / jnp.sqrt(v + eps)

def _scatter_add(tgt, idx, src, axis=0):
    return tgt.at[idx].add(src)

def _segment_sum(src, seg, n):
    return jax.ops.segment_sum(src, seg, n)
kernel_name = 'mk_gnn_preln_d4_gnn_r16_9fab94'

def setup_inputs(seed: int=0):
    np.random.seed(seed)
    _w = jnp.asarray

    def _rec_inputs():
        import jax
        import jax.numpy as jnp
        _gk = jax.random.key(seed)
        x = -0.0003713 + 1 * jax.random.normal(jax.random.fold_in(_gk, 1), (6250, 128), jnp.float32)
        src = jax.random.randint(jax.random.fold_in(_gk, 2), (100000,), 0, 6250, jnp.int32)
        dst = jax.random.randint(jax.random.fold_in(_gk, 3), (100000,), 0, 6250, jnp.int32)
        _o = jnp.argsort(dst, stable=True)
        src = src[_o]
        dst = dst[_o]
        edge_attr_128 = -6.47781e-05 + 0.999943 * jax.random.normal(jax.random.fold_in(_gk, 12), (100000, 128), jnp.float32)
        edge_weight = jax.random.uniform(jax.random.fold_in(_gk, 14), (100000,), jnp.float32, 0.0, 0.0625)
        return (x, src, dst, edge_attr_128, edge_weight)
    x, src, dst, edge_attr_128, edge_weight = _rec_inputs()

    def _L0_gnn_setup():
        import jax, jax.numpy as jnp
        import numpy as np
        N_NODES = 6250
        key = jax.random.key(seed)
        k1, k2, k3, k4, k5 = jax.random.split(key, 5)
        E = 100000
        IN_F, OUT_F = (128, 128)
        x = jax.random.normal(k1, (N_NODES, IN_F), dtype=jnp.float32)
        src = jax.random.randint(k2, (E,), 0, N_NODES, dtype=jnp.int64)
        dst = jax.random.randint(k3, (E,), 0, N_NODES, dtype=jnp.int64)
        stdv = 1.0 / np.sqrt(OUT_F)
        weight = jax.random.uniform(k4, (IN_F, OUT_F), dtype=jnp.float32, minval=-stdv, maxval=stdv)
        b = jax.random.uniform(k5, (OUT_F,), dtype=jnp.float32, minval=-stdv, maxval=stdv)
        return {'x': x, 'src': src, 'dst': dst, 'weight': weight, 'b': b}
    _L0_gnn_all = _L0_gnn_setup()
    _L0_gnn_in = {k: v for k, v in _L0_gnn_all.items() if k in ('weight', 'b')}
    del _L0_gnn_all

    def _L1_gnn_setup():
        import jax, jax.numpy as jnp
        import numpy as np
        N = 6250
        E = 100000
        D = 128
        NEG_SLOPE = 0.2
        EPS = 1e-12
        key = jax.random.key(seed)
        k1, k2, k3, k4, k5, k6 = jax.random.split(key, 6)
        ego = jax.random.normal(k1, (N, D), dtype=jnp.float32)
        std = float(np.sqrt(2.0 / (D + D)))
        W1 = jax.random.normal(k2, (D, D), dtype=jnp.float32) * std
        W2 = jax.random.normal(k3, (D, D), dtype=jnp.float32) * std
        b1 = jnp.zeros((1, D), dtype=jnp.float32)
        b2 = jnp.zeros((1, D), dtype=jnp.float32)
        src = jax.random.randint(k4, (E,), 0, N)
        dst = jax.random.randint(k5, (E,), 0, N)
        adj_vals = jax.random.uniform(k6, (E,), dtype=jnp.float32) * (1.0 / 16.0)
        return {'ego_embeddings': ego, 'W1': W1, 'W2': W2, 'b1': b1, 'b2': b2, 'adj_vals': adj_vals, 'src': src, 'dst': dst}
    _L1_gnn_all = _L1_gnn_setup()
    _L1_gnn_in = {k: v for k, v in _L1_gnn_all.items() if k in ('W1', 'W2', 'b1', 'b2')}
    del _L1_gnn_all

    def _L2_gnn_setup():
        import jax, jax.numpy as jnp
        import numpy as np
        LOG2 = float(np.log(2.0))

        def ssp(x):
            return jax.nn.softplus(x) - LOG2

        def linear(x, W, b):
            return x @ W.T + b
        N, E, H, F = (6250, 100000, 128, 128)
        key = jax.random.key(seed)
        ks = jax.random.split(key, 14)
        s = 1.0 / np.sqrt(H)
        inp = {'h': jax.random.normal(ks[0], (N, H), dtype=jnp.float32), 'e': jax.random.normal(ks[1], (E, F), dtype=jnp.float32), 'W_node': jax.random.uniform(ks[2], (H, H), minval=-s, maxval=s), 'b_node': jax.random.uniform(ks[3], (H,), minval=-s, maxval=s), 'W_e1': jax.random.uniform(ks[4], (H, F), minval=-s, maxval=s), 'b_e1': jax.random.uniform(ks[5], (H,), minval=-s, maxval=s), 'W_e2': jax.random.uniform(ks[6], (H, H), minval=-s, maxval=s), 'b_e2': jax.random.uniform(ks[7], (H,), minval=-s, maxval=s), 'W_fc1': jax.random.uniform(ks[8], (H, H), minval=-s, maxval=s), 'b_fc1': jax.random.uniform(ks[9], (H,), minval=-s, maxval=s), 'W_fc2': jax.random.uniform(ks[10], (H, H), minval=-s, maxval=s), 'b_fc2': jax.random.uniform(ks[11], (H,), minval=-s, maxval=s), 'src': jax.random.randint(ks[12], (E,), 0, N, dtype=jnp.int32), 'dst': jax.random.randint(ks[13], (E,), 0, N, dtype=jnp.int32)}
        return inp
    _L2_gnn_all = _L2_gnn_setup()
    _L2_gnn_in = {k: v for k, v in _L2_gnn_all.items() if k in ('W_node', 'b_node', 'W_e1', 'b_e1', 'W_e2', 'b_e2', 'W_fc1', 'b_fc1', 'W_fc2', 'b_fc2')}
    del _L2_gnn_all

    def _L3_gnn_setup():
        import jax, jax.numpy as jnp
        import numpy as np
        N_NODES = 3125
        N_EDGES = 25000
        D_MODEL = 128
        HEADS = 4
        NEG_SLOPE = 0.2
        LN_EPS = 1e-05

        def _gat_forward(x, edge_index, W, att_src, att_dst, bias):
            N = x.shape[0]
            h = (x @ W).reshape(N, HEADS, D_MODEL)
            a_src = jnp.einsum('nhc,hc->nh', h, att_src)
            a_dst = jnp.einsum('nhc,hc->nh', h, att_dst)
            loop = jnp.arange(N, dtype=edge_index.dtype)
            src = jnp.concatenate([edge_index[0], loop])
            dst = jnp.concatenate([edge_index[1], loop])
            e = jax.nn.leaky_relu(a_src[src] + a_dst[dst], NEG_SLOPE)
            m = jax.ops.segment_max(e, dst, num_segments=N)
            w = jnp.exp(e - m[dst])
            z = jax.ops.segment_sum(w, dst, num_segments=N)
            alpha = w / z[dst]
            msg = h[src] * alpha[:, :, None]
            out = jax.ops.segment_sum(msg, dst, num_segments=N)
            return out.mean(axis=1) + bias
        key = jax.random.key(seed)
        ks = jax.random.split(key, 6)
        x = jax.random.normal(ks[0], (N_NODES, D_MODEL), dtype=jnp.float32)
        edge_index = jax.random.randint(ks[1], (2, N_EDGES), 0, N_NODES, dtype=jnp.int64)
        sc = 1.0 / np.sqrt(D_MODEL)
        W = jax.random.normal(ks[2], (D_MODEL, HEADS * D_MODEL), dtype=jnp.float32) * sc
        att_src = jax.random.normal(ks[3], (HEADS, D_MODEL), dtype=jnp.float32) * sc
        att_dst = jax.random.normal(ks[4], (HEADS, D_MODEL), dtype=jnp.float32) * sc
        bias = jnp.zeros((D_MODEL,), dtype=jnp.float32)
        ln_gamma = jnp.ones((D_MODEL,), dtype=jnp.float32)
        ln_beta = jnp.zeros((D_MODEL,), dtype=jnp.float32)
        return {'x': x, 'edge_index': edge_index, 'W': W, 'att_src': att_src, 'att_dst': att_dst, 'bias': bias, 'ln_gamma': ln_gamma, 'ln_beta': ln_beta}
    _L3_gnn_all = _L3_gnn_setup()
    _L3_gnn_in = {k: v for k, v in _L3_gnn_all.items() if k in ('W', 'att_src', 'att_dst', 'bias', 'ln_gamma', 'ln_beta')}
    del _L3_gnn_all
    return {'x': x, 'src': src, 'dst': dst, 'edge_attr_128': edge_attr_128, 'edge_weight': edge_weight, 'L0_gnn_weight': _L0_gnn_in['weight'], 'L0_gnn_b': _L0_gnn_in['b'], 'L1_gnn_W1': _L1_gnn_in['W1'], 'L1_gnn_W2': _L1_gnn_in['W2'], 'L1_gnn_b1': _L1_gnn_in['b1'], 'L1_gnn_b2': _L1_gnn_in['b2'], 'L2_gnn_W_node': _L2_gnn_in['W_node'], 'L2_gnn_b_node': _L2_gnn_in['b_node'], 'L2_gnn_W_e1': _L2_gnn_in['W_e1'], 'L2_gnn_b_e1': _L2_gnn_in['b_e1'], 'L2_gnn_W_e2': _L2_gnn_in['W_e2'], 'L2_gnn_b_e2': _L2_gnn_in['b_e2'], 'L2_gnn_W_fc1': _L2_gnn_in['W_fc1'], 'L2_gnn_b_fc1': _L2_gnn_in['b_fc1'], 'L2_gnn_W_fc2': _L2_gnn_in['W_fc2'], 'L2_gnn_b_fc2': _L2_gnn_in['b_fc2'], 'L3_gnn_W': _L3_gnn_in['W'], 'L3_gnn_att_src': _L3_gnn_in['att_src'], 'L3_gnn_att_dst': _L3_gnn_in['att_dst'], 'L3_gnn_bias': _L3_gnn_in['bias'], 'L3_gnn_ln_gamma': _L3_gnn_in['ln_gamma'], 'L3_gnn_ln_beta': _L3_gnn_in['ln_beta']}

def reference(x, src, dst, edge_attr_128, edge_weight, L0_gnn_weight, L0_gnn_b, L1_gnn_W1, L1_gnn_W2, L1_gnn_b1, L1_gnn_b2, L2_gnn_W_node, L2_gnn_b_node, L2_gnn_W_e1, L2_gnn_b_e1, L2_gnn_W_e2, L2_gnn_b_e2, L2_gnn_W_fc1, L2_gnn_b_fc1, L2_gnn_W_fc2, L2_gnn_b_fc2, L3_gnn_W, L3_gnn_att_src, L3_gnn_att_dst, L3_gnn_bias, L3_gnn_ln_gamma, L3_gnn_ln_beta):
    import jax
    import jax.numpy as jnp

    def _L0_gnn_ref(x, src, dst, weight, b):
        import jax, jax.numpy as jnp
        import numpy as np
        N_NODES = 6250
        support = jnp.matmul(x, weight)
        self_idx = jnp.arange(N_NODES, dtype=src.dtype)
        src_all = jnp.concatenate([src, self_idx])
        dst_all = jnp.concatenate([dst, self_idx])
        agg = jax.ops.segment_sum(support[src_all], dst_all, num_segments=N_NODES)
        cnt = jax.ops.segment_sum(jnp.ones_like(src_all, dtype=support.dtype), dst_all, num_segments=N_NODES)
        out = agg / cnt[:, None]
        return out + b

    def _L1_gnn_ref(ego_embeddings, W1, W2, b1, b2, adj_vals, src, dst):
        import jax, jax.numpy as jnp
        import numpy as np
        N = 6250
        E = 100000
        D = 128
        NEG_SLOPE = 0.2
        EPS = 1e-12
        msgs = ego_embeddings[src] * adj_vals[:, None]
        lap = jax.ops.segment_sum(msgs, dst, num_segments=ego_embeddings.shape[0])
        first = (ego_embeddings + lap) @ W1 + b1
        second = ego_embeddings * lap @ W2 + b2
        out = jax.nn.leaky_relu(first + second, negative_slope=NEG_SLOPE)
        norm = jnp.sqrt(jnp.sum(out * out, axis=1, keepdims=True))
        return out / jnp.maximum(norm, EPS)

    def _L2_gnn_ref(h, e, W_node, b_node, W_e1, b_e1, W_e2, b_e2, W_fc1, b_fc1, W_fc2, b_fc2, src, dst):
        import jax, jax.numpy as jnp
        import numpy as np
        LOG2 = float(np.log(2.0))

        def ssp(x):
            return jax.nn.softplus(x) - LOG2

        def linear(x, W, b):
            return x @ W.T + b
        N = h.shape[0]
        hn = linear(h, W_node, b_node)
        ef = ssp(linear(e, W_e1, b_e1))
        ef = ssp(linear(ef, W_e2, b_e2))
        m = hn[src] * ef
        agg = jax.ops.segment_sum(m, dst, num_segments=N)
        out = ssp(linear(agg, W_fc1, b_fc1))
        out = linear(out, W_fc2, b_fc2)
        return out

    def _L3_gnn_ref(x, edge_index, W, att_src, att_dst, bias, ln_gamma, ln_beta):
        import jax, jax.numpy as jnp
        import numpy as np
        N_NODES = 3125
        N_EDGES = 25000
        D_MODEL = 128
        HEADS = 4
        NEG_SLOPE = 0.2
        LN_EPS = 1e-05

        def _gat_forward(x, edge_index, W, att_src, att_dst, bias):
            N = x.shape[0]
            h = (x @ W).reshape(N, HEADS, D_MODEL)
            a_src = jnp.einsum('nhc,hc->nh', h, att_src)
            a_dst = jnp.einsum('nhc,hc->nh', h, att_dst)
            loop = jnp.arange(N, dtype=edge_index.dtype)
            src = jnp.concatenate([edge_index[0], loop])
            dst = jnp.concatenate([edge_index[1], loop])
            e = jax.nn.leaky_relu(a_src[src] + a_dst[dst], NEG_SLOPE)
            m = jax.ops.segment_max(e, dst, num_segments=N)
            w = jnp.exp(e - m[dst])
            z = jax.ops.segment_sum(w, dst, num_segments=N)
            alpha = w / z[dst]
            msg = h[src] * alpha[:, :, None]
            out = jax.ops.segment_sum(msg, dst, num_segments=N)
            return out.mean(axis=1) + bias
        out = _gat_forward(x, edge_index, W, att_src, att_dst, bias)
        mu = out.mean(axis=-1, keepdims=True)
        var = ((out - mu) ** 2).mean(axis=-1, keepdims=True)
        ln = ln_gamma * (out - mu) * jax.lax.rsqrt(var + LN_EPS) + ln_beta
        return jax.nn.relu(ln) + x
    edge_index = jnp.stack([src, dst])
    h = jnp.maximum(_layernorm(x, axis=-1), 0.0)
    x = x + _L0_gnn_ref(h, src, dst, L0_gnn_weight, L0_gnn_b)
    h = jnp.maximum(_layernorm(x, axis=-1), 0.0)
    x = x + _L1_gnn_ref(h, L1_gnn_W1, L1_gnn_W2, L1_gnn_b1, L1_gnn_b2, edge_weight, src, dst)
    h = jnp.maximum(_layernorm(x, axis=-1), 0.0)
    x = x + _L2_gnn_ref(h, edge_attr_128, L2_gnn_W_node, L2_gnn_b_node, L2_gnn_W_e1, L2_gnn_b_e1, L2_gnn_W_e2, L2_gnn_b_e2, L2_gnn_W_fc1, L2_gnn_b_fc1, L2_gnn_W_fc2, L2_gnn_b_fc2, src, dst)
    h = jnp.maximum(_layernorm(x, axis=-1), 0.0)
    x = x + _L3_gnn_ref(h, edge_index, L3_gnn_W, L3_gnn_att_src, L3_gnn_att_dst, L3_gnn_bias, L3_gnn_ln_gamma, L3_gnn_ln_beta)
    return x

_drawn_inputs = setup_inputs


def setup_inputs(seed=0):
    import zlib

    import numpy as np

    out = dict(_drawn_inputs(seed))
    spreads = {'L1_gnn_b1': (0.0, 0.8),
     'L1_gnn_b2': (0.0, 0.702),
     'L3_gnn_bias': (0.0, 0.1),
     'L3_gnn_ln_gamma': (1.0, 0.2),
     'L3_gnn_ln_beta': (0.0, 0.1)}
    factors = {'edge_attr_128': 2.772,
     'edge_weight': 8.0,
     'L1_gnn_W2': 3.562,
     'L2_gnn_b_node': 8.0,
     'L2_gnn_W_e1': 2.78,
     'L2_gnn_b_e1': 8.0,
     'L2_gnn_b_e2': 3.451,
     'L2_gnn_b_fc1': 3.74,
     'L3_gnn_att_dst': 3.65}
    for name, (base, spread) in spreads.items():
        noise = np.random.default_rng([zlib.crc32(name.encode()), seed]).standard_normal(out[name].shape)
        drawn = base * np.exp(spread * noise) if base else spread * noise
        out[name] = jnp.asarray(drawn.astype(out[name].dtype))
    for name, factor in factors.items():
        out[name] = (out[name] * factor).astype(out[name].dtype)
    return out
```

```python
from contextlib import ExitStack

import numpy as np

import concourse.bass as bass
from concourse import mybir

F32 = mybir.dt.float32
I32 = mybir.dt.int32
ALU = mybir.AluOpType
ACT = mybir.ActivationFunctionType
AX = mybir.AxisListType
ENG = mybir.EngineType

N, E, D = 6250, 100000, 128
P = 128
NT = -(-N // P)
NP = NT * P
LAST = N - (NT - 1) * P
ET = -(-E // P)
HEADS = 4
LOG2 = float(np.log(2.0))
FAR = -1.0e30
EXP_LN = "natural_log_exp_and_others"

WA, WB = 256, 32
BA, BB = -(-N // WA), -(-N // WB)
QUAD = 4
RINGA, RINGB = 4, 6
STEPSA = QUAD * RINGA * -(-(ET + BA - 1) // (QUAD * RINGA))
STEPSB = QUAD * RINGB * -(-(ET + BB - 1) // (QUAD * RINGB))
ITERSA, ITERSB = STEPSA // (QUAD * RINGA), STEPSB // (QUAD * RINGB)
TABA = P * -(-(STEPSA + QUAD * RINGA) // P)
TABB = P * -(-(STEPSB + QUAD * RINGB) // P)
GB = 2
PB = BB // GB
assert BB % GB == 0
ROWS = TABA
NODESA = BA * WA
GRP = 512
GROUPS = 2 * 2 * ITERSA
ECOLS = (GROUPS + 2) * GRP
ROW3 = HEADS + D + 1
ACC3 = D + 1


def const_layout():
    at, out = 0, {}
    for name, width in (("ident", P), ("iota", WA), ("limA", 2), ("limB", 4 * GB), ("stepcol", TABB // P), ("ones", P)):
        out[name] = (at, at + width)
        at += width
    return out, at


def const_table():
    cols, width = const_layout()
    c = np.zeros((P, width), np.float32)
    p = np.arange(P, dtype=np.float32)

    def put(name, value):
        a, b = cols[name]
        c[:, a:b] = value

    put("ident", np.eye(P))
    put("iota", np.arange(WA)[None, :])
    put("limA", np.stack([WA * p, p], 1))
    lim = np.zeros((P, GB, 4), np.float32)
    for g in range(GB):
        b = g * PB + p
        lim[:, g] = np.stack([WB * b, b, WB * (b + 1), b + 1], 1)
        lim[b + 1 >= BB, g, 3] = 1.0e6
    put("limB", lim.reshape(P, -1))
    put("stepcol", np.arange(TABB // P)[None, :] * P + p[:, None])
    put("ones", 1.0)
    return c


class Lane:

    def __init__(self, engine, sem):
        self.e, self.sem, self.n = engine, sem, 0

    def did(self, ins):
        self.n += 1
        ins.then_inc(self.sem, 1)
        return (self.sem, self.n)


def need(engine, *marks):
    for sem, value in marks:
        engine.wait_ge(sem, value)


def build(nc, a, out):
    with ExitStack() as ctx:
        def sb(name, shape, dt=F32):
            return ctx.enter_context(nc.sbuf_tensor("t_" + name, shape, dt))

        def sem(name):
            return ctx.enter_context(nc.semaphore(name))

        def dram(name, shape, dt=F32):
            return nc.dram_tensor("d_" + name, shape, dt, kind="Internal").ap()

        pe, dve, act, pool, sp = nc.tensor, nc.vector, nc.scalar, nc.gpsimd, nc.sync
        V = Lane(dve, sem("v_done"))
        A = Lane(act, sem("a_done"))
        T = Lane(pe, sem("t_done"))

        class Load:

            def __init__(self, name):
                self.sem, self.n = sem(name), 0

            def add(self, ins, k=1):
                ins.then_inc(self.sem, 16)
                self.n += 16 * k
                return (self.sem, self.n)

            @property
            def mark(self):
                return (self.sem, self.n)

        cols, cwidth = const_layout()
        cst = sb("cst", [P, cwidth])

        def c_(name):
            x, y = cols[name]
            return cst[:, x:y]

        ident, iota, ones = c_("ident"), c_("iota"), c_("ones")
        x_n = sb("x", [P, NT, D])
        hT = sb("hT", [P, NODESA])
        acc = sb("acc", [P, BB * ACC3])
        work = sb("work", [P, QUAD * RINGA * ACC3 + 2 * QUAD * WA])
        assert QUAD * RINGB * ROW3 <= work.shape[1]
        masks = work[:, QUAD * RINGA * ACC3:].rearrange("p (s k w) -> p s k w", s=2, k=QUAD)
        tabA = sb("tabA", [P, 3, TABA])
        idxA, relA, wgtA = tabA[:, 0, :].bitcast(I32), tabA[:, 1, :], tabA[:, 2, :]
        idxB = sb("idxB", [P, TABB], I32)
        relB = sb("relB", [P, TABB])
        stage = sb("stage", [P, RINGB, QUAD], I32)
        winA, tileA = sb("winA", [1, TABA], I32), sb("tileA", [1, TABA], I32)
        winB = sb("winB", [1, TABB], I32)
        wts = sb("wts", [P, 8, D])
        W0, W1, W2, WN, WE1, WE2, WF1, WF2 = (wts[:, k, :] for k in range(8))
        bias = sb("bias", [1, 5, D])
        bcol = sb("bcol", [P, 8])
        stat = sb("stat", [P, 4, NT])
        small = sb("small", [P, 64])

        XC, SQ = NT * P + 2 * ACC3 + 2, NT * P + 2 * ACC3 + 2 + NP
        MLP = SQ + NT * ROW3
        xc = acc[:, XC:XC + NP]
        sq = acc[:, SQ:SQ + NP]

        def mlp(k, n=1):
            assert MLP + (k + n) * GRP <= BB * ACC3
            return acc[:, MLP + k * GRP:MLP + (k + n) * GRP]

        ps = ctx.enter_context(nc.psum_tensor("ps", [P, 8, 512], F32))

        edge_net = dram("edge_net", [GROUPS * QUAD, P, D])
        T0, T1, T2, T3 = dram("T0", [NP, D + 1]), dram("T1", [NP, D]), dram("T2", [NP, D]), dram("T3", [NP, ROW3])
        scores = dram("scores", [2 * HEADS, NP])
        windows_b = dram("windows_b", [1, TABB])

        ld_c, ld_x, ld_w = Load("ld_c"), Load("ld_x"), Load("ld_w")
        ld_l = Load("ld_l")
        lastb = acc[:, 0:ROWS].bitcast(I32)
        ld_l.add(sp.dma_start(lastb, a["lasts"].to_broadcast([P, ROWS])))
        ld_c.add(sp.dma_start(cst[:], a["consts"]))
        steps = hT[:, 4 * TABB:5 * TABB]
        ld_c.add(sp.dma_start(steps, a["steps"].to_broadcast([P, TABB])))
        x_pad = V.did(dve.memset(x_n[:, NT - 1, :], 0.0))
        for lo in range(0, NT - 1, 12):
            hi = min(lo + 12, NT - 1)
            ld_x.add(sp.dma_start(x_n[:, lo:hi, :], a["x"][lo * P:hi * P, :].rearrange("(t p) d -> p t d", p=P)))
        need(sp, x_pad)
        ld_x.add(sp.dma_start(x_n[0:LAST, NT - 1, :], a["x"][(NT - 1) * P:N, :]))
        for k, name in enumerate(("w0", "w1", "w2", "wnT", "we1T", "we2T", "wf1T", "wf2T")):
            ld_w.add(act.dma_start(wts[:, k, :], a[name]))
        for k, name in enumerate(("b0", "b1a", "b1b", "bn", "bf2")):
            ld_w.add(act.dma_start(bias[:, k, :], a[name]))
        B0, B1, B1B, BN, BF2 = (bias[:, k, :] for k in range(5))
        be2row = sb("be2row", [1, D])
        ld_w.add(act.dma_start(be2row[:], a["be2"]))
        ld_w.add(act.dma_start(bcol[:, 0:1], a["be1"]))
        ld_w.add(act.dma_start(bcol[:, 1:2], a["bf1"]))
        lastf = acc[:, ROWS:2 * ROWS]
        cmp = acc[:, 2 * ROWS:3 * ROWS]
        need(dve, ld_l.mark)
        m = V.did(dve.tensor_copy(lastf, lastb))
        need(dve, m, ld_c.mark)
        la, _ = cols["limA"]
        lb, _ = cols["limB"]
        first = small[:, 0:8]
        starts = [(0, BA, la)] + [(1 + 2 * g + j, PB, lb + 4 * g + 2 * j) for g in range(GB) for j in range(2)]
        for k, n, c in starts:
            m = V.did(dve.tensor_scalar(cmp[0:n, :], lastf[0:n, :], cst[0:n, c:c + 1], None, ALU.is_lt))
            need(dve, m)
            m = V.did(dve.tensor_reduce(first[0:n, k:k + 1], cmp[0:n, :], AX.X, ALU.add))
            need(dve, m)
            m = V.did(dve.tensor_tensor(out=first[0:n, k:k + 1], in0=first[0:n, k:k + 1],
                                        in1=cst[0:n, c + 1:c + 2], op=ALU.add))
            need(dve, m)
        startedA = acc[:, 4000:4000 + TABA]
        startedB = [acc[:, 5000 + 1100 * g:5000 + 1100 * g + TABB] for g in range(GB)]
        V.did(dve.tensor_scalar(startedA[0:BA, :], steps[0:BA, 0:TABA], first[0:BA, 0:1], None, ALU.is_ge))
        onehot = [hT[:, 1100 * g:1100 * g + TABB] for g in range(GB)]
        for g in range(GB):
            k = 1 + 2 * g
            V.did(dve.tensor_scalar(startedB[g][0:PB, :], steps[0:PB, :], first[0:PB, k:k + 1], None,
                                    ALU.is_ge))
            m = V.did(dve.tensor_scalar(onehot[g][0:PB, :], steps[0:PB, :], first[0:PB, k + 1:k + 2], None,
                                        ALU.is_lt))
            need(dve, m)
            m = V.did(dve.tensor_tensor(out=onehot[g][0:PB, :], in0=onehot[g][0:PB, :],
                                        in1=startedB[g][0:PB, :], op=ALU.mult))
        need(pe, m)
        halfA, halfB = TABA // 2, TABB // 2
        bcA = ps[:, 0:2, 0:halfA]
        bcB = ps[:, 2:4, 0:halfB]
        for h in range(2):
            pe.matmul(ps[:, h, 0:halfA], ones[0:BA, :], startedA[0:BA, h * halfA:(h + 1) * halfA],
                      start=True, stop=True)
            for g in range(GB):
                pe.matmul(ps[:, 2 + h, 0:halfB], ones[0:PB, :], startedB[g][0:PB, h * halfB:(h + 1) * halfB],
                          start=(g == 0), stop=(g == GB - 1))
        CA, CB = TABA // P, TABB // P
        for c in range(CA):
            pe.matmul(ps[:, 4, c:c + 1], startedA[0:BA, c * P:(c + 1) * P], ones[0:BA, 0:1], start=True, stop=True)
        for c in range(CB):
            for g in range(GB):
                last = pe.matmul(ps[:, 4, 16 + c:17 + c], startedB[g][0:PB, c * P:(c + 1) * P], ones[0:PB, 0:1],
                                 start=(g == 0), stop=(g == GB - 1))
        counted = T.did(last)
        need(dve, counted)

        for win, counts in ((winA, bcA), (winB, bcB)):
            V.did(dve.tensor_scalar(win[:].rearrange("p (h n) -> p h n", h=2), counts[0:1], -1.0, None, ALU.add))
        m = V.did(dve.tensor_tensor(
            out=tileA[:].rearrange("p (h n) -> p h n", h=2),
            in0=steps[0:1, 0:TABA].rearrange("p (h n) -> p h n", h=2), in1=bcA[0:1], op=ALU.subtract))
        need(dve, m)
        V.did(dve.tensor_scalar(tileA[:], tileA[:], 1.0, None, ALU.add))
        tcol = sb("tcol", [P, 16], I32)
        wcol = small[:, 16:32]
        tcf = small[:, 32:48]
        for base, n, off, w in ((0, CA, 0, WA), (8, CB, 16, WB)):
            x0, _ = cols["stepcol"]
            m = V.did(dve.tensor_tensor(out=tcf[:, base:base + n], in0=cst[:, x0:x0 + n],
                                        in1=ps[:, 4, off:off + n], op=ALU.subtract))
            need(dve, m)
            V.did(dve.tensor_scalar(tcol[:, base:base + n], tcf[:, base:base + n], 1.0, None, ALU.add))
            wcol_ready = V.did(dve.tensor_scalar(wcol[:, base:base + n], ps[:, 4, off:off + n], 1.0, float(w),
                                                 ALU.subtract, ALU.mult))
        win_f = acc[0:1, 8000:8000 + TABB]
        m = V.did(dve.tensor_copy(win_f.rearrange("p (h n) -> p h n", h=2), bcB[0:1]))
        need(sp, m)
        kept = Load("kept")
        kept.add(sp.dma_start(windows_b, win_f))
        need(sp, kept.mark)

        need(pool, wcol_ready)
        got = [sem(f"got{k}") for k in range(2)]
        edges = acc[:, 9100:9100 + 3 * 2 * 2 * P].bitcast(I32)
        wraw = acc[:, 10900:10900 + 2 * P]
        ef = acc[:, 11200:11200 + 4 * P].rearrange("p (s n) -> p s n", s=2)
        chunks = [("A", c) for c in range(CA)] + [("B", c) for c in range(CB)]
        turned, freed = {}, {}
        n_got = [0, 0]
        for j, (path, c) in enumerate(chunks):
            k = j % 2
            col = c if path == "A" else 8 + c
            e_raw = edges[:, k * 2 * P:(k + 1) * 2 * P]
            w_raw = wraw[:, k * P:(k + 1) * P]
            efs = ef[:, k, :]
            if j >= 2:
                need(pool, freed[j - 2])
            off = bass.IndirectOffsetOnAxis(ap=tcol[:, col:col + 1], axis=0)
            pool.indirect_dma_start(out=e_raw, out_offset=None, in_=a["edges"], in_offset=off).then_inc(got[k], 16)
            n_got[k] += 16
            if path == "A":
                off = bass.IndirectOffsetOnAxis(ap=tcol[:, col:col + 1], axis=0)
                pool.indirect_dma_start(out=w_raw, out_offset=None, in_=a["weights"], in_offset=off)\
                    .then_inc(got[k], 16)
                n_got[k] += 16
            need(dve, (got[k], n_got[k]))
            if j >= 2:
                need(dve, turned[j - 2])
            V.did(dve.tensor_copy(efs[:, 0:P], e_raw[:, 0:P]))
            m = V.did(dve.tensor_scalar(efs[:, P:2 * P], e_raw[:, P:2 * P], wcol[:, col:col + 1], None,
                                        ALU.subtract))
            need(pe, m)
            if j >= 2:
                need(pe, freed[j - 2])
            bank = 5 + k
            pe.transpose(ps[:, bank, 0:P], efs[:, 0:P], ident)
            last = pe.transpose(ps[:, bank, P:2 * P], efs[:, P:2 * P], ident)
            if path == "A":
                need(pe, (got[k], n_got[k]))
                last = pe.transpose(ps[:, bank, 2 * P:3 * P], w_raw, ident)
            turned[j] = T.did(last)
            need(dve, turned[j])
            idx, rel = (idxA, relA) if path == "A" else (idxB, relB)
            V.did(dve.tensor_copy(idx[:, c * P:(c + 1) * P], ps[:, bank, 0:P]))
            freed[j] = V.did(dve.tensor_copy(rel[:, c * P:(c + 1) * P], ps[:, bank, P:2 * P]))
            if path == "A":
                freed[j] = V.did(dve.tensor_copy(wgtA[:, c * P:(c + 1) * P], ps[:, bank, 2 * P:3 * P]))
        tables = freed[len(chunks) - 1]

        need(dve, ld_w.mark)
        V.did(dve.tensor_scalar(bcol[:, 2:4], bcol[:, 0:2], -1.0, 40.0, ALU.mult, ALU.add))
        V.did(dve.tensor_scalar(bcol[:, 4:6], bcol[:, 0:2], -LOG2, None, ALU.add))
        V.did(dve.tensor_tensor(out=B1, in0=B1, in1=B1B, op=ALU.add))
        V.did(dve.memset(bcol[:, 6:7], 40.0))
        V.did(dve.memset(bcol[:, 7:8], 0.5))
        half = small[:, 48:49]
        V.did(dve.memset(small[:, 49:50], 1e-5))
        prepared = V.did(dve.memset(half, 1.0))
        eps_c = small[:, 49:50]
        forty, halfc = bcol[:, 6:7], bcol[:, 7:8]
        need(act, prepared)

        XCH = [(7 * k, min(7 * k + 7, NT)) for k in range(-(-NT // 7))]

        def layernorm(ready, hn, hn_at, deps, src=None, relu=True):
            src = x_n if src is None else src
            need(dve, ready, *deps)
            mean, var, rstd = stat[:, 0, :], stat[:, 1, :], stat[:, 2, :]
            xcv = xc.rearrange("p (t d) -> p t d", d=D)
            sqv = sq.rearrange("p (t d) -> p t d", d=D)
            squared = []
            for lo, hi in XCH:
                m = V.did(dve.tensor_reduce(mean[:, lo:hi], src[:, lo:hi, :], AX.X, ALU.add))
                need(dve, m)
                m = V.did(dve.tensor_scalar(mean[:, lo:hi], mean[:, lo:hi], 1.0 / D, None, ALU.mult))
                need(dve, m)
                m = V.did(dve.tensor_tensor(out=xcv[:, lo:hi, :], in0=src[:, lo:hi, :],
                                            in1=mean[:, lo:hi].unsqueeze(2).to_broadcast([P, hi - lo, D]),
                                            op=ALU.subtract))
                need(act, m)
                squared.append(A.did(act.activation(sqv[:, lo:hi, :], xcv[:, lo:hi, :], ACT.Square)))
            for (lo, hi), s in zip(XCH, squared):
                need(dve, s)
                m = V.did(dve.tensor_reduce(var[:, lo:hi], sqv[:, lo:hi, :], AX.X, ALU.add))
            need(act, m)
            s = A.did(act.activation(var, var, ACT.Sqrt, bias=eps_c, scale=1.0 / D))
            need(dve, s)
            m = V.did(dve.reciprocal(rstd, var))
            need(dve, m)
            done = []
            for lo, hi in XCH:
                done.append(V.did(dve.scalar_tensor_tensor(
                    out=hn[:, lo:hi, hn_at:hn_at + D], in0=xcv[:, lo:hi, :], scalar=0.0 if relu else 1.0,
                    in1=rstd[:, lo:hi].unsqueeze(2).to_broadcast([P, hi - lo, D]),
                    op0=ALU.max if relu else ALU.mult, op1=ALU.mult)))
            return done

        def transposed(src_of, done, dst, deps, banks=(0, 1)):
            marks = []
            need(pe, *deps)
            need(act, *deps)
            for g in range(-(-NT // 4)):
                lo, hi = 4 * g, min(4 * g + 4, NT)
                need(pe, done[(hi - 1) // 7])
                if g >= len(banks):
                    need(pe, marks[g - len(banks)])
                bank = banks[g % len(banks)]
                for t in range(lo, hi):
                    last = pe.transpose(ps[:, bank, (t - lo) * P:(t - lo + 1) * P], src_of(t), ident)
                need(act, T.did(last))
                marks.append(A.did(act.copy(dst[:, lo * P:hi * P], ps[:, bank, 0:(hi - lo) * P])))
            return marks

        s_idx, s_msk, s_mm, s_acc, s_mul = (sem(n) for n in ("s_idx", "s_msk", "s_mm", "s_acc", "s_mul"))
        s_go = sem("s_go")
        s_g = [sem(f"s_g{q}") for q in range(RINGB)]
        s_ef = [sem(f"s_ef{q}") for q in range(RINGA)]
        base = dict(idx=0, msk=0, mm=RINGA, acc=2 * QUAD, mul=RINGA)
        base_g = [0] * RINGB
        pe.sem_inc(s_mm, RINGA)
        dve.sem_inc(s_acc, 2 * QUAD)
        dve.sem_inc(s_mul, RINGA)
        s_ei = [sem(f"s_ei{k}") for k in range(2)]
        s_es = [sem(f"s_es{k}") for k in range(2)]
        s_z1, s_z2, s_ac, s_pw = (sem(n) for n in ("s_z1", "s_z2", "s_ac", "s_pw"))
        Z1C, PWC = 2, 2
        pe.sem_inc(s_z1, Z1C)
        dve.sem_inc(s_pw, PWC)
        ein = [mlp(k) for k in range(2)]
        efo = [mlp(2 + k) for k in range(2)]
        sp1, ar, ae, al = mlp(4), mlp(5), mlp(6), mlp(7)
        need(sp, tables)
        for k in range(2):
            sp.dma_start(efo[k][:, 0:D], a["we1T"]).then_inc(s_es[k], 16)
        for k in range(2):
            sp.dma_start(ein[k], a["edge_attrT"][:, k * GRP:(k + 1) * GRP]).then_inc(s_ei[k], 16)
        Z1, Z2 = 6, 7
        flat = ps[:].rearrange("p b n -> p (b n)")

        def sums_of(layer, par, k):
            if layer > 0:
                return ps[:, 2 * par + k // 2, (k % 2) * WA:(k % 2 + 1) * WA]
            c = 2 * k
            at = [par * 3 * 512 + (x // 3) * 512 + (x % 3) * ACC3 for x in (c, c + 1)]
            step = at[1] - at[0]
            return flat[:, at[0]:at[0] + 2 * step].rearrange("p (j n) -> p j n", j=2)[:, :, 0:ACC3]

        def softplus_part(z, b40):
            return ((ar, z, ACT.Relu, b40, -1.0), (ae, ar, ACT.Exp, forty, -1.0), (al, ae, ACT.Ln, halfc, 0.5))

        def edge_loop(layer, table, deps):
            width = table.shape[1]
            slots = work[:, 0:QUAD * RINGA * width].rearrange("p (q k w) -> p q k w", q=RINGA, k=QUAD)
            net = layer < 2
            wide = 2 * ACC3 if layer == 0 else WA
            windows = acc[:, 0:BA * wide].rearrange("p (b w) -> p b w", b=BA)
            ef_in = acc[:, XC:XC + RINGA * QUAD * D].rearrange("p (q k w) -> p q k w", q=RINGA, k=QUAD)
            b_idx, b_msk, b_mm, b_acc, b_mul = (base[k] for k in ("idx", "msk", "mm", "acc", "mul"))
            bg = list(base_g)
            i0 = ITERSA * layer
            for e in (pe, dve, act, pool, sp):
                need(e, *deps)

            def stage_indices(n, col, slot):
                act.wait_ge(s_mm, n + (1 - RINGA + b_mm))
                act.copy(stage[:, slot, :], idxA[:, bass.ds(col, QUAD)]).then_inc(s_idx, 1)

            def make_mask(col, par, k):
                r = relA[:, bass.ds(col, 1)]
                if layer == 1:
                    return dve.tensor_scalar(masks[:, par, k, :], iota, r, wgtA[:, bass.ds(col, 1)],
                                             ALU.is_equal, ALU.mult)
                return dve.tensor_scalar(masks[:, par, k, :], iota, r, None, ALU.is_equal)

            def load_net_rows(n, col, slot):
                sp.wait_ge(s_mul, n + (1 - RINGA + b_mul))
                _, tiles = nc.values_load_multi_w_load_instructions(
                    tileA[0:1, bass.ds(col, QUAD)], engines=[ENG.SP], min_val=0, max_val=GROUPS * QUAD - 1,
                    skip_runtime_bounds_check_because="s - b_s; b_s counts the windows that have started")
                for k, t in enumerate(tiles):
                    sp.dma_start(ef_in[:, slot, k, :], edge_net[bass.ds(t, 1), :, :].rearrange("t p d -> p (t d)"))\
                        .then_inc(s_ef[slot], 16)

            if net:
                act.preload_act_table_set(EXP_LN)
            def gather(n, slot):
                pool.wait_ge(s_idx, n + (1 + b_idx))
                pool.sem_inc(s_go, 1)
                for k in range(QUAD):
                    pool.indirect_dma_start(
                        out=slots[:, slot, k, :], out_offset=None, in_=table,
                        in_offset=bass.IndirectOffsetOnAxis(ap=stage[:, slot, k:k + 1], axis=0)).then_inc(s_g[slot], 16)

            def multiply(turn, slot):
                dve.wait_ge(s_g[slot], turn * 64 + (64 + bg[slot]))
                dve.wait_ge(s_ef[slot], turn * 64 + 64)
                dve.tensor_tensor(out=slots[:, slot, :, :], in0=slots[:, slot, :, :], in1=ef_in[:, slot, :, :],
                                  op=ALU.mult).then_inc(s_mul, 1)

            for q in range(RINGA - 1):
                stage_indices(q, q * QUAD, q)
                if layer == 2:
                    load_net_rows(q, q * QUAD, q)
            for q in range(2):
                for k in range(QUAD):
                    ins = make_mask(q * QUAD + k, q, k)
                ins.then_inc(s_msk, 1)
            if layer == 2:
                gather(0, 0)
                multiply(0, 0)

            with nc.Fori(0, ITERSA) as i:
                _, offv = nc.values_load_multi_w_load_instructions(
                    winA[0:1, bass.ds(i * (QUAD * RINGA), QUAD * RINGA)], engines=[ENG.DVE], min_val=0, max_val=BA - 1,
                    skip_runtime_bounds_check_because="b_s counts the windows that have started")
                for q in range(RINGA):
                    nq = i * RINGA + q
                    col = i * (QUAD * RINGA) + q * QUAD
                    par = q % 2
                    ahead = (q + RINGA - 1) % RINGA
                    if layer < 2:
                        gather(nq, q)
                    stage_indices(nq + (RINGA - 1), col + (RINGA - 1) * QUAD, ahead)
                    if layer == 2:
                        load_net_rows(nq + (RINGA - 1), col + (RINGA - 1) * QUAD, ahead)
                        after = (q + 1) % RINGA
                        gather(nq + 1, after)
                        multiply(i + (q + 1) // RINGA, after)
                        pe.wait_ge(s_mul, nq + (1 + b_mul))
                    else:
                        pe.wait_ge(s_g[q], i * 64 + (64 + bg[q]))
                    pe.wait_ge(s_msk, nq + (1 + b_msk))
                    pe.wait_ge(s_acc, nq * QUAD + (b_acc - QUAD))
                    for k in range(QUAD):
                        o = sums_of(layer, par, k)
                        if layer == 0:
                            for j in range(WA // P):
                                last = pe.matmul(o[:, j, :], masks[:, par, k, j * P:(j + 1) * P], slots[:, q, k, :],
                                                 start=True, stop=True)
                        else:
                            last = pe.matmul(o, slots[:, q, k, :], masks[:, par, k, :], start=True, stop=True)
                    last.then_inc(s_mm, 1)
                    dve.wait_ge(s_mm, nq + (1 + b_mm))
                    for k in range(QUAD):
                        ins = make_mask(col + (2 * QUAD + k), par, k)
                        if k == QUAD - 1:
                            ins.then_inc(s_msk, 1)
                        dve.wait_ge(s_acc, nq * QUAD + (k + b_acc))
                        o = windows[:, bass.ds(offv[q * QUAD + k], 1), :]
                        if layer == 0:
                            o = o.rearrange("p b (j n) -> p (b j) n", j=2)
                        else:
                            o = o.rearrange("p b n -> p (b n)")
                        dve.tensor_tensor(out=o, in0=o, in1=sums_of(layer, par, k), op=ALU.add).then_inc(s_acc, 1)
                    if not net:
                        continue
                    h = q // 2
                    m = i * 2 + (2 * i0 + h)
                    m2 = i * 4 + (4 * i0 + 2 * h)
                    m6 = i * 12 + (12 * i0 + 6 * h)
                    if q % 2 == 0:
                        pe.wait_ge(s_ei[h], i * 16 + (16 * i0 + 16))
                        pe.wait_ge(s_pw, m2 + (PWC - 1))
                        pe.matmul(ps[:, Z1, :], WE1, ein[h], start=True, stop=True).then_inc(s_z1, 1)
                        act.wait_ge(s_z1, m + (1 + Z1C))
                        z, b40, b2, first_of, al_free, o = ps[:, Z1, :], bcol[:, 2:3], bcol[:, 4:5], 0, PWC, sp1
                    else:
                        pe.wait_ge(s_pw, m2 + (1 + PWC))
                        pe.matmul(ps[:, Z2, :], ones[0:1, :],
                                  be2row[:].unsqueeze(1).to_broadcast([1, QUAD, D]), start=True, stop=False)
                        for k in range(QUAD):
                            last = pe.matmul(ps[:, Z2, k * D:(k + 1) * D], sp1[:, k * P:(k + 1) * P], WE2,
                                             start=False, stop=(k == QUAD - 1))
                        last.then_inc(s_z2, 1)
                        act.wait_ge(s_z2, m + 1)
                        z, b40, b2, first_of, al_free, o = ps[:, Z2, :], forty, -LOG2, 3, 1 + PWC, efo[h]
                    for j, (dst, src, f, bb, sc) in enumerate(softplus_part(z, b40)):
                        if j:
                            act.wait_ge(s_ac, m6 + (first_of + j))
                        if j == 2:
                            act.wait_ge(s_pw, m2 + al_free)
                        act.activation(dst, src, f, bias=bb, scale=sc).then_inc(s_ac, 1)
                    dve.wait_ge(s_ac, m6 + (first_of + 3))
                    if q % 2:
                        dve.wait_ge(s_es[h], i * 16 + (16 * i0 + 16))
                    dve.scalar_tensor_tensor(out=o, in0=z, scalar=b2, in1=al, op0=ALU.add, op1=ALU.max)\
                        .then_inc(s_pw, 1)
                    if q % 2 == 0:
                        sp.wait_ge(s_z1, m + (1 + Z1C))
                        sp.dma_start(ein[h], a["edge_attrT"][:, bass.ds(i * (2 * GRP) + (2 * i0 + h + 2) * GRP, GRP)])\
                            .then_inc(s_ei[h], 16)
                    else:
                        sp.wait_ge(s_pw, m2 + (2 + PWC))
                        sp.dma_start(edge_net[bass.ds(i * (2 * QUAD) + (2 * i0 + h) * QUAD, QUAD), :, :]
                                     .rearrange("t p d -> p t d"),
                                     efo[h].rearrange("p (t d) -> p t d", d=D)).then_inc(s_es[h], 16)
            quads = RINGA * ITERSA
            base.update(idx=b_idx + quads + RINGA - 1, msk=b_msk + quads + 2, mm=b_mm + quads,
                        acc=b_acc + QUAD * quads, mul=b_mul + (quads + 1 if layer == 2 else 0))
            for q in range(RINGA):
                base_g[q] += 64 * (ITERSA + (layer == 2 and q == 0))
            over = [(s_acc, base["acc"]), (s_mm, base["mm"]), (s_idx, base["idx"]), (s_msk, base["msk"])]
            if layer == 1:
                over += [(s_ei[k], 16 * (2 * ITERSA + 1)) for k in range(2)]
                over += [(s_es[k], 16 * (2 * ITERSA + 1)) for k in range(2)]
                over += [(s_ac, 6 * GROUPS), (s_pw, 2 * GROUPS + PWC)]
            if layer == 2:
                over += [(s_mul, base["mul"])] + [(s_ef[q], 64 * (ITERSA + (q < RINGA - 1))) for q in range(RINGA)]
            return over

        def store_nodes(table, src, done):
            ld = Load("st_" + table.tensor.name)
            tv = table.rearrange("(t p) w -> p t w", p=P)
            for c, (lo, hi) in enumerate(XCH):
                need(sp, done[c])
                ld.add(sp.dma_start(tv[:, lo:hi, :], src[:, lo:hi, :]))
            return ld.mark

        def project(pairs, brow, ready, take, banks=(4, 5)):
            marks = []
            for g in range(-(-NT // 4)):
                lo, hi = 4 * g, min(4 * g + 4, NT)
                need(pe, *ready(g))
                if g >= len(banks):
                    need(pe, marks[g - len(banks)])
                bank = banks[g % len(banks)]
                pe.matmul(ps[:, bank, 0:(hi - lo) * D], ones[0:1, :],
                          brow.unsqueeze(1).to_broadcast([1, hi - lo, D]), start=True, stop=False)
                for t in range(lo, hi):
                    for j, (lhs, w) in enumerate(pairs):
                        last = pe.matmul(ps[:, bank, (t - lo) * D:(t - lo + 1) * D], lhs(t), w, start=False,
                                         stop=(t == hi - 1 and j == len(pairs) - 1))
                marks.append(take(g, lo, hi, bank, T.did(last)))
            return marks

        def add_to_x(g, lo, hi, bank, mm):
            need(dve, mm)
            return V.did(dve.tensor_tensor(out=x_n[:, lo:hi, :], in0=x_n[:, lo:hi, :],
                                           in1=ps[:, bank, 0:(hi - lo) * D].rearrange("p (t d) -> p t d", d=D),
                                           op=ALU.add))

        def tile_of(flat_view):
            return lambda t: flat_view[:, t * P:(t + 1) * P]

        def finish(final):
            st = Load("st_out")
            need(sp, *final)
            st.add(sp.dma_start(out[0:(NT - 1) * P, :].rearrange("(t p) d -> p t d", p=P), x_n[:, 0:NT - 1, :]))
            st.add(sp.dma_start(out[(NT - 1) * P:N, :], x_n[0:LAST, NT - 1, :]))
            need(sp, st.mark)

        acc0 = acc[:, 0:2 * BA * ACC3].rearrange("p (t w) -> p t w", w=ACC3)
        m1 = V.did(dve.memset(acc0[:, NT:2 * BA, :], 0.0))
        need(dve, m1, tables)
        m1 = V.did(dve.memset(acc0[:, 0:NT, D:ACC3], 1.0))
        done = layernorm(ld_x.mark, acc0, 0, [tables, kept.mark])
        stored = store_nodes(T0, acc0, done + [m1])
        over = edge_loop(0, T0, [stored, prepared])

        need(dve, *over)
        m1 = V.did(dve.reciprocal(stat[:, 3, :], acc0[:, 0:NT, D]))
        need(dve, m1)
        xcv = xc.rearrange("p (t d) -> p t d", d=D)
        done = [V.did(dve.tensor_tensor(out=xcv[:, lo:hi, :], in0=acc0[:, lo:hi, 0:D],
                                        in1=stat[:, 3, lo:hi].unsqueeze(2).to_broadcast([P, hi - lo, D]),
                                        op=ALU.mult)) for lo, hi in XCH]
        turned = transposed(lambda t: xcv[:, t, :], done, hT, [over[0]])
        added = project([(tile_of(hT), W0)], B0, lambda g: [turned[g]], add_to_x)

        hn = acc[:, SQ:SQ + NP].rearrange("p (t d) -> p t d", d=D)
        done = layernorm(added[-1], hn, 0, [])
        stored = store_nodes(T1, hn, done)
        turned = transposed(lambda t: hn[:, t, :], done, hT, [added[-1]])
        m1 = V.did(dve.memset(acc[:, 0:NODESA], 0.0))
        over = edge_loop(1, T1, [stored, m1, turned[-1]])

        need(dve, *over)
        need(act, *over)
        u, v = acc[:, XC:XC + NP], acc[:, 0:NP]
        uv = []
        for g in range(-(-NT // 4)):
            cs = slice(g * 512, min(g * 512 + 512, NP))
            V.did(dve.tensor_tensor(out=u[:, cs], in0=hT[:, cs], in1=acc[:, cs], op=ALU.add))
            need(dve, (V.sem, V.n))
            uv.append(V.did(dve.tensor_tensor(out=v[:, cs], in0=hT[:, cs], in1=acc[:, cs], op=ALU.mult)))
        zo = acc[:, SQ:SQ + NP].rearrange("p (t d) -> p t d", d=D)
        ss, rn = stat[:, 0, :], stat[:, 1, :]
        slopes = {}

        def leaky(g, lo, hi, bank, mm):
            zs = zo[:, lo:hi, :]
            need(act, mm)
            m = A.did(act.copy(zs, ps[:, bank, 0:(hi - lo) * D].rearrange("p (t d) -> p t d", d=D)))
            need(dve, m)
            slopes[g] = V.did(dve.scalar_tensor_tensor(out=zs, in0=zs, scalar=0.2, in1=zs, op0=ALU.mult, op1=ALU.max))
            return m

        project([(tile_of(u), W1), (tile_of(v), W2)], B1, lambda g: [uv[g]], leaky)
        sq2 = hT[:, 0:NP].rearrange("p (t d) -> p t d", d=D)
        for lo, hi in XCH:
            need(act, slopes[(hi - 1) // 4])
            m = A.did(act.activation(sq2[:, lo:hi, :], zo[:, lo:hi, :], ACT.Square))
            need(dve, m)
            m1 = V.did(dve.tensor_reduce(ss[:, lo:hi], sq2[:, lo:hi, :], AX.X, ALU.add))
        need(act, m1)
        m = A.did(act.activation(ss, ss, ACT.Sqrt))
        need(dve, m)
        m = V.did(dve.tensor_scalar(ss, ss, 1e-12, None, ALU.max))
        need(dve, m)
        m = V.did(dve.reciprocal(rn, ss))
        need(dve, m)
        for lo, hi in XCH:
            m = V.did(dve.tensor_tensor(out=zo[:, lo:hi, :], in0=zo[:, lo:hi, :],
                                        in1=rn[:, lo:hi].unsqueeze(2).to_broadcast([P, hi - lo, D]), op=ALU.mult))
            need(dve, m)
            m1 = V.did(dve.tensor_tensor(out=x_n[:, lo:hi, :], in0=x_n[:, lo:hi, :], in1=zo[:, lo:hi, :],
                                         op=ALU.add))

        done = layernorm(m1, hn, 0, [])
        turned = transposed(lambda t: hn[:, t, :], done, hT, [m1])
        hw = acc[:, XC:XC + NP].rearrange("p (t d) -> p t d", d=D)
        last_h = done[-1]

        def to_rows(g, lo, hi, bank, mm):
            need(act, mm, last_h)
            return A.did(act.copy(hw[:, lo:hi, :], ps[:, bank, 0:(hi - lo) * D].rearrange("p (t d) -> p t d", d=D)))

        made = project([(tile_of(hT), WN)], BN, lambda g: [turned[g]], to_rows)
        stored = store_nodes(T2, hw, [made[(hi - 1) // 4] for _, hi in XCH])
        m1 = V.did(dve.memset(acc[:, 0:NODESA], 0.0))
        over = edge_loop(2, T2, [stored, m1, made[-1]])

        for e in (pe, dve, act, sp):
            need(e, *over)
        act.preload_act_table_set(EXP_LN)
        spn = [acc[:, SQ + k * GRP:SQ + (k + 1) * GRP] for k in range(2)]
        f1, f2, added = {}, {}, {}
        for g in range(-(-NT // 4)):
            lo, hi = 4 * g, min(4 * g + 4, NT)
            w = (hi - lo) * P
            z = ps[:, g % 2, 0:w]
            if g >= 2:
                need(pe, f1[g - 2])
            m = T.did(pe.matmul(z, WF1, acc[:, lo * P:hi * P], start=True, stop=True))
            need(act, m)
            for j, (dst, src, f, bb, sc) in enumerate(softplus_part(z, bcol[:, 3:4])):
                if j:
                    need(act, m)
                if j == 2 and g >= 1:
                    need(act, f1[g - 1])
                m = A.did(act.activation(dst[:, 0:w], src if j == 0 else src[:, 0:w], f, bias=bb, scale=sc))
            need(dve, m)
            if g >= 2:
                need(dve, f2[g - 2])
            f1[g] = V.did(dve.scalar_tensor_tensor(out=spn[g % 2][:, 0:w], in0=z, scalar=bcol[:, 5:6],
                                                   in1=al[:, 0:w], op0=ALU.add, op1=ALU.max))
            need(pe, f1[g])
            if g >= 2:
                need(pe, added[g - 2])
            bank = 4 + g % 2
            pe.matmul(ps[:, bank, 0:w], ones[0:1, :], BF2.unsqueeze(1).to_broadcast([1, hi - lo, D]),
                      start=True, stop=False)
            for t in range(lo, hi):
                last = pe.matmul(ps[:, bank, (t - lo) * D:(t - lo + 1) * D],
                                 spn[g % 2][:, (t - lo) * P:(t - lo + 1) * P], WF2, start=False, stop=(t == hi - 1))
            f2[g] = T.did(last)
            added[g] = add_to_x(g, lo, hi, bank, f2[g])

        rows3 = acc[:, SQ:SQ + NT * ROW3].rearrange("p (t w) -> p t w", w=ROW3)
        h3 = rows3[:, :, HEADS:HEADS + D]
        need(sp, added[g])
        W3 = wts[:, 0:HEADS, :].rearrange("p h c -> p (h c)")
        GAMMA, BETA, BIAS3 = wts[:, 4, :], wts[:, 5, :], bias[:, 0, :]
        onehots = acc[:, 0:2 * TABB].rearrange("p (g s) -> p g s", g=GB)
        win_b = acc[:, 2 * TABB:3 * TABB]
        sc_b = acc[:, 3 * TABB:3 * TABB + GB * 2 * P].rearrange("p (g q n) -> p g q n", g=GB, n=WB)
        w3T = acc[:, 3600:3600 + HEADS * P].rearrange("p (h f) -> p h f", h=HEADS)
        att = acc[:, 4200:4200 + 2 * HEADS]
        vs = small[:, 0:2 * HEADS]
        ld_3 = Load("ld_3")
        ld_3.add(sp.dma_start(w3T, a["w3T"].rearrange("(h c) f -> c h f", h=HEADS)))
        ld_3.add(sp.dma_start(att[:, 0:HEADS], a["att_srcT"]))
        ld_3.add(sp.dma_start(att[:, HEADS:], a["att_dstT"]))
        ld_3.add(sp.dma_start(W3, a["w3"]))
        ld_3.add(sp.dma_start(GAMMA, a["gamma3"].to_broadcast([P, D])))
        ld_3.add(sp.dma_start(BETA, a["beta3"].to_broadcast([P, D])))
        ld_3.add(sp.dma_start(BIAS3, a["bias3"]))
        ld_3.add(sp.dma_start(win_b, windows_b.to_broadcast([P, TABB])))

        flatA = tabA[:].rearrange("p a n -> p (a n)")
        fresh, selfs = flatA[:, 0:TABB], flatA[:, TABB:2 * TABB]
        tw = [hT[:, k * 512:(k + 1) * 512] for k in range(2)]
        ex = [hT[:, 1024 + k * 1024:1024 + (k + 1) * 1024] for k in range(2)]
        pw = [hT[:, 3072 + k * 512:3072 + (k + 1) * 512] for k in range(2)]
        ads = hT[:, 4 * TABB:6 * TABB].rearrange("p (j s) -> p j s", j=2)
        scr = hT[:, 6 * TABB:6 * TABB + 128]
        corr = scr[:, 0:RINGB * QUAD].rearrange("p (q k) -> p q k", q=RINGB)
        run = [scr[:, 24 + 10 * k:34 + 10 * k].rearrange("p (j n) -> p j n", j=2) for k in range(2)]
        top = [scr[:, 44 + 4 * k:48 + 4 * k] for k in range(2)]
        mx = [scr[:, 52 + 8 * k:60 + 8 * k].rearrange("p (j n) -> p j n", j=2) for k in range(2)]
        off = [scr[:, 68 + 8 * k:76 + 8 * k].rearrange("p (j n) -> p j n", j=2) for k in range(2)]
        drop = [scr[:, 84 + 4 * k:88 + 4 * k] for k in range(2)]
        pen = [wts[:, 6 + k, :].rearrange("p (k n) -> p k n", k=QUAD) for k in range(2)]

        done = layernorm(added[g], rows3, HEADS, [])
        turned = transposed(lambda t: rows3[:, t, HEADS:HEADS + D], done, hT, [added[g]])
        m_one = V.did(dve.memset(rows3[:, :, HEADS + D:ROW3], 1.0))
        for lo, hi in XCH:
            need(dve, done[-1])
            m_res = V.did(dve.tensor_tensor(out=x_n[:, lo:hi, :], in0=x_n[:, lo:hi, :], in1=h3[:, lo:hi, :],
                                            op=ALU.add))
        need(pe, ld_3.mark, turned[-1])
        for j in range(2):
            for h in range(HEADS):
                q = j * HEADS + h
                last = pe.matmul(ps[:, 2, q:q + 1], w3T[:, h, :], att[:, q:q + 1], start=True, stop=True)
        m = T.did(last)
        need(act, m)
        m = A.did(act.copy(vs, ps[:, 2, 0:2 * HEADS]))
        need(pe, m)
        for t in range(NT):
            last = pe.matmul(ps[:, 3, t * HEADS:(t + 1) * HEADS], hT[:, t * P:(t + 1) * P], vs[:, 0:HEADS],
                             start=True, stop=True)
        m = T.did(last)
        need(act, m)
        m_sc = A.did(act.copy(rows3[:, :, 0:HEADS], ps[:, 3, 0:NT * HEADS].rearrange("p (t h) -> p t h", h=HEADS)))
        st_3 = Load("st_3")
        tv = T3.rearrange("(t p) w -> p t w", p=P)
        need(sp, m_sc, m_one, *done)
        for lo, hi in XCH:
            st_3.add(sp.dma_start(tv[:, lo:hi, :], rows3[:, lo:hi, :]))
        rowbuf = acc[0:2 * HEADS, XC:XC + NP]
        marks = []
        for c in range(-(-NP // 512)):
            lo, hi = c * 512, min(c * 512 + 512, NP)
            if c >= 2:
                need(pe, marks[c - 2])
            m = T.did(pe.matmul(ps[0:2 * HEADS, c % 2, 0:hi - lo], vs, hT[:, lo:hi], start=True, stop=True))
            need(act, m, done[-1])
            marks.append(A.did(act.copy(rowbuf[:, lo:hi], ps[0:2 * HEADS, c % 2, 0:hi - lo])))
        need(sp, marks[-1])
        st_s = Load("st_s")
        need(sp, st_s.add(sp.dma_start(scores, rowbuf)))
        ld_s = Load("ld_s")
        for grp in range(GB):
            ld_s.add(sp.dma_start(sc_b[0:PB, grp, :, :], scores.rearrange("q (b n) -> b q n", n=WB)
                                  [grp * PB:(grp + 1) * PB]))
        need(dve, ld_3.mark, m_sc)
        m = V.did(dve.memset(fresh[:, 0:1], FAR))
        m = V.did(dve.tensor_tensor(out=fresh[:, 1:TABB], in0=win_b[:, 1:TABB], in1=win_b[:, 0:TABB - 1],
                                    op=ALU.is_equal))
        need(dve, m)
        V.did(dve.tensor_scalar(fresh[:, 1:TABB], fresh[:, 1:TABB], 1.0, -FAR, ALU.subtract, ALU.mult))
        lb, _ = cols["limB"]
        for grp in range(GB):
            c0 = lb + 4 * grp + 1
            m = V.did(dve.tensor_scalar(onehots[0:PB, grp, :], win_b[0:PB, :], 1.0, cst[0:PB, c0:c0 + 1],
                                        ALU.subtract, ALU.is_equal))
        need(pe, m, ld_s.mark)
        for j in range(2):
            for half in range(2):
                for grp in range(GB):
                    q0 = HEADS * (1 - j)
                    last = pe.matmul(ps[:, 4 + 2 * j + half, :],
                                     sc_b[0:PB, grp, q0:q0 + HEADS, :].rearrange("p q n -> p (q n)"),
                                     onehots[0:PB, grp, half * 512:(half + 1) * 512],
                                     start=(grp == 0), stop=(grp == GB - 1))
        m_pt = T.did(last)
        need(dve, m_pt)
        for j in range(2):
            m = V.did(dve.tensor_scalar(ads[:, j, :].rearrange("p (b n) -> p b n", b=2), ps[:, 4:6, :],
                                        1.0 if j == 0 else 0.2, None, ALU.mult))
        m = V.did(dve.tensor_copy(selfs.rearrange("p (b n) -> p b n", b=2), ps[:, 6:8, :]))
        m_tab = V.did(dve.memset(run[0][:, 0, 0:1], 0.0))
        acc3 = acc[:].rearrange("p (b w) -> p b w", w=ACC3)
        need(sp, st_3.mark, m_res, m_tab, m_pt, st_s.mark)
        ld_a = Load("ld_a")
        tv = T3.rearrange("(b n) w -> n b w", n=WB)
        for h in range(HEADS):
            for b0 in range(0, BB, 49):
                ld_a.add(sp.dma_start(acc3[h * WB:(h + 1) * WB, b0:b0 + 49, :], tv[:, b0:b0 + 49, HEADS:ROW3]))

        slots3 = work[:, 0:RINGB * QUAD * ROW3].rearrange("p (q k w) -> p q k w", q=RINGB, k=QUAD)
        PT, PB_, OUT = 0, 2, 4
        names = ("s_bld", "s_pt", "s_ch", "s_ex", "s_pm", "s_pb", "s_cp")
        s_bld, s_pt, s_ch, s_ex, s_pm, s_pb, s_cp = (sem(n) for n in names)
        C = 2
        for e, mine in ((dve, (s_bld, s_ch, s_pm)), (pe, (s_pt, s_pb)), (act, (s_ex, s_cp))):
            need(e, m_tab, (st_3.sem, st_3.n), (s_mm, base["mm"]))
            for s in mine:
                e.sem_inc(s, C)
        need(pool, st_3.mark, (s_mm, base["mm"]))
        b_idx, b_o, b_acc = base["idx"], base["mm"], base["acc"]
        CHAIN = 10

        def at(i, q, mult, extra=0):
            return mult * q + extra if i is None else i * (mult * RINGB) + (mult * q + extra)

        def sl(i, q):
            return bass.ds(at(i, q, QUAD), QUAD) if i is not None else slice(QUAD * q, QUAD * q + QUAD)

        def stage3(i, q):
            act.copy(stage[:, q % RINGB, :], idxB[:, sl(i, q)]).then_inc(s_idx, 1)

        def gather3(i, q):
            pool.wait_ge(s_idx, at(i, q, 1, b_idx + 1))
            pool.sem_inc(s_go, 1)
            for k in range(QUAD):
                pool.indirect_dma_start(
                    out=slots3[:, q % RINGB, k, :], out_offset=None, in_=T3,
                    in_offset=bass.IndirectOffsetOnAxis(ap=stage[:, q % RINGB, k:k + 1], axis=0))\
                    .then_inc(s_g[q % RINGB], 16)

        def slot3(i, q, offs):
            head, chain, weigh, add = q + 4, q + 3, q + 2, q
            if i is None:
                chain, weigh, add = (x if x >= 0 else None for x in (chain, weigh, add))

            def add_step(k):
                if add is None:
                    return
                dve.wait_ge(s_acc, at(i, add, QUAD, b_acc + k))
                bank = OUT + 2 * (add % 2) + k // 2
                o = acc3[:, bass.ds(offs[k], 1), :].rearrange("p b n -> p (b n)")
                dve.scalar_tensor_tensor(out=o, in0=o, scalar=corr[:, add % RINGB, k:k + 1],
                                         in1=ps[:, bank, (k % 2) * ACC3:(k % 2 + 1) * ACC3],
                                         op0=ALU.mult, op1=ALU.add).then_inc(s_acc, 1)

            hp = head % 2

            def head_step(k):
                if k == 0:
                    dve.wait_ge(s_pt, at(i, head, 1, C - 1))
                    dve.tensor_tensor(out=pen[hp], in0=iota[:, 0:WB].unsqueeze(1).to_broadcast([P, QUAD, WB]),
                                      in1=relB[:, sl(i, head)].unsqueeze(2).to_broadcast([P, QUAD, WB]),
                                      op=ALU.is_equal).then_inc(s_bld, 1)
                elif k == 1:
                    dve.wait_ge(s_bld, at(i, head, 3, C + 1))
                    dve.tensor_scalar(pen[hp], pen[hp], 1.0, -FAR, ALU.subtract, ALU.mult).then_inc(s_bld, 1)
                else:
                    dve.wait_ge(s_g[head % RINGB], base_g[head % RINGB] + 64 * (head // RINGB + 1) if i is None else
                                i * 64 + (base_g[head % RINGB] + 64 * (head // RINGB + 1)))
                    dve.wait_ge(s_bld, at(i, head, 3, C + 2))
                    dve.tensor_tensor(
                        out=tw[hp].rearrange("p (k h n) -> p k h n", k=QUAD, h=HEADS),
                        in0=slots3[:, head % RINGB, :, 0:HEADS].unsqueeze(3).to_broadcast([P, QUAD, HEADS, WB]),
                        in1=pen[hp].unsqueeze(2).to_broadcast([P, QUAD, HEADS, WB]), op=ALU.add).then_inc(s_bld, 1)

            if weigh is not None:
                wp = weigh % 2
                e1, e2 = ex[wp][:, 0:512], ex[wp][:, 512:1024]

            def weigh_step():
                if weigh is not None:
                    dve.wait_ge(s_ex, at(i, weigh, 1, C + 1))
                    dve.tensor_tensor(out=e1, in0=e1, in1=e2, op=ALU.max).then_inc(s_pm, 1)

            fill = {1: lambda: head_step(0), 2: lambda: add_step(0), 3: lambda: head_step(1),
                    5: lambda: head_step(2), 6: lambda: add_step(1), 7: lambda: add_step(2),
                    8: lambda: add_step(3), 10: weigh_step}
            if chain is None:
                for k in range(3):
                    head_step(k)

            if chain is not None:
                cp = chain % 2
                table = sl(i, chain)
                step = [0]

                def link(ins, awaited=True):
                    ins.then_inc(s_ch, 1)
                    step[0] += 1
                    if step[0] in fill:
                        fill[step[0]]()
                    if awaited:
                        dve.wait_ge(s_ch, at(i, chain, CHAIN, C + step[0]))

                r, b = top[cp], run[cp]
                if add is not None:
                    dve.wait_ge(s_mm, at(i, add, 1, b_o + 1))
                dve.wait_ge(s_pt, at(i, chain, 1, C + 1))
                dve.wait_ge(s_ch, at(i, chain, CHAIN, C))
                link(dve.tensor_reduce(r, ps[:, PT + cp, :].rearrange("p (k e) -> p k e", k=QUAD), AX.X, ALU.max))
                link(dve.tensor_tensor(out=r, in0=r, in1=selfs[:, table], op=ALU.max))
                link(dve.tensor_tensor_scan(out=b[:, 0, 1:5], data0=fresh[:, table], data1=r,
                                            initial=b[:, 0, 0:1], op0=ALU.add, op1=ALU.max))
                link(dve.tensor_copy(run[1 - cp][:, 0, 0:1], b[:, 0, 4:5]), False)
                link(dve.tensor_tensor(out=b[:, 1, 1:5], in0=b[:, 0, 0:4], in1=fresh[:, table], op=ALU.add))
                link(dve.tensor_tensor(out=b[:, 1, 1:5], in0=b[:, 1, 1:5], in1=selfs[:, table], op=ALU.max))
                mm = mx[cp]
                link(dve.tensor_tensor(out=mm, in0=b[:, :, 1:5],
                                       in1=ads[:, 0, table].unsqueeze(1).to_broadcast([P, 2, QUAD]), op=ALU.add))
                link(dve.scalar_tensor_tensor(out=mm, in0=mm, scalar=0.2, in1=mm, op0=ALU.mult, op1=ALU.max))
                link(dve.tensor_tensor(out=drop[cp], in0=mm[:, 1, :], in1=mm[:, 0, :], op=ALU.subtract), False)
                link(dve.tensor_tensor(out=off[cp], in0=ads[:, :, table],
                                       in1=mm[:, 0:1, :].to_broadcast([P, 2, QUAD]), op=ALU.subtract), False)
                act.wait_ge(s_ch, at(i, chain, CHAIN, C + CHAIN))
                act.wait_ge(s_pm, at(i, chain, 1, C - 1))
                act.wait_ge(s_pb, at(i, chain, 1, C - 1))
                act.activation(corr[:, chain % RINGB, :], drop[cp], ACT.Exp)
                for j in range(2):
                    for k in range(QUAD):
                        last = act.activation(ex[cp][:, j * 512 + k * P:j * 512 + (k + 1) * P],
                                              ps[:, PT + cp, k * P:(k + 1) * P], ACT.Exp,
                                              bias=off[cp][:, j, k:k + 1], scale=1.0 if j == 0 else 0.2)
                last.then_inc(s_ex, 1)

            pe.wait_ge(s_bld, at(i, head, 3, C + 3))
            pe.wait_ge(s_ex, at(i, head, 1, C - 1))
            for k in range(QUAD):
                last = pe.transpose(ps[:, PT + hp, k * P:(k + 1) * P], tw[hp][:, k * P:(k + 1) * P], ident)
            last.then_inc(s_pt, 1)

            if weigh is not None:
                pe.wait_ge(s_pm, at(i, weigh, 1, C + 1))
                pe.wait_ge(s_cp, at(i, weigh, 1, C - 1))
                for k in range(QUAD):
                    last = pe.transpose(ps[:, PB_ + wp, k * P:(k + 1) * P], e1[:, k * P:(k + 1) * P], ident)
                last.then_inc(s_pb, 1)
                act.wait_ge(s_pb, at(i, weigh, 1, C + 1))
                act.wait_ge(s_mm, at(i, weigh, 1, b_o - 1))
                act.copy(pw[wp], ps[:, PB_ + wp, :]).then_inc(s_cp, 1)
                pe.wait_ge(s_cp, at(i, weigh, 1, C + 1))
                pe.wait_ge(s_acc, at(i, weigh, QUAD, b_acc - QUAD))
                for k in range(QUAD):
                    bank = OUT + 2 * wp + k // 2
                    o = ps[:, bank, (k % 2) * ACC3:(k % 2 + 1) * ACC3]
                    last = pe.matmul(o, pw[wp][:, k * P:(k + 1) * P], slots3[:, weigh % RINGB, k, HEADS:ROW3],
                                     start=True, stop=True)
                last.then_inc(s_mm, 1)

        for q in range(RINGB):
            stage3(None, q)
            gather3(None, q)
        for q in range(-4, 0):
            slot3(None, q, None)
        act.wait_ge(s_mm, b_o + 1)
        stage3(None, RINGB)
        gather3(None, RINGB)
        need(dve, ld_a.mark)
        with nc.Fori(0, ITERSB) as i:
            for q in range(RINGB):
                _, offs = nc.values_load_multi_w_load_instructions(
                    winB[0:1, sl(i, q)], engines=[ENG.DVE], min_val=0, max_val=BB - 1,
                    skip_runtime_bounds_check_because="b_s counts the windows that have started")
                slot3(i, q, offs)
                act.wait_ge(s_mm, at(i, q + 1, 1, b_o + 1))
                stage3(i, q + 1 + RINGB)
                gather3(i, q + 1 + RINGB)
        quads = RINGB * ITERSB
        for q in range(RINGB):
            need(dve, (s_g[q], base_g[q] + 64 * (ITERSB + 1 + (q == 0))))
        need(dve, (s_acc, b_acc + QUAD * quads), (s_pt, C + quads + 4), (s_pb, C + quads + 2),
             (s_ex, C + quads + 3), (s_mm, b_o + quads + 2), (s_cp, C + quads + 2), (s_idx, b_idx + quads + RINGB + 1))

        zr = flatA[:, 0:BB]
        m = V.did(dve.tensor_scalar(zr, acc3[:, :, D], float(HEADS), None, ALU.mult))
        need(dve, m)
        m = V.did(dve.reciprocal(zr, zr))
        need(dve, m)
        scaled = []
        for lo, hi in XCH:
            s4 = slice(4 * lo, 4 * hi)
            scaled.append(V.did(dve.tensor_tensor(
                out=acc3[:, s4, 0:D], in0=acc3[:, s4, 0:D],
                in1=zr[:, s4].unsqueeze(2).to_broadcast([P, 4 * (hi - lo), D]), op=ALU.mult)))
        turned_w = [flatA[:, 256 + 512 * k:768 + 512 * k] for k in range(2)]
        WPT = P // WB
        gat = hT[:, 0:NP].rearrange("p (t d) -> p t d", d=D)
        need(act, m)
        w_turned, w_free, marks = {}, {}, {}
        for t in range(NT + 1):
            if t < NT:
                need(pe, scaled[t // 7])
                if t >= 2:
                    need(pe, w_turned[t - 2])
                for w in range(WPT):
                    last = pe.transpose(ps[:, t % 2, w * P:(w + 1) * P], acc3[:, t * WPT + w, 0:D], ident)
                need(act, T.did(last))
                if t >= 2:
                    need(act, w_free[t - 2])
                w_turned[t] = A.did(act.copy(
                    turned_w[t % 2].rearrange("p (h w n) -> p w h n", h=HEADS, w=WPT),
                    ps[:, t % 2, :].rearrange("p (w h n) -> p w h n", w=WPT, h=HEADS)))
            if t > 0:
                u = t - 1
                grp, c = u // 4, u % 4
                bank = 4 + grp % 2
                if c == 0 and grp >= 2:
                    need(pe, marks[grp - 2])
                need(pe, w_turned[u])
                o = ps[:, bank, c * D:(c + 1) * D]
                pe.matmul(o, ones[0:1, :], BIAS3, start=True, stop=False)
                for h in range(HEADS):
                    last = pe.matmul(o, turned_w[u % 2][:, h * P:(h + 1) * P], W3[:, h * D:(h + 1) * D],
                                     start=False, stop=(h == HEADS - 1))
                w_free[u] = T.did(last)
                if c == 3 or u == NT - 1:
                    need(dve, w_free[u])
                    marks[grp] = V.did(dve.tensor_copy(
                        gat[:, 4 * grp:u + 1, :], ps[:, bank, 0:(c + 1) * D].rearrange("p (t d) -> p t d", d=D)))
        done = layernorm(marks[grp], gat, 0, [], src=gat, relu=False)
        for lo, hi in XCH:
            n = hi - lo
            gc = gat[:, lo:hi, :]
            for vec, op in ((GAMMA, ALU.mult), (BETA, ALU.add)):
                need(dve, (V.sem, V.n))
                V.did(dve.tensor_tensor(out=gc, in0=gc, in1=vec.unsqueeze(1).to_broadcast([P, n, D]), op=op))
            need(dve, (V.sem, V.n))
            m = V.did(dve.scalar_tensor_tensor(out=x_n[:, lo:hi, :], in0=gc, scalar=0.0, in1=x_n[:, lo:hi, :],
                                               op0=ALU.max, op1=ALU.add))
        finish([m])


def kernel(**inputs):
    import concourse.bacc as bacc
    from concourse.bass_utils import run_bass_kernel_spmd

    def arr(name):
        return np.asarray(inputs[name])

    pad = ROWS * P - E
    src = np.concatenate([arr("src"), np.zeros(pad, np.int32)]).reshape(ROWS, P)
    dst = np.concatenate([arr("dst"), np.full(pad, 1 << 20, np.int32)]).reshape(ROWS, P)
    arrays = {
        "x": arr("x"),
        "edges": np.concatenate([src, dst], axis=1),
        "lasts": dst[:, P - 1].reshape(1, ROWS),
        "weights": np.concatenate([arr("edge_weight"), np.zeros(pad, np.float32)]).reshape(ROWS, P),
        "edge_attrT": np.concatenate([arr("edge_attr_128").T, np.zeros((P, ECOLS - E), np.float32)], axis=1),
        "consts": const_table(), "steps": np.arange(TABB, dtype=np.float32).reshape(1, TABB),
        "w0": arr("L0_gnn_weight"), "w1": arr("L1_gnn_W1"), "w2": arr("L1_gnn_W2"),
        "wnT": arr("L2_gnn_W_node").T, "we1T": arr("L2_gnn_W_e1").T, "we2T": arr("L2_gnn_W_e2").T,
        "wf1T": arr("L2_gnn_W_fc1").T, "wf2T": arr("L2_gnn_W_fc2").T,
        "w3": arr("L3_gnn_W"), "w3T": arr("L3_gnn_W").T,
        "att_srcT": arr("L3_gnn_att_src").T, "att_dstT": arr("L3_gnn_att_dst").T,
        "b0": arr("L0_gnn_b").reshape(1, D), "b1a": arr("L1_gnn_b1"), "b1b": arr("L1_gnn_b2"),
        "bn": arr("L2_gnn_b_node").reshape(1, D), "bf2": arr("L2_gnn_b_fc2").reshape(1, D),
        "be2": arr("L2_gnn_b_e2").reshape(1, D),
        "be1": arr("L2_gnn_b_e1").reshape(D, 1), "bf1": arr("L2_gnn_b_fc1").reshape(D, 1),
        "bias3": arr("L3_gnn_bias").reshape(1, D), "gamma3": arr("L3_gnn_ln_gamma").reshape(1, D),
        "beta3": arr("L3_gnn_ln_beta").reshape(1, D),
    }
    arrays = {"in_" + k: np.ascontiguousarray(v) for k, v in arrays.items()}
    nc = bacc.Bacc("TRN2", target_bir_lowering=False, num_devices=1)
    aps = {k[3:]: nc.dram_tensor(k, v.shape, mybir.dt.from_np(v.dtype), kind="ExternalInput").ap()
           for k, v in arrays.items()}
    out = nc.dram_tensor("out", (N, D), F32, kind="ExternalOutput").ap()
    build(nc, aps, out)
    r = run_bass_kernel_spmd(nc, [arrays], core_ids=[0])
    return r.results[0]["out"]
```

```python
from contextlib import ExitStack

import numpy as np

import concourse.bass as bass
from concourse import mybir

F32 = mybir.dt.float32
I32 = mybir.dt.int32
ALU = mybir.AluOpType
ACT = mybir.ActivationFunctionType
AX = mybir.AxisListType
ENG = mybir.EngineType

N, E, D = 6250, 100000, 128
P = 128
NT = -(-N // P)
NP = NT * P
LAST = N - (NT - 1) * P
ET = -(-E // P)
HEADS = 4
LOG2 = float(np.log(2.0))
FAR = -1.0e30
EXP_LN = "natural_log_exp_and_others"

WA, WB = 256, 32
BA, BB = -(-N // WA), -(-N // WB)
QUAD = 4
RINGA, RINGB = 4, 6
STEPSA = QUAD * RINGA * -(-(ET + BA - 1) // (QUAD * RINGA))
STEPSB = QUAD * RINGB * -(-(ET + BB - 1) // (QUAD * RINGB))
ITERSA, ITERSB = STEPSA // (QUAD * RINGA), STEPSB // (QUAD * RINGB)
TABA = P * -(-(STEPSA + QUAD * RINGA) // P)
TABB = P * -(-(STEPSB + QUAD * RINGB) // P)
GB = 2
PB = BB // GB
assert BB % GB == 0
ROWS = TABA
NODESA = BA * WA
GRP = 512
GROUPS = 2 * 2 * ITERSA
ECOLS = (GROUPS + 2) * GRP
ROW3 = HEADS + D + 1
ACC3 = D + 1


def const_layout():
    at, out = 0, {}
    for name, width in (("ident", P), ("iota", WA), ("limA", 2), ("limB", 2 * GB), ("stepcol", TABB // P), ("ones", P)):
        out[name] = (at, at + width)
        at += width
    return out, at


def const_table():
    cols, width = const_layout()
    c = np.zeros((P, width), np.float32)
    p = np.arange(P, dtype=np.float32)

    def put(name, value):
        a, b = cols[name]
        c[:, a:b] = value

    put("ident", np.eye(P))
    put("iota", np.arange(WA)[None, :])
    put("limA", np.stack([WA * p, p], 1))
    lim = np.zeros((P, GB, 2), np.float32)
    for g in range(GB):
        lim[:, g] = np.stack([WB * (g * PB + p), g * PB + p], 1)
    put("limB", lim.reshape(P, -1))
    put("stepcol", np.arange(TABB // P)[None, :] * P + p[:, None])
    put("ones", 1.0)
    return c


class Lane:

    def __init__(self, engine, sem):
        self.e, self.sem, self.n = engine, sem, 0

    def did(self, ins):
        self.n += 1
        ins.then_inc(self.sem, 1)
        return (self.sem, self.n)


def need(engine, *marks):
    for sem, value in marks:
        engine.wait_ge(sem, value)


def build(nc, a, out):
    with ExitStack() as ctx:
        def sb(name, shape, dt=F32):
            return ctx.enter_context(nc.sbuf_tensor("t_" + name, shape, dt))

        def sem(name):
            return ctx.enter_context(nc.semaphore(name))

        def dram(name, shape, dt=F32):
            return nc.dram_tensor("d_" + name, shape, dt, kind="Internal").ap()

        pe, dve, act, pool, sp = nc.tensor, nc.vector, nc.scalar, nc.gpsimd, nc.sync
        V = Lane(dve, sem("v_done"))
        A = Lane(act, sem("a_done"))
        T = Lane(pe, sem("t_done"))
        G = Lane(pool, sem("g_done"))

        class Load:

            def __init__(self, name):
                self.sem, self.n = sem(name), 0

            def add(self, ins, k=1):
                ins.then_inc(self.sem, 16)
                self.n += 16 * k
                return (self.sem, self.n)

            @property
            def mark(self):
                return (self.sem, self.n)

        cols, cwidth = const_layout()
        cst = sb("cst", [P, cwidth])

        def c_(name):
            x, y = cols[name]
            return cst[:, x:y]

        ident, iota, ones = c_("ident"), c_("iota"), c_("ones")
        x_n = sb("x", [P, NT, D])
        hT = sb("hT", [P, NODESA])
        acc = sb("acc", [P, BB * ACC3])
        work = sb("work", [P, QUAD * RINGA * ACC3 + 2 * QUAD * WA])
        assert QUAD * RINGB * ROW3 <= work.shape[1]
        masks = work[:, QUAD * RINGA * ACC3:].rearrange("p (s k w) -> p s k w", s=2, k=QUAD)
        tabA = sb("tabA", [P, 3, TABA])
        idxA, relA, wgtA = tabA[:, 0, :].bitcast(I32), tabA[:, 1, :], tabA[:, 2, :]
        idxB = sb("idxB", [P, TABB], I32)
        relB = sb("relB", [P, TABB])
        stage = sb("stage", [P, RINGB, QUAD], I32)
        winA, tileA = sb("winA", [1, TABA], I32), sb("tileA", [1, TABA], I32)
        winB = sb("winB", [1, TABB], I32)
        wts = sb("wts", [P, 8, D])
        W0, W1, W2, WN, WE1, WE2, WF1, WF2 = (wts[:, k, :] for k in range(8))
        bias = sb("bias", [1, 5, D])
        bcol = sb("bcol", [P, 8])
        rn = sb("rn", [P, 2, NT])
        halves = sb("halves", [P, NT, 6])
        meanvar = sb("meanvar", [P, NT, 2])
        dev = sb("dev", [P, 2, NT])
        small = sb("small", [P, 64])

        XC, SQ = NT * P + 2 * ACC3 + 2, NT * P + 2 * ACC3 + 2 + NP
        MLP = SQ + NT * ROW3

        def mlp(k, n=1):
            assert MLP + (k + n) * GRP <= BB * ACC3
            return acc[:, MLP + k * GRP:MLP + (k + n) * GRP]

        ps = ctx.enter_context(nc.psum_tensor("ps", [P, 8, 512], F32))

        edge_net = dram("edge_net", [(1 + GROUPS) * QUAD, P, D])
        T0, T1, T2, T3 = dram("T0", [NP, D + 1]), dram("T1", [NP, D]), dram("T2", [NP, D]), dram("T3", [NP, ROW3])
        scores = dram("scores", [2 * HEADS, NP])
        windows_b = dram("windows_b", [1, TABB])

        ld_c, ld_x, ld_w = Load("ld_c"), Load("ld_x"), Load("ld_w")
        ld_l = Load("ld_l")
        scratch, at_scratch = acc[:, NT * ACC3 + 2 * ACC3 + 150:], [0]

        def take(n):
            lo = at_scratch[0]
            at_scratch[0] += n
            return scratch[:, lo:lo + n]

        lastb = take(ROWS).bitcast(I32)
        ld_l.add(sp.dma_start(lastb, a["lasts"].to_broadcast([P, ROWS])))
        ld_c.add(sp.dma_start(cst[:], a["consts"]))
        steps = hT[:, 4 * TABB:5 * TABB]
        ld_c.add(sp.dma_start(steps, a["steps"].to_broadcast([P, TABB])))
        x_pad = V.did(dve.memset(x_n[:, NT - 1, :], 0.0))
        for lo in range(0, NT - 1, 12):
            hi = min(lo + 12, NT - 1)
            ld_x.add(sp.dma_start(x_n[:, lo:hi, :], a["x"][lo * P:hi * P, :].rearrange("(t p) d -> p t d", p=P)))
        need(sp, x_pad)
        ld_x.add(sp.dma_start(x_n[0:LAST, NT - 1, :], a["x"][(NT - 1) * P:N, :]))
        for k, name in enumerate(("w0", "w1", "w2", "wnT", "we1T", "we2T", "wf1T", "wf2T")):
            ld_w.add(act.dma_start(wts[:, k, :], a[name]))
        for k, name in enumerate(("b0", "b1a", "b1b", "bn", "bf2")):
            ld_w.add(act.dma_start(bias[:, k, :], a[name]))
        B0, B1, B1B, BN, BF2 = (bias[:, k, :] for k in range(5))
        be2row = sb("be2row", [1, D])
        ld_w.add(act.dma_start(be2row[:], a["be2"]))
        ld_w.add(act.dma_start(bcol[:, 0:1], a["be1"]))
        ld_w.add(act.dma_start(bcol[:, 1:2], a["bf1"]))
        eps_c = small[:, 49:50]
        m_eps = V.did(dve.memset(eps_c, 1e-5))
        need(act, m_eps)

        GRS = [(lo, min(lo + 4, NT)) for lo in range(0, NT, 4)]

        def pipeline_step(step, *stages):
            for k in reversed(range(len(stages))):
                if 0 <= step - k < len(GRS):
                    stages[k](step - k, *GRS[step - k])

        def pipeline(*stages):
            for step in range(len(GRS) + len(stages) - 1):
                pipeline_step(step, *stages)

        def rows(view, lo, hi):
            return view[:, lo:hi, :]

        def banked(bank, n):
            return ps[:, bank, 0:n * D].rearrange("p (t d) -> p t d", d=D)

        def spread(v, n):
            return v.unsqueeze(2).to_broadcast([P, n, D])

        def statistics(src_of, lo, hi, ready):
            need(dve, ready)
            for t in range(lo, hi):
                m = V.did(dve.bn_stats(halves[:, t, :], src_of(t)))
            need(dve, m)
            for t in range(lo, hi):
                m = V.did(dve.bn_aggr(meanvar[:, t, :], halves[:, t, :]))
            return m

        def deviation(lo, hi, ready):
            need(act, ready)
            return A.did(act.activation(dev[:, 0, lo:hi], meanvar[:, lo:hi, 1], ACT.Sqrt, bias=eps_c))

        def normalise(src_of, dst_of, lo, hi, ready):
            need(dve, ready)
            need(dve, V.did(dve.reciprocal(dev[:, 1, lo:hi], dev[:, 0, lo:hi])))
            for t in range(lo, hi):
                m = V.did(dve.tensor_scalar(dst_of(t), src_of(t), meanvar[:, t, 0:1], dev[:, 1, t:t + 1],
                                            ALU.subtract, ALU.mult))
            return m

        def rectify(view, lo, hi, ready):
            need(act, ready)
            return A.did(act.activation(rows(view, lo, hi), rows(view, lo, hi), ACT.Relu))

        def x_of(t):
            return x_n[:, t, :]

        def turn(g, lo, hi, src_of, ready, marks, dst, bank0):
            need(pe, ready)
            if g >= 2:
                need(pe, marks[g - 2])
            bank = bank0 + g % 2
            for t in range(lo, hi):
                last = pe.transpose(ps[:, bank, (t - lo) * P:(t - lo + 1) * P], src_of(t), ident)
            need(act, T.did(last))
            marks[g] = A.did(act.copy(dst[:, lo * P:hi * P], ps[:, bank, 0:(hi - lo) * P]))

        def project(lo, hi, bank, pairs, brow, ready):
            need(pe, *ready)
            pe.matmul(ps[:, bank, 0:(hi - lo) * D], ones[0:1, :], brow.unsqueeze(1).to_broadcast([1, hi - lo, D]),
                      start=True, stop=False)
            for t in range(lo, hi):
                for j, (lhs, w) in enumerate(pairs):
                    last = pe.matmul(ps[:, bank, (t - lo) * D:(t - lo + 1) * D], lhs[:, t * P:(t + 1) * P], w,
                                     start=False, stop=(t == hi - 1 and j == len(pairs) - 1))
            return T.did(last)

        def add_to_x(lo, hi, bank, ready):
            need(dve, ready)
            return V.did(dve.tensor_tensor(out=rows(x_n, lo, hi), in0=rows(x_n, lo, hi), in1=banked(bank, hi - lo),
                                           op=ALU.add))

        def store_rows(ld, table, src, lo, hi, ready):
            need(sp, *ready)
            ld.add(sp.dma_start(table.rearrange("(t p) w -> p t w", p=P)[:, lo:hi, :], rows(src, lo, hi)))

        lastf, cmp = take(ROWS), take(ROWS)
        need(dve, ld_l.mark)
        m = V.did(dve.tensor_copy(lastf, lastb))
        need(dve, m, ld_c.mark)
        la, _ = cols["limA"]
        lb, _ = cols["limB"]
        first = small[:, 0:8]
        starts = [(0, BA, la)] + [(1 + g, PB, lb + 2 * g) for g in range(GB)]
        for k, n, c in starts:
            m = V.did(dve.tensor_scalar(cmp[0:n, :], lastf[0:n, :], cst[0:n, c:c + 1], None, ALU.is_lt))
            need(dve, m)
            m = V.did(dve.tensor_reduce(first[0:n, k:k + 1], cmp[0:n, :], AX.X, ALU.add))
            need(dve, m)
            m = V.did(dve.tensor_tensor(out=first[0:n, k:k + 1], in0=first[0:n, k:k + 1],
                                        in1=cst[0:n, c + 1:c + 2], op=ALU.add))
            need(dve, m)
        startedA, startedB = take(TABA), [take(TABB) for g in range(GB)]
        V.did(dve.tensor_scalar(startedA[0:BA, :], steps[0:BA, 0:TABA], first[0:BA, 0:1], None, ALU.is_ge))
        for g in range(GB):
            m = V.did(dve.tensor_scalar(startedB[g][0:PB, :], steps[0:PB, :], first[0:PB, 1 + g:2 + g], None,
                                        ALU.is_ge))
        need(pe, m)
        halfA, halfB = TABA // 2, TABB // 2
        bcA = ps[:, 0:2, 0:halfA]
        bcB = ps[:, 2:4, 0:halfB]
        for h in range(2):
            pe.matmul(ps[:, h, 0:halfA], ones[0:BA, :], startedA[0:BA, h * halfA:(h + 1) * halfA],
                      start=True, stop=True)
            for g in range(GB):
                pe.matmul(ps[:, 2 + h, 0:halfB], ones[0:PB, :], startedB[g][0:PB, h * halfB:(h + 1) * halfB],
                          start=(g == 0), stop=(g == GB - 1))
        CA, CB = TABA // P, TABB // P
        for c in range(CA):
            pe.matmul(ps[:, 4, c:c + 1], startedA[0:BA, c * P:(c + 1) * P], ones[0:BA, 0:1], start=True, stop=True)
        for c in range(CB):
            for g in range(GB):
                last = pe.matmul(ps[:, 4, 16 + c:17 + c], startedB[g][0:PB, c * P:(c + 1) * P], ones[0:PB, 0:1],
                                 start=(g == 0), stop=(g == GB - 1))
        counted = T.did(last)
        need(dve, counted)

        for win, counts, width in ((winA, bcA, 2 * ACC3), (winB, bcB, ACC3)):
            V.did(dve.tensor_scalar(win[:].rearrange("p (h n) -> p h n", h=2), counts[0:1], 1.0, float(width),
                                    ALU.subtract, ALU.mult))
        m = V.did(dve.tensor_tensor(
            out=tileA[:].rearrange("p (h n) -> p h n", h=2),
            in0=steps[0:1, 0:TABA].rearrange("p (h n) -> p h n", h=2), in1=bcA[0:1], op=ALU.subtract))
        need(dve, m)
        V.did(dve.tensor_scalar(tileA[:], tileA[:], 1.0, None, ALU.add))
        tcol = sb("tcol", [P, 16], I32)
        wcol = small[:, 16:32]
        tcf = small[:, 32:48]
        for base, n, off, w in ((0, CA, 0, WA), (8, CB, 16, WB)):
            x0, _ = cols["stepcol"]
            m = V.did(dve.tensor_tensor(out=tcf[:, base:base + n], in0=cst[:, x0:x0 + n],
                                        in1=ps[:, 4, off:off + n], op=ALU.subtract))
            need(dve, m)
            V.did(dve.tensor_scalar(tcol[:, base:base + n], tcf[:, base:base + n], 1.0, None, ALU.add))
            wcol_ready = V.did(dve.tensor_scalar(wcol[:, base:base + n], ps[:, 4, off:off + n], 1.0, float(w),
                                                 ALU.subtract, ALU.mult))
        win_f = take(TABB)[0:1, :]
        m = V.did(dve.tensor_copy(win_f.rearrange("p (h n) -> p h n", h=2), bcB[0:1]))
        need(sp, m)
        kept = Load("kept")
        kept.add(sp.dma_start(windows_b, win_f))
        need(sp, kept.mark)

        need(pool, wcol_ready)
        SLOTS = 3
        got = [sem(f"got{k}") for k in range(SLOTS)]
        edges = [take(2 * P).bitcast(I32) for k in range(SLOTS)]
        wraw = [take(P) for k in range(SLOTS)]
        ef = [take(2 * P) for k in range(SLOTS)]
        assert at_scratch[0] <= MLP - (NT + 2) * ACC3 - 150
        chunks = [("A", c) for c in range(CA)] + [("B", c) for c in range(CB)]
        turned, freed = {}, {}
        n_got = [0] * SLOTS

        acc0 = acc[:, 0:2 * BA * ACC3].rearrange("p (t w) -> p t w", w=ACC3)
        pool.memset(acc0[:, NT:2 * BA, :], 0.0)
        ones_set = G.did(pool.memset(acc0[:, 0:NT, D:ACC3], 1.0))
        st_0, dv0, nm0 = Load("st_0"), {}, {}

        def table0_measure(g, lo, hi):
            dv0[g] = deviation(lo, hi, statistics(x_of, lo, hi, ld_x.mark))

        def table0_scale(g, lo, hi):
            nm0[g] = normalise(x_of, lambda t: acc0[:, t, 0:D], lo, hi, dv0[g])

        def table0_finish(g, lo, hi):
            m = rectify(acc0[:, :, 0:D], lo, hi, nm0[g])
            store_rows(st_0, T0, acc0, lo, hi, [m, ones_set])

        for j, (path, c) in enumerate(chunks):
            k = j % SLOTS
            col = c if path == "A" else 8 + c
            e_raw, w_raw, efs = edges[k], wraw[k], ef[k]
            if j >= SLOTS:
                need(pool, freed[j - SLOTS])
            off = bass.IndirectOffsetOnAxis(ap=tcol[:, col:col + 1], axis=0)
            pool.indirect_dma_start(out=e_raw, out_offset=None, in_=a["edges"], in_offset=off).then_inc(got[k], 16)
            n_got[k] += 16
            if path == "A":
                off = bass.IndirectOffsetOnAxis(ap=tcol[:, col:col + 1], axis=0)
                pool.indirect_dma_start(out=w_raw, out_offset=None, in_=a["weights"], in_offset=off)\
                    .then_inc(got[k], 16)
                n_got[k] += 16
            need(dve, (got[k], n_got[k]))
            if j >= SLOTS:
                need(dve, turned[j - SLOTS])
            V.did(dve.tensor_copy(efs[:, 0:P], e_raw[:, 0:P]))
            m = V.did(dve.tensor_scalar(efs[:, P:2 * P], e_raw[:, P:2 * P], wcol[:, col:col + 1], None,
                                        ALU.subtract))
            need(pe, m)
            if j >= SLOTS:
                need(pe, freed[j - SLOTS])
            bank = 5 + k
            pe.transpose(ps[:, bank, 0:P], efs[:, 0:P], ident)
            last = pe.transpose(ps[:, bank, P:2 * P], efs[:, P:2 * P], ident)
            if path == "A":
                need(pe, (got[k], n_got[k]))
                last = pe.transpose(ps[:, bank, 2 * P:3 * P], w_raw, ident)
            turned[j] = T.did(last)
            need(dve, turned[j])
            idx, rel = (idxA, relA) if path == "A" else (idxB, relB)
            V.did(dve.tensor_copy(idx[:, c * P:(c + 1) * P], ps[:, bank, 0:P]))
            freed[j] = V.did(dve.tensor_copy(rel[:, c * P:(c + 1) * P], ps[:, bank, P:2 * P]))
            if path == "A":
                freed[j] = V.did(dve.tensor_copy(wgtA[:, c * P:(c + 1) * P], ps[:, bank, 2 * P:3 * P]))
            pipeline_step(j, table0_measure, table0_scale, table0_finish)
        assert len(chunks) >= len(GRS) + 2
        tables = freed[len(chunks) - 1]

        need(dve, ld_w.mark)
        V.did(dve.tensor_scalar(bcol[:, 2:4], bcol[:, 0:2], -1.0, 40.0, ALU.mult, ALU.add))
        V.did(dve.tensor_scalar(bcol[:, 4:6], bcol[:, 0:2], -LOG2, None, ALU.add))
        V.did(dve.tensor_tensor(out=B1, in0=B1, in1=B1B, op=ALU.add))
        V.did(dve.memset(bcol[:, 6:7], 40.0))
        prepared = V.did(dve.memset(bcol[:, 7:8], 0.5))
        forty, halfc = bcol[:, 6:7], bcol[:, 7:8]
        need(act, prepared)

        s_idx, s_msk, s_mm, s_acc, s_mul = (sem(n) for n in ("s_idx", "s_msk", "s_mm", "s_acc", "s_mul"))
        s_go = sem("s_go")
        s_g = [sem(f"s_g{q}") for q in range(RINGB)]
        s_ef = [sem(f"s_ef{q}") for q in range(RINGA)]
        base = dict(idx=0, msk=0, mm=RINGA, acc=2 * QUAD, mul=RINGA)
        base_g = [0] * RINGB
        pe.sem_inc(s_mm, RINGA)
        dve.sem_inc(s_acc, 2 * QUAD)
        dve.sem_inc(s_mul, RINGA)
        s_ei = [sem(f"s_ei{k}") for k in range(2)]
        s_es = [sem(f"s_es{k}") for k in range(2)]
        s_z, s_ac, s_pw = (sem(n) for n in ("s_z", "s_ac", "s_pw"))
        PWC = 1
        dve.sem_inc(s_pw, PWC)
        ein = [mlp(k) for k in range(2)]
        efo = [mlp(2 + k) for k in range(2)]
        sp1, ar, ae, al = mlp(4), mlp(5), mlp(6), mlp(7)
        need(sp, tables)
        for k in range(2):
            sp.dma_start(efo[k][:, 0:D], a["we1T"]).then_inc(s_es[k], 16)
        for k in range(2):
            sp.dma_start(ein[k], a["edge_attrT"][:, k * GRP:(k + 1) * GRP]).then_inc(s_ei[k], 16)
        flat = ps[:].rearrange("p b n -> p (b n)")

        def sums_of(layer, par, k):
            if layer > 0:
                return ps[:, 2 * par + k // 2, (k % 2) * WA:(k % 2 + 1) * WA]
            c = 2 * k
            at = [par * 3 * 512 + (x // 3) * 512 + (x % 3) * ACC3 for x in (c, c + 1)]
            step = at[1] - at[0]
            return flat[:, at[0]:at[0] + 2 * step].rearrange("p (j n) -> p j n", j=2)[:, :, 0:ACC3]

        def softplus_part(z, b40):
            return ((ar, z, ACT.Relu, b40, -1.0), (ae, ar, ACT.Exp, forty, -1.0), (al, ae, ACT.Ln, halfc, 0.5))

        def net_product(q, event, ready):
            need(pe, *ready)
            z = ps[:, 6 + q % 2, :]
            if q < 2:
                pe.matmul(z, WE1, ein[q], start=True, stop=True).then_inc(s_z, 1)
                return
            pe.matmul(z, ones[0:1, :], be2row[:].unsqueeze(1).to_broadcast([1, QUAD, D]), start=True, stop=False)
            for k in range(QUAD):
                last = pe.matmul(z[:, k * D:(k + 1) * D], sp1[:, k * P:(k + 1) * P], WE2, start=False,
                                 stop=(k == QUAD - 1))
            last.then_inc(s_z, 1)

        def net_chain(q, event, event3):
            act.wait_ge(s_z, event + 1)
            for j, (dst, src, f, bb, sc) in enumerate(softplus_part(ps[:, 6 + q % 2, :], bcol[:, 2:3] if q < 2 else forty)):
                if j:
                    act.wait_ge(s_ac, event3 + j)
                if j == 2:
                    act.wait_ge(s_pw, event + PWC)
                act.activation(dst, src, f, bias=bb, scale=sc).then_inc(s_ac, 1)

        def net_softplus(q, event, event3, turns):
            dve.wait_ge(s_ac, event3 + 3)
            if q < 2:
                dve.wait_ge(s_z, event + 2 * q)
                o, b2 = sp1, bcol[:, 4:5]
            else:
                dve.wait_ge(s_es[q - 2], turns * 16 + 16)
                o, b2 = efo[q - 2], -LOG2
            dve.scalar_tensor_tensor(out=o, in0=ps[:, 6 + q % 2, :], scalar=b2, in1=al, op0=ALU.add, op1=ALU.max)\
                .then_inc(s_pw, 1)

        def net_store(h, event, row):
            sp.wait_ge(s_pw, event + (1 + PWC))
            dst = edge_net[row:row + QUAD, :, :] if isinstance(row, int) else edge_net[bass.ds(row, QUAD), :, :]
            sp.dma_start(dst.rearrange("t p d -> p t d"), efo[h].rearrange("p (t d) -> p t d", d=D))\
                .then_inc(s_es[h], 16)

        def edge_loop(layer, table, deps):
            width = table.shape[1]
            slots = work[:, 0:QUAD * RINGA * width].rearrange("p (q k w) -> p q k w", q=RINGA, k=QUAD)
            net = layer < 2
            ef_in = acc[:, XC:XC + RINGA * QUAD * D].rearrange("p (q k w) -> p q k w", q=RINGA, k=QUAD)
            b_idx, b_msk, b_mm, b_acc, b_mul = (base[k] for k in ("idx", "msk", "mm", "acc", "mul"))
            bg = list(base_g)
            i0 = ITERSA * layer
            for e in (pe, dve, act, pool, sp):
                need(e, *deps)

            def stage_indices(n, col, slot):
                act.wait_ge(s_mm, n + (1 - RINGA + b_mm))
                act.copy(stage[:, slot, :], idxA[:, bass.ds(col, QUAD)]).then_inc(s_idx, 1)

            def make_mask(col, par, k):
                r = relA[:, bass.ds(col, 1)]
                if layer == 1:
                    return dve.tensor_scalar(masks[:, par, k, :], iota, r, wgtA[:, bass.ds(col, 1)],
                                             ALU.is_equal, ALU.mult)
                return dve.tensor_scalar(masks[:, par, k, :], iota, r, None, ALU.is_equal)

            def load_net_rows(n, col, slot):
                sp.wait_ge(s_mul, n + (1 - RINGA + b_mul))
                _, tiles = nc.values_load_multi_w_load_instructions(
                    tileA[0:1, bass.ds(col, QUAD)], engines=[ENG.SP], min_val=0, max_val=GROUPS * QUAD - 1,
                    skip_runtime_bounds_check_because="s - b_s; b_s counts the windows that have started")
                for k, t in enumerate(tiles):
                    sp.dma_start(ef_in[:, slot, k, :], edge_net[bass.ds(t + QUAD, 1), :, :].rearrange("t p d -> p (t d)"))\
                        .then_inc(s_ef[slot], 16)

            if net:
                act.preload_act_table_set(EXP_LN)
            if layer == 0:
                net_product(3, 0, [V.did(dve.memset(sp1, 0.0))])
                net_chain(3, 0, 0)
            def gather(n, slot):
                pool.wait_ge(s_idx, n + (1 + b_idx))
                pool.sem_inc(s_go, 1)
                for k in range(QUAD):
                    pool.indirect_dma_start(
                        out=slots[:, slot, k, :], out_offset=None, in_=table,
                        in_offset=bass.IndirectOffsetOnAxis(ap=stage[:, slot, k:k + 1], axis=0)).then_inc(s_g[slot], 16)

            def multiply(turn, slot):
                dve.wait_ge(s_g[slot], turn * 64 + (64 + bg[slot]))
                dve.wait_ge(s_ef[slot], turn * 64 + 64)
                dve.tensor_tensor(out=slots[:, slot, :, :], in0=slots[:, slot, :, :], in1=ef_in[:, slot, :, :],
                                  op=ALU.mult).then_inc(s_mul, 1)

            for q in range(RINGA - 1):
                stage_indices(q, q * QUAD, q)
                if layer == 2:
                    load_net_rows(q, q * QUAD, q)
            for q in range(2):
                for k in range(QUAD):
                    ins = make_mask(q * QUAD + k, q, k)
                ins.then_inc(s_msk, 1)
            if layer == 2:
                gather(0, 0)
                multiply(0, 0)

            with nc.Fori(0, ITERSA) as i:
                _, offv = nc.values_load_multi_w_load_instructions(
                    winA[0:1, bass.ds(i * (QUAD * RINGA), QUAD * RINGA)], engines=[ENG.DVE], min_val=0,
                    max_val=(BA - 1) * 2 * ACC3,
                    skip_runtime_bounds_check_because="b_s counts the windows that have started")
                for q in range(RINGA):
                    nq = i * RINGA + q
                    col = i * (QUAD * RINGA) + q * QUAD
                    par = q % 2
                    ahead = (q + RINGA - 1) % RINGA
                    if layer < 2:
                        gather(nq, q)
                    stage_indices(nq + (RINGA - 1), col + (RINGA - 1) * QUAD, ahead)
                    if layer == 2:
                        load_net_rows(nq + (RINGA - 1), col + (RINGA - 1) * QUAD, ahead)
                        after = (q + 1) % RINGA
                        gather(nq + 1, after)
                        multiply(i + (q + 1) // RINGA, after)
                        pe.wait_ge(s_mul, nq + (1 + b_mul))
                    else:
                        pe.wait_ge(s_g[q], i * 64 + (64 + bg[q]))
                    pe.wait_ge(s_msk, nq + (1 + b_msk))
                    pe.wait_ge(s_acc, nq * QUAD + (b_acc - QUAD))
                    for k in range(QUAD):
                        o = sums_of(layer, par, k)
                        if layer == 0:
                            for j in range(WA // P):
                                last = pe.matmul(o[:, j, :], masks[:, par, k, j * P:(j + 1) * P], slots[:, q, k, :],
                                                 start=True, stop=True)
                        else:
                            last = pe.matmul(o, slots[:, q, k, :], masks[:, par, k, :], start=True, stop=True)
                    last.then_inc(s_mm, 1)
                    dve.wait_ge(s_mm, nq + (1 + b_mm))
                    for k in range(QUAD):
                        ins = make_mask(col + (2 * QUAD + k), par, k)
                        if k == QUAD - 1:
                            ins.then_inc(s_msk, 1)
                        dve.wait_ge(s_acc, nq * QUAD + (k + b_acc))
                        if layer == 0:
                            o = acc[:, bass.ds(offv[q * QUAD + k], 2 * ACC3)].rearrange("p (j n) -> p j n", j=2)
                        else:
                            o = acc[:, bass.ds(offv[q * QUAD + k], WA)]
                        dve.tensor_tensor(out=o, in0=o, in1=sums_of(layer, par, k), op=ALU.add).then_inc(s_acc, 1)
                    if not net:
                        continue
                    event, event3 = i * 4 + (4 * i0 + q + 1), i * 12 + (12 * i0 + 3 * q + 3)
                    ready = [(s_pw, event + (PWC - 1))]
                    if q < 2:
                        ready.append((s_ei[q], i * 16 + (16 * i0 + 16)))
                    net_product(q, event, ready)
                    net_chain(q, event, event3)
                    net_softplus((q + 3) % 4, i * 4 + (4 * i0 + q), i * 12 + (12 * i0 + 3 * q), i + i0)
                    if q == 0:
                        net_store(1, i * 4 + 4 * i0, i * (2 * QUAD) + 2 * i0 * QUAD)
                    if q == 3:
                        net_store(0, i * 4 + (4 * i0 + 3), i * (2 * QUAD) + (2 * i0 + 1) * QUAD)
                    if q < 2:
                        sp.wait_ge(s_z, event + 1)
                        sp.dma_start(ein[q], a["edge_attrT"][:, bass.ds(i * (2 * GRP) + (2 * i0 + q + 2) * GRP, GRP)])\
                            .then_inc(s_ei[q], 16)
            if layer == 1:
                events = 8 * ITERSA
                net_softplus(3, events, 3 * events, 2 * ITERSA)
                net_store(1, events, GROUPS * QUAD)
            quads = RINGA * ITERSA
            base.update(idx=b_idx + quads + RINGA - 1, msk=b_msk + quads + 2, mm=b_mm + quads,
                        acc=b_acc + QUAD * quads, mul=b_mul + (quads + 1 if layer == 2 else 0))
            for q in range(RINGA):
                base_g[q] += 64 * (ITERSA + (layer == 2 and q == 0))
            over = [(s_acc, base["acc"]), (s_mm, base["mm"]), (s_idx, base["idx"]), (s_msk, base["msk"])]
            if layer == 1:
                over += [(s_ei[k], 16 * (2 * ITERSA + 1)) for k in range(2)]
                over += [(s_es[k], 16 * (2 * ITERSA + 1 + k)) for k in range(2)]
                over += [(s_ac, 3 * (events + 1)), (s_pw, events + 1 + PWC)]
            if layer == 2:
                over += [(s_mul, base["mul"])] + [(s_ef[q], 64 * (ITERSA + (q < RINGA - 1))) for q in range(RINGA)]
            return over

        laps = acc[:, 0:BA * 2 * ACC3].rearrange("p (b w) -> p b w", b=BA)

        def lap_of(lo, hi):
            if (hi - lo) % 2:
                assert hi - lo == 1
                return laps[:, lo // 2, 0:P]
            return laps[:, lo // 2:hi // 2, 0:WA]

        over = edge_loop(0, T0, [st_0.mark, prepared, tables, kept.mark])
        for e in (pe, dve, act, pool, sp):
            need(e, *over)
        counts_inv = rn[:, 1, :]
        m = V.did(dve.reciprocal(counts_inv, acc0[:, 0:NT, D]))
        need(dve, m)
        means = acc[:, XC:XC + NP].rearrange("p (t d) -> p t d", d=D)
        hn = acc[:, SQ:SQ + NP].rearrange("p (t d) -> p t d", d=D)
        avg, m_turned, m_proj, added, dv, nm, relu, h_turned = ({} for _ in range(8))
        st_1 = Load("st_1")

        def average(g, lo, hi):
            avg[g] = V.did(dve.tensor_tensor(out=rows(means, lo, hi), in0=acc0[:, lo:hi, 0:D],
                                             in1=spread(counts_inv[:, lo:hi], hi - lo), op=ALU.mult))

        def add_product(g, lo, hi):
            bank = 4 + g % 2
            mm = project(lo, hi, bank, [(hT, W0)], B0, [m_turned[g]] + ([added[g - 2]] if g >= 2 else []))
            added[g] = add_to_x(lo, hi, bank, mm)

        def measure(g, lo, hi):
            dv[g] = deviation(lo, hi, statistics(x_of, lo, hi, added[g]))

        def scale_rows(g, lo, hi):
            nm[g] = normalise(x_of, lambda t: hn[:, t, :], lo, hi, dv[g])

        def finish_rows(g, lo, hi):
            relu[g] = rectify(hn, lo, hi, nm[g])
            store_rows(st_1, T1, hn, lo, hi, [relu[g]])

        def turn_rows(g, lo, hi):
            turn(g, lo, hi, lambda t: hn[:, t, :], relu[g], h_turned, hT, 2)

        pipeline(average, lambda g, lo, hi: turn(g, lo, hi, lambda t: means[:, t, :], avg[g], m_turned, hT, 0),
                 add_product, measure, scale_rows, finish_rows, turn_rows)
        last_g = len(GRS) - 1
        need(pool, avg[last_g])
        zeroed = G.did(pool.memset(laps, 0.0))

        over = edge_loop(1, T1, [st_1.mark, zeroed, h_turned[last_g]])
        for e in (pe, dve, act, pool, sp):
            need(e, *over)
        u, v = acc[:, XC:XC + NP], acc[:, SQ:SQ + NP]
        uv, used, drawn, bent, squared, nrm, added, dv, nm, relu, h_turned, made = ({} for _ in range(12))
        st_2 = Load("st_2")
        squares = [mlp(k).rearrange("p (t d) -> p t d", d=D) for k in range(2)]

        def combine(g, lo, hi):
            cs, lap = slice(lo * P, hi * P), lap_of(lo, hi)

            def shaped(view):
                return view if hi - lo == 1 else view.rearrange("p (b w) -> p b w", w=WA)

            G.did(pool.tensor_tensor(out=shaped(u[:, cs]), in0=shaped(hT[:, cs]), in1=lap, op=ALU.add))
            uv[g] = G.did(pool.tensor_tensor(out=shaped(v[:, cs]), in0=shaped(hT[:, cs]), in1=lap, op=ALU.mult))

        def product1(g, lo, hi):
            bank = 4 + g % 2
            used[g] = project(lo, hi, bank, [(u, W1), (v, W2)], B1, [uv[g]] + ([drawn[g - 2]] if g >= 2 else []))
            need(act, used[g])
            drawn[g] = A.did(act.copy(rows(hn, lo, hi), banked(bank, hi - lo)))

        def bend(g, lo, hi):
            need(dve, drawn[g])
            bent[g] = V.did(dve.scalar_tensor_tensor(out=rows(hn, lo, hi), in0=rows(hn, lo, hi), scalar=0.2,
                                                     in1=rows(hn, lo, hi), op0=ALU.mult, op1=ALU.max))
            need(act, bent[g])
            if g >= 2:
                need(act, squared[g - 2])
            m = A.did(act.activation(squares[g % 2][:, 0:hi - lo, :], rows(hn, lo, hi), ACT.Square))
            nrm[g] = m

        def norms(g, lo, hi):
            need(dve, nrm[g])
            squared[g] = V.did(dve.tensor_reduce(rn[:, 0, lo:hi], squares[g % 2][:, 0:hi - lo, :], AX.X, ALU.add))
            need(act, squared[g])
            nrm[g] = A.did(act.activation(rn[:, 0, lo:hi], rn[:, 0, lo:hi], ACT.Sqrt))

        def add_normed(g, lo, hi):
            need(dve, nrm[g])
            need(dve, V.did(dve.tensor_scalar(rn[:, 0, lo:hi], rn[:, 0, lo:hi], 1e-12, None, ALU.max)))
            need(dve, V.did(dve.reciprocal(rn[:, 1, lo:hi], rn[:, 0, lo:hi])))
            for t in range(lo, hi):
                added[g] = V.did(dve.scalar_tensor_tensor(out=x_n[:, t, :], in0=hn[:, t, :], scalar=rn[:, 1, t:t + 1],
                                                          in1=x_n[:, t, :], op0=ALU.mult, op1=ALU.add))

        hw = acc[:, XC:XC + NP].rearrange("p (t d) -> p t d", d=D)

        def product_n(g, lo, hi):
            bank = 6 + g % 2
            mm = project(lo, hi, bank, [(hT, WN)], BN, [h_turned[g]] + ([made[g - 2]] if g >= 2 else []))
            need(act, mm)
            made[g] = A.did(act.copy(rows(hw, lo, hi), banked(bank, hi - lo)))
            store_rows(st_2, T2, hw, lo, hi, [made[g]])

        def finish_only(g, lo, hi):
            relu[g] = rectify(hn, lo, hi, nm[g])

        pipeline(combine, product1, bend, norms, add_normed,
                 lambda g, lo, hi: dv.update({g: deviation(lo, hi, statistics(x_of, lo, hi, added[g]))}),
                 lambda g, lo, hi: nm.update({g: normalise(x_of, lambda t: hn[:, t, :], lo, hi, dv[g])}),
                 finish_only,
                 lambda g, lo, hi: turn(g, lo, hi, lambda t: hn[:, t, :], relu[g], h_turned, hT, 2), product_n)
        need(pool, used[last_g])
        zeroed = G.did(pool.memset(laps, 0.0))

        over = edge_loop(2, T2, [st_2.mark, zeroed, made[last_g]])
        for e in (pe, dve, act, pool, sp):
            need(e, *over)
        act.preload_act_table_set(EXP_LN)

        rows3 = acc[:, SQ:SQ + NT * ROW3].rearrange("p (t w) -> p t w", w=ROW3)
        h3 = rows3[:, :, HEADS:HEADS + D]
        own = acc[:, XC:XC + NP]
        onehots = own[:, 0:2 * TABB].rearrange("p (g s) -> p g s", g=GB)
        win_b = own[:, 2 * TABB:3 * TABB]
        sc_b = own[:, 3 * TABB:3 * TABB + GB * 2 * P].rearrange("p (g q n) -> p g q n", g=GB, n=WB)
        w3T = own[:, 3600:3600 + HEADS * P].rearrange("p (h f) -> p h f", h=HEADS)
        att = own[:, 4200:4200 + 2 * HEADS]
        spn = [own[:, 4300 + k * GRP:4300 + (k + 1) * GRP] for k in range(2)]
        vs = small[:, 0:2 * HEADS]
        ld_v = Load("ld_v")
        ld_v.add(sp.dma_start(w3T, a["w3T"].rearrange("(h c) f -> c h f", h=HEADS)))
        ld_v.add(sp.dma_start(att[:, 0:HEADS], a["att_srcT"]))
        ld_v.add(sp.dma_start(att[:, HEADS:], a["att_dstT"]))
        ld_v.add(sp.dma_start(win_b, windows_b.to_broadcast([P, TABB])))
        flatA = tabA[:].rearrange("p a n -> p (a n)")
        fresh, selfs = flatA[:, 0:TABB], flatA[:, TABB:2 * TABB]

        z1, f1, f2, added, st, nm, relu, h_turned = ({} for _ in range(8))

        def product_1(g, lo, hi):
            if g >= 2:
                need(pe, f1[g - 2])
            z1[g] = T.did(pe.matmul(ps[:, g % 2, 0:(hi - lo) * P], WF1, lap_of(lo, hi), start=True, stop=True))

        def soft(g, lo, hi):
            w = (hi - lo) * P
            z = ps[:, g % 2, 0:w]
            need(act, z1[g])
            for j, (dst, src, f, bb, sc) in enumerate(softplus_part(z, bcol[:, 3:4])):
                if j:
                    need(act, m)
                if j == 2 and g >= 1:
                    need(act, f1[g - 1])
                m = A.did(act.activation(dst[:, 0:w], src if j == 0 else src[:, 0:w], f, bias=bb, scale=sc))
            need(dve, m)
            if g >= 2:
                need(dve, f2[g - 2])
            f1[g] = V.did(dve.scalar_tensor_tensor(out=spn[g % 2][:, 0:w], in0=z, scalar=bcol[:, 5:6],
                                                   in1=al[:, 0:w], op0=ALU.add, op1=ALU.max))

        def product_2(g, lo, hi):
            bank = 4 + g % 2
            need(pe, f1[g])
            if g >= 2:
                need(pe, added[g - 2])
            pe.matmul(ps[:, bank, 0:(hi - lo) * D], ones[0:1, :], BF2.unsqueeze(1).to_broadcast([1, hi - lo, D]),
                      start=True, stop=False)
            for t in range(lo, hi):
                last = pe.matmul(ps[:, bank, (t - lo) * D:(t - lo + 1) * D],
                                 spn[g % 2][:, (t - lo) * P:(t - lo + 1) * P], WF2, start=False, stop=(t == hi - 1))
            f2[g] = T.did(last)
            added[g] = add_to_x(lo, hi, bank, f2[g])

        pipeline(product_1, soft, product_2, lambda g, lo, hi: st.update({g: statistics(x_of, lo, hi, added[g])}))
        need(sp, f2[last_g])
        W3 = wts[:, 0:HEADS, :].rearrange("p h c -> p (h c)")
        GAMMA, BETA, BIAS3 = wts[:, 4, :], wts[:, 5, :], bias[:, 0, :]
        ld_3 = Load("ld_3")
        ld_3.add(sp.dma_start(W3, a["w3"]))
        ld_3.add(sp.dma_start(GAMMA, a["gamma3"].to_broadcast([P, D])))
        ld_3.add(sp.dma_start(BETA, a["beta3"].to_broadcast([P, D])))
        ld_3.add(sp.dma_start(BIAS3, a["bias3"]))


        tw = [hT[:, k * 512:(k + 1) * 512] for k in range(2)]
        ex = [hT[:, 1024 + k * 1024:1024 + (k + 1) * 1024] for k in range(2)]
        pw = [hT[:, 3072 + k * 512:3072 + (k + 1) * 512] for k in range(2)]
        ads = hT[:, 4 * TABB:6 * TABB].rearrange("p (j s) -> p j s", j=2)
        scr = hT[:, 6 * TABB:6 * TABB + 128]
        corr = scr[:, 0:RINGB * QUAD].rearrange("p (q k) -> p q k", q=RINGB)
        run = [scr[:, 24 + 10 * k:34 + 10 * k].rearrange("p (j n) -> p j n", j=2) for k in range(2)]
        top = [scr[:, 44 + 4 * k:48 + 4 * k] for k in range(2)]
        mx = [scr[:, 52 + 8 * k:60 + 8 * k].rearrange("p (j n) -> p j n", j=2) for k in range(2)]
        off = [scr[:, 68 + 8 * k:76 + 8 * k].rearrange("p (j n) -> p j n", j=2) for k in range(2)]
        drop = [scr[:, 84 + 4 * k:88 + 4 * k] for k in range(2)]
        pen = [wts[:, 6 + k, :].rearrange("p (k n) -> p k n", k=QUAD) for k in range(2)]

        need(pe, ld_v.mark, *st.values())
        for q in range(2 * HEADS):
            last = pe.matmul(ps[:, 2, q:q + 1], w3T[:, q % HEADS, :], att[:, q:q + 1], start=True, stop=True)
        m = T.did(last)
        need(act, m)
        m_vs = A.did(act.copy(vs, ps[:, 2, 0:2 * HEADS]))
        need(pe, m_vs)
        m_dev = deviation(0, NT, st[last_g])
        m_one = V.did(dve.memset(rows3[:, :, HEADS + D:ROW3], 1.0))
        need(dve, ld_v.mark)
        V.did(dve.memset(fresh[:, 0:1], FAR))
        m = V.did(dve.tensor_tensor(out=fresh[:, 1:TABB], in0=win_b[:, 1:TABB], in1=win_b[:, 0:TABB - 1],
                                    op=ALU.is_equal))
        need(dve, m)
        V.did(dve.tensor_scalar(fresh[:, 1:TABB], fresh[:, 1:TABB], 1.0, -FAR, ALU.subtract, ALU.mult))
        lb, _ = cols["limB"]
        for grp in range(GB):
            c0 = lb + 2 * grp + 1
            m_hot = V.did(dve.tensor_scalar(onehots[0:PB, grp, :], win_b[0:PB, :], 1.0, cst[0:PB, c0:c0 + 1],
                                            ALU.subtract, ALU.is_equal))
        rowbuf = acc[0:2 * HEADS, 0:NP]
        st_3 = Load("st_3")
        kept_h, score, sc_row = {}, {}, {}

        def norm_rows(g, lo, hi):
            nm[g] = normalise(x_of, lambda t: rows3[:, t, HEADS:HEADS + D], lo, hi, m_dev)

        def relu_rows(g, lo, hi):
            relu[g] = rectify(h3, lo, hi, nm[g])
            need(pool, relu[g])
            kept_h[g] = G.did(pool.tensor_tensor(out=rows(x_n, lo, hi), in0=rows(x_n, lo, hi), in1=rows(h3, lo, hi),
                                                 op=ALU.add))

        def scores_of(g, lo, hi):
            need(pe, h_turned[g])
            if g >= 2:
                need(pe, sc_row[g - 2])
            w = (hi - lo) * P
            for t in range(lo, hi):
                pe.matmul(ps[:, 6 + g % 2, (t - lo) * HEADS:(t - lo + 1) * HEADS], hT[:, t * P:(t + 1) * P],
                          vs[:, 0:HEADS], start=True, stop=True)
            m = T.did(pe.matmul(ps[0:2 * HEADS, g % 2, 0:w], vs, hT[:, lo * P:hi * P], start=True, stop=True))
            need(act, m)
            score[g] = A.did(act.copy(rows3[:, lo:hi, 0:HEADS], ps[:, 6 + g % 2, 0:(hi - lo) * HEADS]
                                      .rearrange("p (t h) -> p t h", h=HEADS)))
            sc_row[g] = A.did(act.copy(rowbuf[:, lo * P:hi * P], ps[0:2 * HEADS, g % 2, 0:w]))
            store_rows(st_3, T3, rows3, lo, hi, [score[g], m_one])

        pipeline(norm_rows, relu_rows,
                 lambda g, lo, hi: turn(g, lo, hi, lambda t: rows3[:, t, HEADS:HEADS + D], relu[g], h_turned, hT, 2),
                 scores_of)
        need(sp, sc_row[last_g])
        st_s = Load("st_s")
        need(sp, st_s.add(sp.dma_start(scores, rowbuf)))
        ld_s = Load("ld_s")
        for grp in range(GB):
            ld_s.add(sp.dma_start(sc_b[0:PB, grp, :, :], scores.rearrange("q (b n) -> b q n", n=WB)
                                  [grp * PB:(grp + 1) * PB]))
        need(pe, m_hot, ld_s.mark, sc_row[last_g])
        for j in range(2):
            for half in range(2):
                for grp in range(GB):
                    q0 = HEADS * (1 - j)
                    last = pe.matmul(ps[:, 4 + 2 * j + half, :],
                                     sc_b[0:PB, grp, q0:q0 + HEADS, :].rearrange("p q n -> p (q n)"),
                                     onehots[0:PB, grp, half * 512:(half + 1) * 512],
                                     start=(grp == 0), stop=(grp == GB - 1))
        m_pt = T.did(last)
        need(dve, m_pt)
        for j in range(2):
            V.did(dve.tensor_scalar(ads[:, j, :].rearrange("p (b n) -> p b n", b=2), ps[:, 4:6, :],
                                    1.0 if j == 0 else 0.2, None, ALU.mult))
        V.did(dve.tensor_copy(selfs.rearrange("p (b n) -> p b n", b=2), ps[:, 6:8, :]))
        m_tab = V.did(dve.memset(run[0][:, 0, 0:1], 0.0))
        m_res = kept_h[last_g]
        need(dve, ld_3.mark)
        acc3 = acc[:].rearrange("p (b w) -> p b w", w=ACC3)
        need(sp, st_3.mark, m_res, ld_3.mark)
        ld_a = Load("ld_a")
        by_window = T3.rearrange("(b n) w -> n b w", n=WB)
        QTR = BB // 4
        assert QTR * 4 == BB and QTR * ACC3 <= XC and XC + 4300 + 2 * GRP <= 2 * QTR * ACC3
        for b0 in (2 * QTR, 3 * QTR, 0, QTR):
            if b0 == QTR:
                need(sp, m_pt, m_tab)
            for h in range(HEADS):
                ld_a.add(sp.dma_start(acc3[h * WB:(h + 1) * WB, b0:b0 + QTR, :], by_window[:, b0:b0 + QTR, HEADS:ROW3]))

        slots3 = work[:, 0:RINGB * QUAD * ROW3].rearrange("p (q k w) -> p q k w", q=RINGB, k=QUAD)
        PT, PB_, OUT = 0, 2, 4
        names = ("s_bld", "s_pt", "s_ch", "s_ex", "s_pm", "s_pb", "s_cp")
        s_bld, s_pt, s_ch, s_ex, s_pm, s_pb, s_cp = (sem(n) for n in names)
        C = 2
        for e, mine in ((dve, (s_bld, s_ch, s_pm)), (pe, (s_pt, s_pb)), (act, (s_ex, s_cp))):
            need(e, m_tab, (st_3.sem, st_3.n), (s_mm, base["mm"]))
            for s in mine:
                e.sem_inc(s, C)
        need(pool, st_3.mark, (s_mm, base["mm"]))
        b_idx, b_o, b_acc = base["idx"], base["mm"], base["acc"]
        CHAIN = 10

        def at(i, q, mult, extra=0):
            return mult * q + extra if i is None else i * (mult * RINGB) + (mult * q + extra)

        def sl(i, q):
            return bass.ds(at(i, q, QUAD), QUAD) if i is not None else slice(QUAD * q, QUAD * q + QUAD)

        def stage3(i, q):
            act.copy(stage[:, q % RINGB, :], idxB[:, sl(i, q)]).then_inc(s_idx, 1)

        def gather3(i, q):
            pool.wait_ge(s_idx, at(i, q, 1, b_idx + 1))
            pool.sem_inc(s_go, 1)
            for k in range(QUAD):
                pool.indirect_dma_start(
                    out=slots3[:, q % RINGB, k, :], out_offset=None, in_=T3,
                    in_offset=bass.IndirectOffsetOnAxis(ap=stage[:, q % RINGB, k:k + 1], axis=0))\
                    .then_inc(s_g[q % RINGB], 16)

        def slot3(i, q, offs):
            head, chain, weigh, add = q + 4, q + 3, q + 2, q
            if i is None:
                chain, weigh, add = (x if x >= 0 else None for x in (chain, weigh, add))

            def add_step(k):
                if add is None:
                    return
                dve.wait_ge(s_acc, at(i, add, QUAD, b_acc + k))
                bank = OUT + 2 * (add % 2) + k // 2
                o = acc[:, bass.ds(offs[k], ACC3)]
                dve.scalar_tensor_tensor(out=o, in0=o, scalar=corr[:, add % RINGB, k:k + 1],
                                         in1=ps[:, bank, (k % 2) * ACC3:(k % 2 + 1) * ACC3],
                                         op0=ALU.mult, op1=ALU.add).then_inc(s_acc, 1)

            hp = head % 2

            def head_step(k):
                if k == 0:
                    dve.wait_ge(s_pt, at(i, head, 1, C - 1))
                    dve.tensor_tensor(out=pen[hp], in0=iota[:, 0:WB].unsqueeze(1).to_broadcast([P, QUAD, WB]),
                                      in1=relB[:, sl(i, head)].unsqueeze(2).to_broadcast([P, QUAD, WB]),
                                      op=ALU.is_equal).then_inc(s_bld, 1)
                elif k == 1:
                    dve.wait_ge(s_bld, at(i, head, 3, C + 1))
                    dve.tensor_scalar(pen[hp], pen[hp], 1.0, -FAR, ALU.subtract, ALU.mult).then_inc(s_bld, 1)
                else:
                    dve.wait_ge(s_g[head % RINGB], base_g[head % RINGB] + 64 * (head // RINGB + 1) if i is None else
                                i * 64 + (base_g[head % RINGB] + 64 * (head // RINGB + 1)))
                    dve.wait_ge(s_bld, at(i, head, 3, C + 2))
                    dve.tensor_tensor(
                        out=tw[hp].rearrange("p (k h n) -> p k h n", k=QUAD, h=HEADS),
                        in0=slots3[:, head % RINGB, :, 0:HEADS].unsqueeze(3).to_broadcast([P, QUAD, HEADS, WB]),
                        in1=pen[hp].unsqueeze(2).to_broadcast([P, QUAD, HEADS, WB]), op=ALU.add).then_inc(s_bld, 1)

            if weigh is not None:
                wp = weigh % 2
                e1, e2 = ex[wp][:, 0:512], ex[wp][:, 512:1024]

            def weigh_step():
                if weigh is not None:
                    dve.wait_ge(s_ex, at(i, weigh, 1, C + 1))
                    dve.tensor_tensor(out=e1, in0=e1, in1=e2, op=ALU.max).then_inc(s_pm, 1)

            fill = {1: lambda: head_step(0), 2: lambda: add_step(0), 3: lambda: head_step(1),
                    5: lambda: head_step(2), 6: lambda: add_step(1), 7: lambda: add_step(2),
                    8: lambda: add_step(3), 10: weigh_step}
            if chain is None:
                for k in range(3):
                    head_step(k)

            if chain is not None:
                cp = chain % 2
                table = sl(i, chain)
                step = [0]

                def link(ins, awaited=True):
                    ins.then_inc(s_ch, 1)
                    step[0] += 1
                    if step[0] in fill:
                        fill[step[0]]()
                    if awaited:
                        dve.wait_ge(s_ch, at(i, chain, CHAIN, C + step[0]))

                r, b = top[cp], run[cp]
                if add is not None:
                    dve.wait_ge(s_mm, at(i, add, 1, b_o + 1))
                dve.wait_ge(s_pt, at(i, chain, 1, C + 1))
                dve.wait_ge(s_ch, at(i, chain, CHAIN, C))
                link(dve.tensor_reduce(r, ps[:, PT + cp, :].rearrange("p (k e) -> p k e", k=QUAD), AX.X, ALU.max))
                link(dve.tensor_tensor(out=r, in0=r, in1=selfs[:, table], op=ALU.max))
                link(dve.tensor_tensor_scan(out=b[:, 0, 1:5], data0=fresh[:, table], data1=r,
                                            initial=b[:, 0, 0:1], op0=ALU.add, op1=ALU.max))
                link(dve.tensor_copy(run[1 - cp][:, 0, 0:1], b[:, 0, 4:5]), False)
                link(dve.tensor_tensor(out=b[:, 1, 1:5], in0=b[:, 0, 0:4], in1=fresh[:, table], op=ALU.add))
                link(dve.tensor_tensor(out=b[:, 1, 1:5], in0=b[:, 1, 1:5], in1=selfs[:, table], op=ALU.max))
                mm = mx[cp]
                link(dve.tensor_tensor(out=mm, in0=b[:, :, 1:5],
                                       in1=ads[:, 0, table].unsqueeze(1).to_broadcast([P, 2, QUAD]), op=ALU.add))
                link(dve.scalar_tensor_tensor(out=mm, in0=mm, scalar=0.2, in1=mm, op0=ALU.mult, op1=ALU.max))
                link(dve.tensor_tensor(out=drop[cp], in0=mm[:, 1, :], in1=mm[:, 0, :], op=ALU.subtract), False)
                link(dve.tensor_tensor(out=off[cp], in0=ads[:, :, table],
                                       in1=mm[:, 0:1, :].to_broadcast([P, 2, QUAD]), op=ALU.subtract), False)
                act.wait_ge(s_ch, at(i, chain, CHAIN, C + CHAIN))
                act.wait_ge(s_pm, at(i, chain, 1, C - 1))
                act.wait_ge(s_pb, at(i, chain, 1, C - 1))
                act.activation(corr[:, chain % RINGB, :], drop[cp], ACT.Exp)
                for j in range(2):
                    for k in range(QUAD):
                        last = act.activation(ex[cp][:, j * 512 + k * P:j * 512 + (k + 1) * P],
                                              ps[:, PT + cp, k * P:(k + 1) * P], ACT.Exp,
                                              bias=off[cp][:, j, k:k + 1], scale=1.0 if j == 0 else 0.2)
                last.then_inc(s_ex, 1)

            pe.wait_ge(s_bld, at(i, head, 3, C + 3))
            pe.wait_ge(s_ex, at(i, head, 1, C - 1))
            for k in range(QUAD):
                last = pe.transpose(ps[:, PT + hp, k * P:(k + 1) * P], tw[hp][:, k * P:(k + 1) * P], ident)
            last.then_inc(s_pt, 1)

            if weigh is not None:
                pe.wait_ge(s_pm, at(i, weigh, 1, C + 1))
                pe.wait_ge(s_cp, at(i, weigh, 1, C - 1))
                for k in range(QUAD):
                    last = pe.transpose(ps[:, PB_ + wp, k * P:(k + 1) * P], e1[:, k * P:(k + 1) * P], ident)
                last.then_inc(s_pb, 1)
                act.wait_ge(s_pb, at(i, weigh, 1, C + 1))
                act.wait_ge(s_mm, at(i, weigh, 1, b_o - 1))
                act.copy(pw[wp], ps[:, PB_ + wp, :]).then_inc(s_cp, 1)
                pe.wait_ge(s_cp, at(i, weigh, 1, C + 1))
                pe.wait_ge(s_acc, at(i, weigh, QUAD, b_acc - QUAD))
                for k in range(QUAD):
                    bank = OUT + 2 * wp + k // 2
                    o = ps[:, bank, (k % 2) * ACC3:(k % 2 + 1) * ACC3]
                    last = pe.matmul(o, pw[wp][:, k * P:(k + 1) * P], slots3[:, weigh % RINGB, k, HEADS:ROW3],
                                     start=True, stop=True)
                last.then_inc(s_mm, 1)

        for q in range(RINGB):
            stage3(None, q)
            gather3(None, q)
        for q in range(-4, 0):
            slot3(None, q, None)
        act.wait_ge(s_mm, b_o + 1)
        stage3(None, RINGB)
        gather3(None, RINGB)
        need(dve, ld_a.mark)
        with nc.Fori(0, ITERSB) as i:
            for q in range(RINGB):
                if q % 3 == 0:
                    _, offs = nc.values_load_multi_w_load_instructions(
                        winB[0:1, bass.ds(at(i, q, QUAD), 3 * QUAD)], engines=[ENG.DVE], min_val=0,
                        max_val=(BB - 1) * ACC3,
                        skip_runtime_bounds_check_because="b_s counts the windows that have started")
                slot3(i, q, offs[q % 3 * QUAD:(q % 3 + 1) * QUAD])
                act.wait_ge(s_mm, at(i, q + 1, 1, b_o + 1))
                stage3(i, q + 1 + RINGB)
                gather3(i, q + 1 + RINGB)
        quads = RINGB * ITERSB
        for q in range(RINGB):
            need(dve, (s_g[q], base_g[q] + 64 * (ITERSB + 1 + (q == 0))))
        need(dve, (s_acc, b_acc + QUAD * quads), (s_pt, C + quads + 4), (s_pb, C + quads + 2),
             (s_ex, C + quads + 3), (s_mm, b_o + quads + 2), (s_cp, C + quads + 2), (s_idx, b_idx + quads + RINGB + 1))

        zr = flatA[:, 0:BB]
        m = V.did(dve.tensor_scalar(zr, acc3[:, :, D], float(HEADS), None, ALU.mult))
        need(dve, m)
        m = V.did(dve.reciprocal(zr, zr))
        need(dve, m)
        turned_w = [flatA[:, 256 + 512 * k:768 + 512 * k] for k in range(2)]
        WPT = P // WB
        gat = hT[:, 0:NP].rearrange("p (t d) -> p t d", d=D)
        need(act, m)
        need(pool, m)
        st_out = Load("st_out")
        scaled, w_turned, w_free, gat_done, dv, nm, shifted = ({} for _ in range(7))

        def scale_sums(g, lo, hi):
            s4 = slice(WPT * lo, WPT * hi)
            scaled[g] = V.did(dve.tensor_tensor(
                out=acc3[:, s4, 0:D], in0=acc3[:, s4, 0:D],
                in1=zr[:, s4].unsqueeze(2).to_broadcast([P, WPT * (hi - lo), D]), op=ALU.mult))

        def turn_windows(t):
            if t >= 2:
                need(pe, w_turned[t - 2])
            for w in range(WPT):
                last = pe.transpose(ps[:, t % 2, w * P:(w + 1) * P], acc3[:, t * WPT + w, 0:D], ident)
            need(act, T.did(last))
            if t >= 2:
                need(act, w_free[t - 2])
            w_turned[t] = A.did(act.copy(
                turned_w[t % 2].rearrange("p (h w n) -> p w h n", h=HEADS, w=WPT),
                ps[:, t % 2, :].rearrange("p (w h n) -> p w h n", w=WPT, h=HEADS)))

        def heads(g, lo, hi):
            need(pe, scaled[g])
            if g >= 2:
                need(pe, nm[g - 2])
            bank = 4 + g % 2
            for t in range(lo, hi + 1):
                if t < hi:
                    turn_windows(t)
                if t > lo:
                    u = t - 1
                    o = ps[:, bank, (u - lo) * D:(u - lo + 1) * D]
                    need(pe, w_turned[u])
                    pe.matmul(o, ones[0:1, :], BIAS3, start=True, stop=False)
                    for h in range(HEADS):
                        last = pe.matmul(o, turned_w[u % 2][:, h * P:(h + 1) * P], W3[:, h * D:(h + 1) * D],
                                         start=False, stop=(h == HEADS - 1))
                    w_free[u] = T.did(last)
            gat_done[g] = w_free[hi - 1]

        def in_bank(g, lo):
            return lambda t: ps[:, 4 + g % 2, (t - lo) * D:(t - lo + 1) * D]

        def measure3(g, lo, hi):
            dv[g] = deviation(lo, hi, statistics(in_bank(g, lo), lo, hi, gat_done[g]))

        def norm3(g, lo, hi):
            nm[g] = normalise(in_bank(g, lo), lambda t: gat[:, t, :], lo, hi, dv[g])

        def affine(g, lo, hi):
            m = nm[g]
            for vec, op in ((GAMMA, ALU.mult), (BETA, ALU.add)):
                need(pool, m)
                m = G.did(pool.tensor_tensor(out=rows(gat, lo, hi), in0=rows(gat, lo, hi),
                                             in1=vec.unsqueeze(1).to_broadcast([P, hi - lo, D]), op=op))
            shifted[g] = m

        def result(g, lo, hi):
            need(dve, shifted[g])
            m = V.did(dve.scalar_tensor_tensor(out=rows(x_n, lo, hi), in0=rows(gat, lo, hi), scalar=0.0,
                                               in1=rows(x_n, lo, hi), op0=ALU.max, op1=ALU.add))
            need(sp, m)
            full = min(hi, NT - 1)
            if full > lo:
                st_out.add(sp.dma_start(out[lo * P:full * P, :].rearrange("(t p) d -> p t d", p=P),
                                        rows(x_n, lo, full)))
            if hi == NT:
                st_out.add(sp.dma_start(out[(NT - 1) * P:N, :], x_n[0:LAST, NT - 1, :]))

        pipeline(scale_sums, heads, measure3, norm3, affine, result)
        need(sp, st_out.mark)


def kernel(**inputs):
    import concourse.bacc as bacc
    from concourse.bass_utils import run_bass_kernel_spmd

    def arr(name):
        return np.asarray(inputs[name])

    pad = ROWS * P - E
    src = np.concatenate([arr("src"), np.zeros(pad, np.int32)]).reshape(ROWS, P)
    dst = np.concatenate([arr("dst"), np.full(pad, 1 << 20, np.int32)]).reshape(ROWS, P)
    arrays = {
        "x": arr("x"),
        "edges": np.concatenate([src, dst], axis=1),
        "lasts": dst[:, P - 1].reshape(1, ROWS),
        "weights": np.concatenate([arr("edge_weight"), np.zeros(pad, np.float32)]).reshape(ROWS, P),
        "edge_attrT": np.concatenate([arr("edge_attr_128").T, np.zeros((P, ECOLS - E), np.float32)], axis=1),
        "consts": const_table(), "steps": np.arange(TABB, dtype=np.float32).reshape(1, TABB),
        "w0": arr("L0_gnn_weight"), "w1": arr("L1_gnn_W1"), "w2": arr("L1_gnn_W2"),
        "wnT": arr("L2_gnn_W_node").T, "we1T": arr("L2_gnn_W_e1").T, "we2T": arr("L2_gnn_W_e2").T,
        "wf1T": arr("L2_gnn_W_fc1").T, "wf2T": arr("L2_gnn_W_fc2").T,
        "w3": arr("L3_gnn_W"), "w3T": arr("L3_gnn_W").T,
        "att_srcT": arr("L3_gnn_att_src").T, "att_dstT": arr("L3_gnn_att_dst").T,
        "b0": arr("L0_gnn_b").reshape(1, D), "b1a": arr("L1_gnn_b1"), "b1b": arr("L1_gnn_b2"),
        "bn": arr("L2_gnn_b_node").reshape(1, D), "bf2": arr("L2_gnn_b_fc2").reshape(1, D),
        "be2": arr("L2_gnn_b_e2").reshape(1, D),
        "be1": arr("L2_gnn_b_e1").reshape(D, 1), "bf1": arr("L2_gnn_b_fc1").reshape(D, 1),
        "bias3": arr("L3_gnn_bias").reshape(1, D), "gamma3": arr("L3_gnn_ln_gamma").reshape(1, D),
        "beta3": arr("L3_gnn_ln_beta").reshape(1, D),
    }
    arrays = {"in_" + k: np.ascontiguousarray(v) for k, v in arrays.items()}
    nc = bacc.Bacc("TRN2", target_bir_lowering=False, num_devices=1)
    aps = {k[3:]: nc.dram_tensor(k, v.shape, mybir.dt.from_np(v.dtype), kind="ExternalInput").ap()
           for k, v in arrays.items()}
    out = nc.dram_tensor("out", (N, D), F32, kind="ExternalOutput").ap()
    build(nc, aps, out)
    r = run_bass_kernel_spmd(nc, [arrays], core_ids=[0])
    return r.results[0]["out"]
```

```python
from contextlib import ExitStack

import numpy as np

import concourse.bass as bass
from concourse import mybir

F32 = mybir.dt.float32
I32 = mybir.dt.int32
ALU = mybir.AluOpType
ACT = mybir.ActivationFunctionType
AX = mybir.AxisListType
ENG = mybir.EngineType

N, E, D = 6250, 100000, 128
P = 128
NT = -(-N // P)
NP = NT * P
LAST = N - (NT - 1) * P
ET = -(-E // P)
HEADS = 4
LOG2 = float(np.log(2.0))
FAR = -1.0e30
EXP_LN = "natural_log_exp_and_others"

WA, WB = 256, 32
BA, BB = -(-N // WA), -(-N // WB)
QUAD = 4
RINGA, RINGB = 4, 6
STEPSA = QUAD * RINGA * -(-(ET + BA - 1) // (QUAD * RINGA))
STEPSB = QUAD * RINGB * -(-(ET + BB - 1) // (QUAD * RINGB))
ITERSA, ITERSB = STEPSA // (QUAD * RINGA), STEPSB // (QUAD * RINGB)
TABA = P * -(-(STEPSA + QUAD * RINGA) // P)
TABB = P * -(-(STEPSB + QUAD * RINGB) // P)
GB = 2
PB = BB // GB
assert BB % GB == 0
ROWS = TABA
NODESA = BA * WA
GRP = 512
GROUPS = 2 * 2 * ITERSA
ECOLS = (GROUPS + 2) * GRP
ROW3 = HEADS + D + 1
ACC3 = D + 1


def const_layout():
    at, out = 0, {}
    for name, width in (("ident", P), ("iota", WA), ("limA", 2), ("limB", 2 * GB), ("stepcol", TABB // P), ("ones", P)):
        out[name] = (at, at + width)
        at += width
    return out, at


def const_table():
    cols, width = const_layout()
    c = np.zeros((P, width), np.float32)
    p = np.arange(P, dtype=np.float32)

    def put(name, value):
        a, b = cols[name]
        c[:, a:b] = value

    put("ident", np.eye(P))
    put("iota", np.arange(WA)[None, :])
    put("limA", np.stack([WA * p, p], 1))
    lim = np.zeros((P, GB, 2), np.float32)
    for g in range(GB):
        lim[:, g] = np.stack([WB * (g * PB + p), g * PB + p], 1)
    put("limB", lim.reshape(P, -1))
    put("stepcol", np.arange(TABB // P)[None, :] * P + p[:, None])
    put("ones", 1.0)
    return c


class Lane:

    def __init__(self, engine, sem):
        self.e, self.sem, self.n = engine, sem, 0

    def did(self, ins):
        self.n += 1
        ins.then_inc(self.sem, 1)
        return (self.sem, self.n)


def need(engine, *marks):
    for sem, value in marks:
        engine.wait_ge(sem, value)


def build(nc, a, out):
    with ExitStack() as ctx:
        def sb(name, shape, dt=F32):
            return ctx.enter_context(nc.sbuf_tensor("t_" + name, shape, dt))

        def sem(name):
            return ctx.enter_context(nc.semaphore(name))

        def dram(name, shape, dt=F32):
            return nc.dram_tensor("d_" + name, shape, dt, kind="Internal").ap()

        pe, dve, act, pool, sp = nc.tensor, nc.vector, nc.scalar, nc.gpsimd, nc.sync
        V = Lane(dve, sem("v_done"))
        A = Lane(act, sem("a_done"))
        T = Lane(pe, sem("t_done"))
        G = Lane(pool, sem("g_done"))

        class Load:

            def __init__(self, name):
                self.sem, self.n = sem(name), 0

            def add(self, ins, k=1):
                ins.then_inc(self.sem, 16)
                self.n += 16 * k
                return (self.sem, self.n)

            @property
            def mark(self):
                return (self.sem, self.n)

        cols, cwidth = const_layout()
        cst = sb("cst", [P, cwidth])

        def c_(name):
            x, y = cols[name]
            return cst[:, x:y]

        ident, iota, ones = c_("ident"), c_("iota"), c_("ones")
        x_n = sb("x", [P, NT, D])
        hT = sb("hT", [P, NODESA])
        acc = sb("acc", [P, BB * ACC3])
        work = sb("work", [P, QUAD * RINGA * ACC3 + 2 * QUAD * WA])
        assert QUAD * RINGB * ROW3 <= work.shape[1]
        masks = work[:, QUAD * RINGA * ACC3:].rearrange("p (s k w) -> p s k w", s=2, k=QUAD)
        tabA = sb("tabA", [P, 3, TABA])
        idxA, relA, wgtA = tabA[:, 0, :].bitcast(I32), tabA[:, 1, :], tabA[:, 2, :]
        idxB = sb("idxB", [P, TABB], I32)
        relB = sb("relB", [P, TABB])
        stage = sb("stage", [P, RINGB, QUAD], I32)
        winA, tileA = sb("winA", [1, TABA], I32), sb("tileA", [1, TABA], I32)
        winB = sb("winB", [1, TABB], I32)
        wts = sb("wts", [P, 8, D])
        W0, W1, W2, WN, WE1, WE2, WF1, WF2 = (wts[:, k, :] for k in range(8))
        bias = sb("bias", [P, 5, D])
        bcol = sb("bcol", [P, 8])
        rn = sb("rn", [P, 2, NT])
        halves = sb("halves", [P, NT, 6])
        meanvar = sb("meanvar", [P, NT, 2])
        dev = sb("dev", [P, 2, NT])
        small = sb("small", [P, 64])

        XC, SQ = NT * P + 2 * ACC3 + 2, NT * P + 2 * ACC3 + 2 + NP
        MLP = SQ + NT * ROW3

        def mlp(k, n=1):
            assert MLP + (k + n) * GRP <= BB * ACC3
            return acc[:, MLP + k * GRP:MLP + (k + n) * GRP]

        ps = ctx.enter_context(nc.psum_tensor("ps", [P, 8, 512], F32))

        edge_net = dram("edge_net", [(1 + GROUPS) * QUAD, P, D])
        T0, T1, T2, T3 = dram("T0", [NP, D + 1]), dram("T1", [NP, D]), dram("T2", [NP, D]), dram("T3", [NP, ROW3])
        scores = dram("scores", [2 * HEADS, NP])
        windows_b = dram("windows_b", [1, TABB])

        ld_c, ld_x, ld_w = Load("ld_c"), Load("ld_x"), Load("ld_w")
        ld_l = Load("ld_l")
        scratch, at_scratch = acc[:, NT * ACC3 + 2 * ACC3 + 150:], [0]

        def take(n):
            lo = at_scratch[0]
            at_scratch[0] += n
            return scratch[:, lo:lo + n]

        lastb = take(ROWS).bitcast(I32)
        ld_l.add(sp.dma_start(lastb, a["lasts"].to_broadcast([P, ROWS])))
        ld_c.add(sp.dma_start(cst[:], a["consts"]))
        steps = hT[:, 4 * TABB:5 * TABB]
        ld_c.add(sp.dma_start(steps, a["steps"].to_broadcast([P, TABB])))
        x_pad = V.did(dve.memset(x_n[:, NT - 1, :], 0.0))
        for lo in range(0, NT - 1, 12):
            hi = min(lo + 12, NT - 1)
            ld_x.add(sp.dma_start(x_n[:, lo:hi, :], a["x"][lo * P:hi * P, :].rearrange("(t p) d -> p t d", p=P)))
        need(sp, x_pad)
        ld_x.add(sp.dma_start(x_n[0:LAST, NT - 1, :], a["x"][(NT - 1) * P:N, :]))
        for k, name in enumerate(("w0", "w1", "w2", "wnT", "we1T", "we2T", "wf1T", "wf2T")):
            ld_w.add(act.dma_start(wts[:, k, :], a[name]))
        for k, name in enumerate(("b0", "b1a", "b1b", "bn", "bf2")):
            ld_w.add(act.dma_start(bias[:, k, :], a[name].to_broadcast([P, D])))
        B0, B1, B1B, BN, BF2 = (bias[:, k, :] for k in range(5))
        be2row = sb("be2row", [1, D])
        ld_w.add(act.dma_start(be2row[:], a["be2"]))
        ld_w.add(act.dma_start(bcol[:, 0:1], a["be1"]))
        ld_w.add(act.dma_start(bcol[:, 1:2], a["bf1"]))
        eps_c = small[:, 49:50]
        m_eps = V.did(dve.memset(eps_c, 1e-5))
        need(act, m_eps)

        GRS = [(lo, min(lo + 4, NT)) for lo in range(0, NT, 4)]

        def pipeline_step(step, *stages):
            for k in reversed(range(len(stages))):
                if 0 <= step - k < len(GRS):
                    stages[k](step - k, *GRS[step - k])

        def pipeline(*stages):
            for step in range(len(GRS) + len(stages) - 1):
                pipeline_step(step, *stages)

        def rows(view, lo, hi):
            return view[:, lo:hi, :]

        def banked(bank, n):
            return ps[:, bank, 0:n * D].rearrange("p (t d) -> p t d", d=D)

        def spread(v, n):
            return v.unsqueeze(2).to_broadcast([P, n, D])

        def statistics(src_of, lo, hi, ready):
            need(dve, ready)
            for t in range(lo, hi):
                m = V.did(dve.bn_stats(halves[:, t, :], src_of(t)))
            need(dve, m)
            for t in range(lo, hi):
                m = V.did(dve.bn_aggr(meanvar[:, t, :], halves[:, t, :]))
            return m

        def deviation(lo, hi, ready):
            need(act, ready)
            return A.did(act.activation(dev[:, 0, lo:hi], meanvar[:, lo:hi, 1], ACT.Sqrt, bias=eps_c))

        def normalise(src_of, dst_of, lo, hi, ready):
            need(dve, ready)
            need(dve, V.did(dve.reciprocal(dev[:, 1, lo:hi], dev[:, 0, lo:hi])))
            for t in range(lo, hi):
                m = V.did(dve.tensor_scalar(dst_of(t), src_of(t), meanvar[:, t, 0:1], dev[:, 1, t:t + 1],
                                            ALU.subtract, ALU.mult))
            return m

        def rectify(view, lo, hi, ready):
            need(act, ready)
            return A.did(act.activation(rows(view, lo, hi), rows(view, lo, hi), ACT.Relu))

        def x_of(t):
            return x_n[:, t, :]

        def turn(g, lo, hi, src_of, ready, marks, dst, bank0):
            need(pe, ready)
            if g >= 2:
                need(pe, marks[g - 2])
            bank = bank0 + g % 2
            for t in range(lo, hi):
                last = pe.transpose(ps[:, bank, (t - lo) * P:(t - lo + 1) * P], src_of(t), ident)
            need(act, T.did(last))
            marks[g] = A.did(act.copy(dst[:, lo * P:hi * P], ps[:, bank, 0:(hi - lo) * P]))

        def project(lo, hi, bank, pairs, ready):
            need(pe, *ready)
            for t in range(lo, hi):
                for j, (lhs, w) in enumerate(pairs):
                    last = pe.matmul(ps[:, bank, (t - lo) * D:(t - lo + 1) * D], lhs[:, t * P:(t + 1) * P], w,
                                     start=(j == 0), stop=(j == len(pairs) - 1))
            return T.did(last)

        def with_bias(engine, lane, out_rows, in_rows, brow, n, ready):
            need(engine, ready)
            return lane.did(engine.tensor_tensor(out=out_rows, in0=in_rows,
                                                 in1=brow.unsqueeze(1).to_broadcast([P, n, D]), op=ALU.add))

        def add_to_x(lo, hi, bank, ready):
            need(dve, ready)
            return V.did(dve.tensor_tensor(out=rows(x_n, lo, hi), in0=rows(x_n, lo, hi), in1=banked(bank, hi - lo),
                                           op=ALU.add))

        def store_rows(ld, table, src, lo, hi, ready):
            need(sp, *ready)
            ld.add(sp.dma_start(table.rearrange("(t p) w -> p t w", p=P)[:, lo:hi, :], rows(src, lo, hi)))

        lastf, cmp = take(ROWS), take(ROWS)
        need(dve, ld_l.mark)
        m = V.did(dve.tensor_copy(lastf, lastb))
        need(dve, m, ld_c.mark)
        la, _ = cols["limA"]
        lb, _ = cols["limB"]
        first = small[:, 0:8]
        startedA, startedB = take(TABA), [take(TABB) for g in range(GB)]
        CA, CB = TABA // P, TABB // P
        halfA, halfB = TABA // 2, TABB // 2
        bcA = ps[:, 0:2, 0:halfA]
        bcB = ps[:, 2:4, 0:halfB]
        tcol = sb("tcol", [P, 16], I32)
        wcol = small[:, 16:32]
        tcf = small[:, 32:48]

        def mark_started(k, n, c, dst, width):
            m = V.did(dve.tensor_scalar(cmp[0:n, :], lastf[0:n, :], cst[0:n, c:c + 1], None, ALU.is_lt))
            need(dve, m)
            m = V.did(dve.tensor_reduce(first[0:n, k:k + 1], cmp[0:n, :], AX.X, ALU.add))
            need(dve, m)
            m = V.did(dve.tensor_tensor(out=first[0:n, k:k + 1], in0=first[0:n, k:k + 1],
                                        in1=cst[0:n, c + 1:c + 2], op=ALU.add))
            need(dve, m)
            return V.did(dve.tensor_scalar(dst[0:n, :], steps[0:n, 0:width], first[0:n, k:k + 1], None, ALU.is_ge))

        def count_columns(parts, n, chunks, off):
            for c in range(chunks):
                for g, part in enumerate(parts):
                    last = pe.matmul(ps[:, 4, off + c:off + c + 1], part[0:n, c * P:(c + 1) * P], ones[0:n, 0:1],
                                     start=(g == 0), stop=(g == len(parts) - 1))
            return T.did(last)

        def place_columns(base, n, off, w):
            x0, _ = cols["stepcol"]
            m = V.did(dve.tensor_tensor(out=tcf[:, base:base + n], in0=cst[:, x0:x0 + n],
                                        in1=ps[:, 4, off:off + n], op=ALU.subtract))
            need(dve, m)
            V.did(dve.tensor_scalar(tcol[:, base:base + n], tcf[:, base:base + n], 1.0, None, ALU.add))
            return V.did(dve.tensor_scalar(wcol[:, base:base + n], ps[:, 4, off:off + n], 1.0, float(w),
                                           ALU.subtract, ALU.mult))

        need(pe, mark_started(0, BA, la, startedA, TABA))
        m = count_columns([startedA], BA, CA, 0)
        m_b = mark_started(1, PB, lb, startedB[0], TABB)
        need(dve, m)
        need(pool, place_columns(0, CA, 0, WA))

        SLOTS = 3
        got = [sem(f"got{k}") for k in range(SLOTS)]
        edges = [take(2 * P).bitcast(I32) for k in range(SLOTS)]
        wraw = [take(P) for k in range(SLOTS)]
        ef = [take(2 * P) for k in range(SLOTS)]
        n_got = [0] * SLOTS

        acc0 = acc[:, 0:2 * BA * ACC3].rearrange("p (t w) -> p t w", w=ACC3)
        pool.memset(acc0[:, NT:2 * BA, :], 0.0)
        ones_set = G.did(pool.memset(acc0[:, 0:NT, D:ACC3], 1.0))
        st_0, dv0, nm0, b0_added = Load("st_0"), {}, {}, {}

        def table0_measure(g, lo, hi):
            dv0[g] = deviation(lo, hi, statistics(x_of, lo, hi, ld_x.mark))

        def table0_scale(g, lo, hi):
            nm0[g] = normalise(x_of, lambda t: acc0[:, t, 0:D], lo, hi, dv0[g])

        def table0_finish(g, lo, hi):
            m = rectify(acc0[:, :, 0:D], lo, hi, nm0[g])
            store_rows(st_0, T0, acc0, lo, hi, [m, ones_set])

        class Turner:

            def __init__(self, path, raws, weights, floats, banks):
                self.path, self.raws, self.weights, self.floats, self.banks = path, raws, weights, floats, banks
                self.turned, self.freed = {}, {}

            def gather(self, c):
                k = c % len(self.raws)
                if c >= len(self.raws):
                    need(pool, self.freed[c - len(self.raws)])
                col = c + (0 if self.path == "A" else 8)
                for dst, table in ((self.raws[k], "edges"), *([(self.weights[k], "weights")] if self.weights else [])):
                    pool.indirect_dma_start(
                        out=dst, out_offset=None, in_=a[table],
                        in_offset=bass.IndirectOffsetOnAxis(ap=tcol[:, col:col + 1], axis=0)).then_inc(got[k], 16)
                    n_got[k] += 16

            def turn(self, c):
                k = c % len(self.raws)
                col = c + (0 if self.path == "A" else 8)
                need(dve, (got[k], n_got[k]))
                if c >= len(self.raws):
                    need(dve, self.turned[c - len(self.raws)])
                if c >= len(self.banks):
                    need(pe, self.freed[c - len(self.banks)])
                V.did(dve.tensor_copy(self.floats[k][:, 0:P], self.raws[k][:, 0:P]))
                m = V.did(dve.tensor_scalar(self.floats[k][:, P:2 * P], self.raws[k][:, P:2 * P],
                                            wcol[:, col:col + 1], None, ALU.subtract))
                need(pe, m)
                bank = self.banks[c % len(self.banks)]
                pe.transpose(ps[:, bank, 0:P], self.floats[k][:, 0:P], ident)
                last = pe.transpose(ps[:, bank, P:2 * P], self.floats[k][:, P:2 * P], ident)
                if self.weights:
                    need(pe, (got[k], n_got[k]))
                    last = pe.transpose(ps[:, bank, 2 * P:3 * P], self.weights[k], ident)
                self.turned[c] = T.did(last)

            def keep(self, c):
                bank = self.banks[c % len(self.banks)]
                need(dve, self.turned[c])
                idx, rel = (idxA, relA) if self.path == "A" else (idxB, relB)
                cs = slice(c * P, (c + 1) * P)
                V.did(dve.tensor_copy(idx[:, cs], ps[:, bank, 0:P]))
                self.freed[c] = V.did(dve.tensor_copy(rel[:, cs], ps[:, bank, P:2 * P]))
                if self.weights:
                    self.freed[c] = V.did(dve.tensor_copy(wgtA[:, cs], ps[:, bank, 2 * P:3 * P]))

        turner = Turner("A", edges, wraw, ef, (5, 6, 7))
        for step in range(len(GRS) + 2):
            if step < CA:
                turner.gather(step)
                turner.turn(step)
                turner.keep(step)
                if step > 0 and step < GB:
                    m_b = mark_started(1 + step, PB, lb + 2 * step, startedB[step], TABB)
            pipeline_step(step, table0_measure, table0_scale, table0_finish)
        assert GB <= CA <= len(GRS) and CB <= len(GRS)
        need(pool, ld_w.mark)
        for g, (lo, hi) in enumerate(GRS):
            b0_added[g] = with_bias(pool, G, rows(x_n, lo, hi), rows(x_n, lo, hi), B0, hi - lo, nm0[g])
        tables = turner.freed[CA - 1]

        need(pe, m_b)
        for h in range(2):
            pe.matmul(ps[:, h, 0:halfA], ones[0:BA, :], startedA[0:BA, h * halfA:(h + 1) * halfA],
                      start=True, stop=True)
            for g in range(GB):
                pe.matmul(ps[:, 2 + h, 0:halfB], ones[0:PB, :], startedB[g][0:PB, h * halfB:(h + 1) * halfB],
                          start=(g == 0), stop=(g == GB - 1))
        need(dve, count_columns(startedB, PB, CB, 16))
        place_columns(8, CB, 16, WB)
        for win, counts, width in ((winA, bcA, 2 * ACC3), (winB, bcB, ACC3)):
            V.did(dve.tensor_scalar(win[:].rearrange("p (h n) -> p h n", h=2), counts[0:1], 1.0, float(width),
                                    ALU.subtract, ALU.mult))
        m = V.did(dve.tensor_tensor(
            out=tileA[:].rearrange("p (h n) -> p h n", h=2),
            in0=steps[0:1, 0:TABA].rearrange("p (h n) -> p h n", h=2), in1=bcA[0:1], op=ALU.subtract))
        need(dve, m)
        V.did(dve.tensor_scalar(tileA[:], tileA[:], 1.0, None, ALU.add))
        assert at_scratch[0] + TABB <= MLP - (NT + 2) * ACC3 - 150
        win_f = take(TABB)[0:1, :]
        m_win = V.did(dve.tensor_copy(win_f.rearrange("p (h n) -> p h n", h=2), bcB[0:1]))
        need(sp, m_win)
        kept = Load("kept")
        kept.add(sp.dma_start(windows_b, win_f))

        need(dve, ld_w.mark)
        V.did(dve.tensor_scalar(bcol[:, 2:4], bcol[:, 0:2], -1.0, 40.0, ALU.mult, ALU.add))
        V.did(dve.tensor_scalar(bcol[:, 4:6], bcol[:, 0:2], -LOG2, None, ALU.add))
        V.did(dve.tensor_tensor(out=B1, in0=B1, in1=B1B, op=ALU.add))
        V.did(dve.memset(bcol[:, 6:7], 40.0))
        prepared = V.did(dve.memset(bcol[:, 7:8], 0.5))
        forty, halfc = bcol[:, 6:7], bcol[:, 7:8]
        need(act, prepared)

        s_idx, s_msk, s_mm, s_acc, s_mul = (sem(n) for n in ("s_idx", "s_msk", "s_mm", "s_acc", "s_mul"))
        s_go = sem("s_go")
        s_g = [sem(f"s_g{q}") for q in range(RINGB)]
        s_ef = [sem(f"s_ef{q}") for q in range(RINGA)]
        base = dict(idx=0, msk=0, mm=RINGA, acc=2 * QUAD, mul=RINGA)
        base_g = [0] * RINGB
        pe.sem_inc(s_mm, RINGA)
        dve.sem_inc(s_acc, 2 * QUAD)
        dve.sem_inc(s_mul, RINGA)
        s_ei = [sem(f"s_ei{k}") for k in range(2)]
        s_es = [sem(f"s_es{k}") for k in range(2)]
        s_z, s_ac, s_pw = (sem(n) for n in ("s_z", "s_ac", "s_pw"))
        PWC = 1
        dve.sem_inc(s_pw, PWC)
        ein = [mlp(k) for k in range(2)]
        efo = [mlp(2 + k) for k in range(2)]
        sp1, ar, ae, al = mlp(4), mlp(5), mlp(6), mlp(7)
        need(sp, tables)
        for k in range(2):
            sp.dma_start(efo[k][:, 0:D], a["we1T"]).then_inc(s_es[k], 16)
        for k in range(2):
            sp.dma_start(ein[k], a["edge_attrT"][:, k * GRP:(k + 1) * GRP]).then_inc(s_ei[k], 16)
        flat = ps[:].rearrange("p b n -> p (b n)")

        def sums_of(layer, par, k):
            if layer > 0:
                return ps[:, 2 * par + k // 2, (k % 2) * WA:(k % 2 + 1) * WA]
            c = 2 * k
            at = [par * 3 * 512 + (x // 3) * 512 + (x % 3) * ACC3 for x in (c, c + 1)]
            step = at[1] - at[0]
            return flat[:, at[0]:at[0] + 2 * step].rearrange("p (j n) -> p j n", j=2)[:, :, 0:ACC3]

        def softplus_part(z, b40):
            return ((ar, z, ACT.Relu, b40, -1.0), (ae, ar, ACT.Exp, forty, -1.0), (al, ae, ACT.Ln, halfc, 0.5))

        def net_product(q, event, ready):
            need(pe, *ready)
            z = ps[:, 6 + q % 2, :]
            if q < 2:
                pe.matmul(z, WE1, ein[q], start=True, stop=True).then_inc(s_z, 1)
                return
            pe.matmul(z, ones[0:1, :], be2row[:].unsqueeze(1).to_broadcast([1, QUAD, D]), start=True, stop=False)
            for k in range(QUAD):
                last = pe.matmul(z[:, k * D:(k + 1) * D], sp1[:, k * P:(k + 1) * P], WE2, start=False,
                                 stop=(k == QUAD - 1))
            last.then_inc(s_z, 1)

        def net_chain(q, event, event3):
            act.wait_ge(s_z, event + 1)
            for j, (dst, src, f, bb, sc) in enumerate(softplus_part(ps[:, 6 + q % 2, :], bcol[:, 2:3] if q < 2 else forty)):
                if j:
                    act.wait_ge(s_ac, event3 + j)
                if j == 2:
                    act.wait_ge(s_pw, event + PWC)
                act.activation(dst, src, f, bias=bb, scale=sc).then_inc(s_ac, 1)

        def net_softplus(q, event, event3, turns):
            dve.wait_ge(s_ac, event3 + 3)
            if q < 2:
                dve.wait_ge(s_z, event + 2 * q)
                o, b2 = sp1, bcol[:, 4:5]
            else:
                dve.wait_ge(s_es[q - 2], turns * 16 + 16)
                o, b2 = efo[q - 2], -LOG2
            dve.scalar_tensor_tensor(out=o, in0=ps[:, 6 + q % 2, :], scalar=b2, in1=al, op0=ALU.add, op1=ALU.max)\
                .then_inc(s_pw, 1)

        def net_store(h, event, row):
            sp.wait_ge(s_pw, event + (1 + PWC))
            dst = edge_net[row:row + QUAD, :, :] if isinstance(row, int) else edge_net[bass.ds(row, QUAD), :, :]
            sp.dma_start(dst.rearrange("t p d -> p t d"), efo[h].rearrange("p (t d) -> p t d", d=D))\
                .then_inc(s_es[h], 16)

        def edge_loop(layer, table, deps):
            width = table.shape[1]
            slots = work[:, 0:QUAD * RINGA * width].rearrange("p (q k w) -> p q k w", q=RINGA, k=QUAD)
            net = layer < 2
            ef_in = acc[:, XC:XC + RINGA * QUAD * D].rearrange("p (q k w) -> p q k w", q=RINGA, k=QUAD)
            b_idx, b_msk, b_mm, b_acc, b_mul = (base[k] for k in ("idx", "msk", "mm", "acc", "mul"))
            bg = list(base_g)
            i0 = ITERSA * layer
            for e in (pe, dve, act, pool, sp):
                need(e, *deps)

            def stage_indices(n, col, slot):
                act.wait_ge(s_mm, n + (1 - RINGA + b_mm))
                act.copy(stage[:, slot, :], idxA[:, bass.ds(col, QUAD)]).then_inc(s_idx, 1)

            def make_mask(col, par, k):
                r = relA[:, bass.ds(col, 1)]
                if layer == 1:
                    return dve.tensor_scalar(masks[:, par, k, :], iota, r, wgtA[:, bass.ds(col, 1)],
                                             ALU.is_equal, ALU.mult)
                return dve.tensor_scalar(masks[:, par, k, :], iota, r, None, ALU.is_equal)

            def load_net_rows(n, col, slot):
                sp.wait_ge(s_mul, n + (1 - RINGA + b_mul))
                _, tiles = nc.values_load_multi_w_load_instructions(
                    tileA[0:1, bass.ds(col, QUAD)], engines=[ENG.SP], min_val=0, max_val=GROUPS * QUAD - 1,
                    skip_runtime_bounds_check_because="s - b_s; b_s counts the windows that have started")
                for k, t in enumerate(tiles):
                    sp.dma_start(ef_in[:, slot, k, :], edge_net[bass.ds(t + QUAD, 1), :, :].rearrange("t p d -> p (t d)"))\
                        .then_inc(s_ef[slot], 16)

            if net:
                act.preload_act_table_set(EXP_LN)
            if layer == 0:
                net_product(3, 0, [V.did(dve.memset(sp1, 0.0))])
                net_chain(3, 0, 0)
            def gather(n, slot):
                pool.wait_ge(s_idx, n + (1 + b_idx))
                pool.sem_inc(s_go, 1)
                for k in range(QUAD):
                    pool.indirect_dma_start(
                        out=slots[:, slot, k, :], out_offset=None, in_=table,
                        in_offset=bass.IndirectOffsetOnAxis(ap=stage[:, slot, k:k + 1], axis=0)).then_inc(s_g[slot], 16)

            def multiply(turn, slot):
                dve.wait_ge(s_g[slot], turn * 64 + (64 + bg[slot]))
                dve.wait_ge(s_ef[slot], turn * 64 + 64)
                dve.tensor_tensor(out=slots[:, slot, :, :], in0=slots[:, slot, :, :], in1=ef_in[:, slot, :, :],
                                  op=ALU.mult).then_inc(s_mul, 1)

            for q in range(RINGA - 1):
                stage_indices(q, q * QUAD, q)
                if layer == 2:
                    load_net_rows(q, q * QUAD, q)
            for q in range(2):
                for k in range(QUAD):
                    ins = make_mask(q * QUAD + k, q, k)
                ins.then_inc(s_msk, 1)
            if layer == 2:
                gather(0, 0)
                multiply(0, 0)

            with nc.Fori(0, ITERSA) as i:
                _, offv = nc.values_load_multi_w_load_instructions(
                    winA[0:1, bass.ds(i * (QUAD * RINGA), QUAD * RINGA)], engines=[ENG.DVE], min_val=0,
                    max_val=(BA - 1) * 2 * ACC3,
                    skip_runtime_bounds_check_because="b_s counts the windows that have started")
                for q in range(RINGA):
                    nq = i * RINGA + q
                    col = i * (QUAD * RINGA) + q * QUAD
                    par = q % 2
                    ahead = (q + RINGA - 1) % RINGA
                    if layer < 2:
                        gather(nq, q)
                    stage_indices(nq + (RINGA - 1), col + (RINGA - 1) * QUAD, ahead)
                    if layer == 2:
                        load_net_rows(nq + (RINGA - 1), col + (RINGA - 1) * QUAD, ahead)
                        after = (q + 1) % RINGA
                        gather(nq + 1, after)
                        multiply(i + (q + 1) // RINGA, after)
                        pe.wait_ge(s_mul, nq + (1 + b_mul))
                    else:
                        pe.wait_ge(s_g[q], i * 64 + (64 + bg[q]))
                    pe.wait_ge(s_msk, nq + (1 + b_msk))
                    pe.wait_ge(s_acc, nq * QUAD + (b_acc - QUAD))
                    for k in range(QUAD):
                        o = sums_of(layer, par, k)
                        if layer == 0:
                            for j in range(WA // P):
                                last = pe.matmul(o[:, j, :], masks[:, par, k, j * P:(j + 1) * P], slots[:, q, k, :],
                                                 start=True, stop=True)
                        else:
                            last = pe.matmul(o, slots[:, q, k, :], masks[:, par, k, :], start=True, stop=True)
                    last.then_inc(s_mm, 1)
                    dve.wait_ge(s_mm, nq + (1 + b_mm))
                    for k in range(QUAD):
                        ins = make_mask(col + (2 * QUAD + k), par, k)
                        if k == QUAD - 1:
                            ins.then_inc(s_msk, 1)
                        dve.wait_ge(s_acc, nq * QUAD + (k + b_acc))
                        if layer == 0:
                            o = acc[:, bass.ds(offv[q * QUAD + k], 2 * ACC3)].rearrange("p (j n) -> p j n", j=2)
                        else:
                            o = acc[:, bass.ds(offv[q * QUAD + k], WA)]
                        dve.tensor_tensor(out=o, in0=o, in1=sums_of(layer, par, k), op=ALU.add).then_inc(s_acc, 1)
                    if not net:
                        continue
                    event, event3 = i * 4 + (4 * i0 + q + 1), i * 12 + (12 * i0 + 3 * q + 3)
                    ready = [(s_pw, event + (PWC - 1))]
                    if q < 2:
                        ready.append((s_ei[q], i * 16 + (16 * i0 + 16)))
                    net_product(q, event, ready)
                    net_chain(q, event, event3)
                    net_softplus((q + 3) % 4, i * 4 + (4 * i0 + q), i * 12 + (12 * i0 + 3 * q), i + i0)
                    if q == 0:
                        net_store(1, i * 4 + 4 * i0, i * (2 * QUAD) + 2 * i0 * QUAD)
                    if q == 3:
                        net_store(0, i * 4 + (4 * i0 + 3), i * (2 * QUAD) + (2 * i0 + 1) * QUAD)
                    if q < 2:
                        sp.wait_ge(s_z, event + 1)
                        sp.dma_start(ein[q], a["edge_attrT"][:, bass.ds(i * (2 * GRP) + (2 * i0 + q + 2) * GRP, GRP)])\
                            .then_inc(s_ei[q], 16)
            if layer == 1:
                events = 8 * ITERSA
                net_softplus(3, events, 3 * events, 2 * ITERSA)
                net_store(1, events, GROUPS * QUAD)
            quads = RINGA * ITERSA
            base.update(idx=b_idx + quads + RINGA - 1, msk=b_msk + quads + 2, mm=b_mm + quads,
                        acc=b_acc + QUAD * quads, mul=b_mul + (quads + 1 if layer == 2 else 0))
            for q in range(RINGA):
                base_g[q] += 64 * (ITERSA + (layer == 2 and q == 0))
            over = [(s_acc, base["acc"]), (s_mm, base["mm"]), (s_idx, base["idx"]), (s_msk, base["msk"])]
            if layer == 1:
                over += [(s_ei[k], 16 * (2 * ITERSA + 1)) for k in range(2)]
                over += [(s_es[k], 16 * (2 * ITERSA + 1 + k)) for k in range(2)]
                over += [(s_ac, 3 * (events + 1)), (s_pw, events + 1 + PWC)]
            if layer == 2:
                over += [(s_mul, base["mul"])] + [(s_ef[q], 64 * (ITERSA + (q < RINGA - 1))) for q in range(RINGA)]
            return over

        laps = acc[:, 0:BA * 2 * ACC3].rearrange("p (b w) -> p b w", b=BA)

        def lap_of(lo, hi):
            if (hi - lo) % 2:
                assert hi - lo == 1
                return laps[:, lo // 2, 0:P]
            return laps[:, lo // 2:hi // 2, 0:WA]

        over = edge_loop(0, T0, [st_0.mark, prepared, tables, kept.mark])
        for e in (pe, dve, act, pool, sp):
            need(e, *over)
        counts_inv = rn[:, 1, :]
        need(pool, V.did(dve.reciprocal(counts_inv, acc0[:, 0:NT, D])))
        means = acc[:, XC:XC + NP].rearrange("p (t d) -> p t d", d=D)
        hn = acc[:, SQ:SQ + NP].rearrange("p (t d) -> p t d", d=D)
        avg, m_turned, m_proj, added, dv, nm, relu, h_turned = ({} for _ in range(8))
        st_1 = Load("st_1")

        def average(g, lo, hi):
            avg[g] = G.did(pool.tensor_tensor(out=rows(means, lo, hi), in0=acc0[:, lo:hi, 0:D],
                                              in1=spread(counts_inv[:, lo:hi], hi - lo), op=ALU.mult))

        def add_product(g, lo, hi):
            bank = 4 + g % 2
            need(dve, b0_added[g])
            mm = project(lo, hi, bank, [(hT, W0)], [m_turned[g]] + ([added[g - 2]] if g >= 2 else []))
            added[g] = add_to_x(lo, hi, bank, mm)

        def measure(g, lo, hi):
            dv[g] = deviation(lo, hi, statistics(x_of, lo, hi, added[g]))

        def scale_rows(g, lo, hi):
            nm[g] = normalise(x_of, lambda t: hn[:, t, :], lo, hi, dv[g])

        def finish_rows(g, lo, hi):
            relu[g] = rectify(hn, lo, hi, nm[g])
            store_rows(st_1, T1, hn, lo, hi, [relu[g]])

        def turn_rows(g, lo, hi):
            turn(g, lo, hi, lambda t: hn[:, t, :], relu[g], h_turned, hT, 2)

        pipeline(average, lambda g, lo, hi: turn(g, lo, hi, lambda t: means[:, t, :], avg[g], m_turned, hT, 0),
                 add_product, measure, scale_rows, finish_rows, turn_rows)
        last_g = len(GRS) - 1
        need(pool, avg[last_g])
        zeroed = G.did(pool.memset(laps, 0.0))

        over = edge_loop(1, T1, [st_1.mark, zeroed, h_turned[last_g]])
        for e in (pe, dve, act, pool, sp):
            need(e, *over)
        u, v = acc[:, XC:XC + NP], acc[:, SQ:SQ + NP]
        uv, used, drawn, bent, squared, nrm, added, dv, nm, relu, h_turned, made = ({} for _ in range(12))
        st_2 = Load("st_2")
        squares = [mlp(k)[:, 0:D] for k in range(2)]

        def combine(g, lo, hi):
            cs, lap = slice(lo * P, hi * P), lap_of(lo, hi)

            def shaped(view):
                return view if hi - lo == 1 else view.rearrange("p (b w) -> p b w", w=WA)

            G.did(pool.tensor_tensor(out=shaped(u[:, cs]), in0=shaped(hT[:, cs]), in1=lap, op=ALU.add))
            uv[g] = G.did(pool.tensor_tensor(out=shaped(v[:, cs]), in0=shaped(hT[:, cs]), in1=lap, op=ALU.mult))
            if g == last_g:
                need(pool, uv[g])
                uv["zeroed"] = G.did(pool.memset(laps, 0.0))

        def product1(g, lo, hi):
            bank = 4 + g % 2
            used[g] = project(lo, hi, bank, [(u, W1), (v, W2)], [uv[g]] + ([drawn[g - 2]] if g >= 2 else []))
            drawn[g] = with_bias(dve, V, rows(hn, lo, hi), banked(bank, hi - lo), B1, hi - lo, used[g])

        def bend(g, lo, hi):
            need(dve, drawn[g])
            bent[g] = V.did(dve.scalar_tensor_tensor(out=rows(hn, lo, hi), in0=rows(hn, lo, hi), scalar=0.2,
                                                     in1=rows(hn, lo, hi), op0=ALU.mult, op1=ALU.max))
            need(act, bent[g])
            for t in range(lo, hi):
                if t >= 2:
                    need(act, squared[t - 2])
                squared[t] = A.did(act.activation(squares[t % 2], hn[:, t, :], ACT.Square, accum_out=rn[:, 0, t:t + 1]))

        def norms(g, lo, hi):
            need(act, squared[hi - 1])
            nrm[g] = A.did(act.activation(rn[:, 0, lo:hi], rn[:, 0, lo:hi], ACT.Sqrt))

        def add_normed(g, lo, hi):
            need(dve, nrm[g])
            need(dve, V.did(dve.tensor_scalar(rn[:, 0, lo:hi], rn[:, 0, lo:hi], 1e-12, None, ALU.max)))
            need(dve, V.did(dve.reciprocal(rn[:, 1, lo:hi], rn[:, 0, lo:hi])))
            for t in range(lo, hi):
                added[g] = V.did(dve.scalar_tensor_tensor(out=x_n[:, t, :], in0=hn[:, t, :], scalar=rn[:, 1, t:t + 1],
                                                          in1=x_n[:, t, :], op0=ALU.mult, op1=ALU.add))

        hw = acc[:, XC:XC + NP].rearrange("p (t d) -> p t d", d=D)

        def product_n(g, lo, hi):
            bank = 6 + g % 2
            mm = project(lo, hi, bank, [(hT, WN)], [h_turned[g]] + ([made[g - 2]] if g >= 2 else []))
            need(act, mm)
            made[g] = A.did(act.copy(rows(hw, lo, hi), banked(bank, hi - lo)))
            store_rows(st_2, T2, hw, lo, hi,
                       [with_bias(pool, G, rows(hw, lo, hi), rows(hw, lo, hi), BN, hi - lo, made[g])])

        def finish_only(g, lo, hi):
            relu[g] = rectify(hn, lo, hi, nm[g])

        turner = Turner("B", [work[:, k * 2 * P:(k + 1) * 2 * P].bitcast(I32) for k in range(SLOTS)], None,
                        [work[:, (SLOTS + k) * 2 * P:(SLOTS + k + 1) * 2 * P] for k in range(SLOTS)], (0, 1))

        def beside(stage, f):
            def both(g, lo, hi):
                stage(g, lo, hi)
                if g < CB:
                    f(g)
            return both

        pipeline(beside(combine, turner.gather), beside(product1, turner.turn), beside(bend, turner.keep), norms,
                 add_normed,
                 lambda g, lo, hi: dv.update({g: deviation(lo, hi, statistics(x_of, lo, hi, added[g]))}),
                 lambda g, lo, hi: nm.update({g: normalise(x_of, lambda t: hn[:, t, :], lo, hi, dv[g])}),
                 finish_only,
                 lambda g, lo, hi: turn(g, lo, hi, lambda t: hn[:, t, :], relu[g], h_turned, hT, 2), product_n)
        zeroed = uv["zeroed"]

        over = edge_loop(2, T2, [st_2.mark, zeroed, made[last_g]])
        for e in (pe, dve, act, pool, sp):
            need(e, *over)
        act.preload_act_table_set(EXP_LN)

        rows3 = acc[:, SQ:SQ + NT * ROW3].rearrange("p (t w) -> p t w", w=ROW3)
        h3 = rows3[:, :, HEADS:HEADS + D]
        own = acc[:, XC:XC + NP]
        onehots = own[:, 0:2 * TABB].rearrange("p (g s) -> p g s", g=GB)
        win_b = own[:, 2 * TABB:3 * TABB]
        sc_b = own[:, 3 * TABB:3 * TABB + GB * 2 * P].rearrange("p (g q n) -> p g q n", g=GB, n=WB)
        w3T = own[:, 3600:3600 + HEADS * P].rearrange("p (h f) -> p h f", h=HEADS)
        att = own[:, 4200:4200 + 2 * HEADS]
        spn = [own[:, 4300 + k * GRP:4300 + (k + 1) * GRP] for k in range(2)]
        vs = small[:, 0:2 * HEADS]
        ld_v = Load("ld_v")
        ld_v.add(sp.dma_start(w3T, a["w3T"].rearrange("(h c) f -> c h f", h=HEADS)))
        ld_v.add(sp.dma_start(att[:, 0:HEADS], a["att_srcT"]))
        ld_v.add(sp.dma_start(att[:, HEADS:], a["att_dstT"]))
        ld_v.add(sp.dma_start(win_b, windows_b.to_broadcast([P, TABB])))
        flatA = tabA[:].rearrange("p a n -> p (a n)")
        fresh, selfs = flatA[:, 0:TABB], flatA[:, TABB:2 * TABB]

        z1, f1, f2, added, st, nm, relu, h_turned = ({} for _ in range(8))

        biased = {}

        def product_1(g, lo, hi):
            biased[g] = with_bias(pool, G, rows(x_n, lo, hi), rows(x_n, lo, hi), BF2, hi - lo, (s_mm, base["mm"]))
            if g >= 2:
                need(pe, f1[g - 2])
            z1[g] = T.did(pe.matmul(ps[:, g % 2, 0:(hi - lo) * P], WF1, lap_of(lo, hi), start=True, stop=True))

        def soft(g, lo, hi):
            w = (hi - lo) * P
            z = ps[:, g % 2, 0:w]
            need(act, z1[g])
            for j, (dst, src, f, bb, sc) in enumerate(softplus_part(z, bcol[:, 3:4])):
                if j:
                    need(act, m)
                if j == 2 and g >= 1:
                    need(act, f1[g - 1])
                m = A.did(act.activation(dst[:, 0:w], src if j == 0 else src[:, 0:w], f, bias=bb, scale=sc))
            need(dve, m)
            if g >= 2:
                need(dve, f2[g - 2])
            f1[g] = V.did(dve.scalar_tensor_tensor(out=spn[g % 2][:, 0:w], in0=z, scalar=bcol[:, 5:6],
                                                   in1=al[:, 0:w], op0=ALU.add, op1=ALU.max))

        def product_2(g, lo, hi):
            bank = 4 + g % 2
            need(pe, f1[g])
            if g >= 2:
                need(pe, added[g - 2])
            for t in range(lo, hi):
                last = pe.matmul(ps[:, bank, (t - lo) * D:(t - lo + 1) * D],
                                 spn[g % 2][:, (t - lo) * P:(t - lo + 1) * P], WF2, start=True, stop=True)
            f2[g] = T.did(last)
            need(dve, biased[g])
            added[g] = add_to_x(lo, hi, bank, f2[g])

        pipeline(product_1, soft, product_2, lambda g, lo, hi: st.update({g: statistics(x_of, lo, hi, added[g])}))
        need(sp, f2[last_g])
        W3 = wts[:, 0:HEADS, :].rearrange("p h c -> p (h c)")
        GAMMA, BETA, BIAS3 = wts[:, 4, :], wts[:, 5, :], bias[:, 0, :]
        ld_3 = Load("ld_3")
        ld_3.add(sp.dma_start(W3, a["w3"]))
        ld_3.add(sp.dma_start(GAMMA, a["gamma3"].to_broadcast([P, D])))
        ld_3.add(sp.dma_start(BETA, a["beta3"].to_broadcast([P, D])))
        ld_3.add(sp.dma_start(BIAS3, a["bias3"].to_broadcast([P, D])))


        tw = [hT[:, k * 512:(k + 1) * 512] for k in range(2)]
        ex = [hT[:, 1024 + k * 1024:1024 + (k + 1) * 1024] for k in range(2)]
        pw = [hT[:, 3072 + k * 512:3072 + (k + 1) * 512] for k in range(2)]
        ads = hT[:, 4 * TABB:6 * TABB].rearrange("p (j s) -> p j s", j=2)
        scr = hT[:, 6 * TABB:6 * TABB + 128]
        corr = scr[:, 0:RINGB * QUAD].rearrange("p (q k) -> p q k", q=RINGB)
        run = [scr[:, 24 + 10 * k:34 + 10 * k].rearrange("p (j n) -> p j n", j=2) for k in range(2)]
        top = [scr[:, 44 + 4 * k:48 + 4 * k] for k in range(2)]
        mx = [scr[:, 52 + 8 * k:60 + 8 * k].rearrange("p (j n) -> p j n", j=2) for k in range(2)]
        off = [scr[:, 68 + 8 * k:76 + 8 * k].rearrange("p (j n) -> p j n", j=2) for k in range(2)]
        drop = [scr[:, 84 + 4 * k:88 + 4 * k] for k in range(2)]
        pen = [wts[:, 6 + k, :].rearrange("p (k n) -> p k n", k=QUAD) for k in range(2)]

        need(pe, ld_v.mark, *st.values())
        for q in range(2 * HEADS):
            last = pe.matmul(ps[:, 2, q:q + 1], w3T[:, q % HEADS, :], att[:, q:q + 1], start=True, stop=True)
        m = T.did(last)
        need(act, m)
        m_vs = A.did(act.copy(vs, ps[:, 2, 0:2 * HEADS]))
        need(pe, m_vs)
        m_dev = deviation(0, NT, st[last_g])
        m_one = V.did(dve.memset(rows3[:, :, HEADS + D:ROW3], 1.0))
        need(dve, ld_v.mark)
        V.did(dve.memset(fresh[:, 0:1], FAR))
        m = V.did(dve.tensor_tensor(out=fresh[:, 1:TABB], in0=win_b[:, 1:TABB], in1=win_b[:, 0:TABB - 1],
                                    op=ALU.is_equal))
        need(dve, m)
        V.did(dve.tensor_scalar(fresh[:, 1:TABB], fresh[:, 1:TABB], 1.0, -FAR, ALU.subtract, ALU.mult))
        lb, _ = cols["limB"]
        for grp in range(GB):
            c0 = lb + 2 * grp + 1
            m_hot = V.did(dve.tensor_scalar(onehots[0:PB, grp, :], win_b[0:PB, :], 1.0, cst[0:PB, c0:c0 + 1],
                                            ALU.subtract, ALU.is_equal))
        rowbuf = acc[0:2 * HEADS, 0:NP]
        st_3 = Load("st_3")
        kept_h, score, sc_row = {}, {}, {}

        def norm_rows(g, lo, hi):
            nm[g] = normalise(x_of, lambda t: rows3[:, t, HEADS:HEADS + D], lo, hi, m_dev)

        def relu_rows(g, lo, hi):
            relu[g] = rectify(h3, lo, hi, nm[g])
            need(pool, relu[g])
            kept_h[g] = G.did(pool.tensor_tensor(out=rows(x_n, lo, hi), in0=rows(x_n, lo, hi), in1=rows(h3, lo, hi),
                                                 op=ALU.add))

        def scores_of(g, lo, hi):
            need(pe, h_turned[g])
            if g >= 2:
                need(pe, sc_row[g - 2])
            w = (hi - lo) * P
            for t in range(lo, hi):
                pe.matmul(ps[:, 6 + g % 2, (t - lo) * HEADS:(t - lo + 1) * HEADS], hT[:, t * P:(t + 1) * P],
                          vs[:, 0:HEADS], start=True, stop=True)
            m = T.did(pe.matmul(ps[0:2 * HEADS, g % 2, 0:w], vs, hT[:, lo * P:hi * P], start=True, stop=True))
            need(act, m)
            score[g] = A.did(act.copy(rows3[:, lo:hi, 0:HEADS], ps[:, 6 + g % 2, 0:(hi - lo) * HEADS]
                                      .rearrange("p (t h) -> p t h", h=HEADS)))
            sc_row[g] = A.did(act.copy(rowbuf[:, lo * P:hi * P], ps[0:2 * HEADS, g % 2, 0:w]))
            store_rows(st_3, T3, rows3, lo, hi, [score[g], m_one])

        pipeline(norm_rows, relu_rows,
                 lambda g, lo, hi: turn(g, lo, hi, lambda t: rows3[:, t, HEADS:HEADS + D], relu[g], h_turned, hT, 2),
                 scores_of)
        need(sp, sc_row[last_g])
        st_s = Load("st_s")
        need(sp, st_s.add(sp.dma_start(scores, rowbuf)))
        ld_s = Load("ld_s")
        for grp in range(GB):
            ld_s.add(sp.dma_start(sc_b[0:PB, grp, :, :], scores.rearrange("q (b n) -> b q n", n=WB)
                                  [grp * PB:(grp + 1) * PB]))
        slots3 = work[:, 0:RINGB * QUAD * ROW3].rearrange("p (q k w) -> p q k w", q=RINGB, k=QUAD)
        b_idx = base["idx"]

        def at(i, q, mult, extra=0):
            return mult * q + extra if i is None else i * (mult * RINGB) + (mult * q + extra)

        def sl(i, q):
            return bass.ds(at(i, q, QUAD), QUAD) if i is not None else slice(QUAD * q, QUAD * q + QUAD)

        def stage3(i, q):
            act.copy(stage[:, q % RINGB, :], idxB[:, sl(i, q)]).then_inc(s_idx, 1)

        def gather3(i, q):
            pool.wait_ge(s_idx, at(i, q, 1, b_idx + 1))
            pool.sem_inc(s_go, 1)
            for k in range(QUAD):
                pool.indirect_dma_start(
                    out=slots3[:, q % RINGB, k, :], out_offset=None, in_=T3,
                    in_offset=bass.IndirectOffsetOnAxis(ap=stage[:, q % RINGB, k:k + 1], axis=0))\
                    .then_inc(s_g[q % RINGB], 16)

        need(pool, st_3.mark)
        for q in range(RINGB):
            stage3(None, q)
            gather3(None, q)

        need(pe, m_hot, ld_s.mark, sc_row[last_g])
        for j in range(2):
            for half in range(2):
                for grp in range(GB):
                    q0 = HEADS * (1 - j)
                    last = pe.matmul(ps[:, 4 + 2 * j + half, :],
                                     sc_b[0:PB, grp, q0:q0 + HEADS, :].rearrange("p q n -> p (q n)"),
                                     onehots[0:PB, grp, half * 512:(half + 1) * 512],
                                     start=(grp == 0), stop=(grp == GB - 1))
        m_pt = T.did(last)
        need(dve, m_pt)
        for j in range(2):
            V.did(dve.tensor_scalar(ads[:, j, :].rearrange("p (b n) -> p b n", b=2), ps[:, 4:6, :],
                                    1.0 if j == 0 else 0.2, None, ALU.mult))
        V.did(dve.tensor_copy(selfs.rearrange("p (b n) -> p b n", b=2), ps[:, 6:8, :]))
        m_tab = V.did(dve.memset(run[0][:, 0, 0:1], 0.0))
        m_res = kept_h[last_g]
        need(dve, ld_3.mark)
        acc3 = acc[:].rearrange("p (b w) -> p b w", w=ACC3)
        need(sp, st_3.mark, m_res, ld_3.mark)
        ld_q, ld_a = Load("ld_q"), Load("ld_a")
        by_window = T3.rearrange("(b n) w -> n b w", n=WB)
        QTR = BB // 4
        assert QTR * 4 == BB and QTR * ACC3 <= XC and XC + 4300 + 2 * GRP <= 2 * QTR * ACC3
        EARLY = QTR // (QUAD * RINGB)
        for b0 in (0, 2 * QTR, 3 * QTR, QTR):
            if b0 == 2 * QTR:
                need(sp, (s_g[RINGB - 1], base_g[RINGB - 1] + 64))
            if b0 == QTR:
                need(sp, m_pt, m_tab)
            for h in range(HEADS):
                (ld_q if b0 == 0 else ld_a).add(sp.dma_start(acc3[h * WB:(h + 1) * WB, b0:b0 + QTR, :],
                                                             by_window[:, b0:b0 + QTR, HEADS:ROW3]))

        PT, PB_, OUT = 0, 2, 4
        s_pt, s_ex, s_pm, s_pb, s_cp, s_out = (sem(n) for n in ("s_pt", "s_ex", "s_pm", "s_pb", "s_cp", "s_out"))
        CHAIN = 10
        s_head = [sem(f"s_head{k}") for k in range(3)]
        s_link = [sem(f"s_link{k}") for k in range(CHAIN)]
        s_add = [sem(f"s_add{k}") for k in range(QUAD)]
        C = 2
        for e, mine in ((dve, (*s_head, *s_link, *s_add, s_pm)), (pe, (s_pt, s_pb, s_out)), (act, (s_ex, s_cp))):
            need(e, m_tab, (st_3.sem, st_3.n), (s_mm, base["mm"]))
            for s in mine:
                e.sem_inc(s, C)

        def slot3(i, q, offs):
            head, chain, weigh, sum_up, add = q + 4, q + 3, q + 2, q + 1, q
            if i is None:
                chain, weigh, sum_up, add = (x if x >= 0 else None for x in (chain, weigh, sum_up, add))

            def add_step(k):
                if add is None:
                    return
                if k == 0:
                    dve.wait_ge(s_out, at(i, add, 1, C + 1))
                dve.wait_ge(s_add[k - 1], at(i, add, 1, C + (k > 0)))
                bank = OUT + 2 * (add % 2) + k // 2
                o = acc[:, bass.ds(offs[k], ACC3)]
                dve.scalar_tensor_tensor(out=o, in0=o, scalar=corr[:, add % RINGB, k:k + 1],
                                         in1=ps[:, bank, (k % 2) * ACC3:(k % 2 + 1) * ACC3],
                                         op0=ALU.mult, op1=ALU.add).then_inc(s_add[k], 1)

            hp = head % 2

            def head_step(k):
                if k == 0:
                    dve.wait_ge(s_pt, at(i, head, 1, C - 1))
                    dve.tensor_tensor(out=pen[hp], in0=iota[:, 0:WB].unsqueeze(1).to_broadcast([P, QUAD, WB]),
                                      in1=relB[:, sl(i, head)].unsqueeze(2).to_broadcast([P, QUAD, WB]),
                                      op=ALU.is_equal).then_inc(s_head[0], 1)
                elif k == 1:
                    dve.wait_ge(s_head[0], at(i, head, 1, C + 1))
                    dve.tensor_scalar(pen[hp], pen[hp], 1.0, -FAR, ALU.subtract, ALU.mult).then_inc(s_head[1], 1)
                else:
                    dve.wait_ge(s_g[head % RINGB], base_g[head % RINGB] + 64 * (head // RINGB + 1) if i is None else
                                i * 64 + (base_g[head % RINGB] + 64 * (head // RINGB + 1)))
                    dve.wait_ge(s_head[1], at(i, head, 1, C + 1))
                    dve.tensor_tensor(
                        out=tw[hp].rearrange("p (k h n) -> p k h n", k=QUAD, h=HEADS),
                        in0=slots3[:, head % RINGB, :, 0:HEADS].unsqueeze(3).to_broadcast([P, QUAD, HEADS, WB]),
                        in1=pen[hp].unsqueeze(2).to_broadcast([P, QUAD, HEADS, WB]), op=ALU.add).then_inc(s_head[2], 1)

            if weigh is not None:
                wp = weigh % 2
                e1, e2 = ex[wp][:, 0:512], ex[wp][:, 512:1024]

            def weigh_step():
                if weigh is not None:
                    dve.wait_ge(s_ex, at(i, weigh, 1, C + 1))
                    dve.tensor_tensor(out=e1, in0=e1, in1=e2, op=ALU.max).then_inc(s_pm, 1)

            fill = {1: lambda: head_step(0), 2: lambda: add_step(0), 3: lambda: head_step(1),
                    5: lambda: head_step(2), 6: lambda: add_step(1), 7: weigh_step,
                    8: lambda: add_step(2), 10: lambda: add_step(3)}
            if chain is None:
                for k in range(3):
                    head_step(k)

            if chain is not None:
                cp = chain % 2
                table = sl(i, chain)
                step = [0]

                def link(ins, awaited=True):
                    mine = s_link[step[0]]
                    ins.then_inc(mine, 1)
                    step[0] += 1
                    if step[0] in fill:
                        fill[step[0]]()
                    if awaited:
                        dve.wait_ge(mine, at(i, chain, 1, C + 1))

                r, b = top[cp], run[cp]
                dve.wait_ge(s_pt, at(i, chain, 1, C + 1))
                dve.wait_ge(s_link[-1], at(i, chain, 1, C))
                link(dve.tensor_reduce(r, ps[:, PT + cp, :].rearrange("p (k e) -> p k e", k=QUAD), AX.X, ALU.max))
                link(dve.tensor_tensor(out=r, in0=r, in1=selfs[:, table], op=ALU.max))
                link(dve.tensor_tensor_scan(out=b[:, 0, 1:5], data0=fresh[:, table], data1=r,
                                            initial=b[:, 0, 0:1], op0=ALU.add, op1=ALU.max))
                link(dve.tensor_copy(run[1 - cp][:, 0, 0:1], b[:, 0, 4:5]), False)
                link(dve.tensor_tensor(out=b[:, 1, 1:5], in0=b[:, 0, 0:4], in1=fresh[:, table], op=ALU.add))
                link(dve.tensor_tensor(out=b[:, 1, 1:5], in0=b[:, 1, 1:5], in1=selfs[:, table], op=ALU.max))
                mm = mx[cp]
                link(dve.tensor_tensor(out=mm, in0=b[:, :, 1:5],
                                       in1=ads[:, 0, table].unsqueeze(1).to_broadcast([P, 2, QUAD]), op=ALU.add))
                link(dve.scalar_tensor_tensor(out=mm, in0=mm, scalar=0.2, in1=mm, op0=ALU.mult, op1=ALU.max))
                link(dve.tensor_tensor(out=drop[cp], in0=mm[:, 1, :], in1=mm[:, 0, :], op=ALU.subtract), False)
                link(dve.tensor_tensor(out=off[cp], in0=ads[:, :, table],
                                       in1=mm[:, 0:1, :].to_broadcast([P, 2, QUAD]), op=ALU.subtract), False)
                act.wait_ge(s_link[-1], at(i, chain, 1, C + 1))
                act.wait_ge(s_pm, at(i, chain, 1, C - 1))
                act.wait_ge(s_pb, at(i, chain, 1, C - 1))
                act.activation(corr[:, chain % RINGB, :], drop[cp], ACT.Exp)
                for j in range(2):
                    for k in range(QUAD):
                        last = act.activation(ex[cp][:, j * 512 + k * P:j * 512 + (k + 1) * P],
                                              ps[:, PT + cp, k * P:(k + 1) * P], ACT.Exp,
                                              bias=off[cp][:, j, k:k + 1], scale=1.0 if j == 0 else 0.2)
                last.then_inc(s_ex, 1)

            pe.wait_ge(s_head[2], at(i, head, 1, C + 1))
            pe.wait_ge(s_ex, at(i, head, 1, C - 1))
            for k in range(QUAD):
                last = pe.transpose(ps[:, PT + hp, k * P:(k + 1) * P], tw[hp][:, k * P:(k + 1) * P], ident)
            last.then_inc(s_pt, 1)

            if sum_up is not None:
                pe.wait_ge(s_cp, at(i, sum_up, 1, C + 1))
                pe.wait_ge(s_add[-1], at(i, sum_up, 1, C - 1))
                for k in range(QUAD):
                    bank = OUT + 2 * (sum_up % 2) + k // 2
                    o = ps[:, bank, (k % 2) * ACC3:(k % 2 + 1) * ACC3]
                    last = pe.matmul(o, pw[sum_up % 2][:, k * P:(k + 1) * P],
                                     slots3[:, sum_up % RINGB, k, HEADS:ROW3], start=True, stop=True)
                last.then_inc(s_out, 1)

            if weigh is not None:
                pe.wait_ge(s_pm, at(i, weigh, 1, C + 1))
                pe.wait_ge(s_cp, at(i, weigh, 1, C - 1))
                for k in range(QUAD):
                    last = pe.transpose(ps[:, PB_ + wp, k * P:(k + 1) * P], e1[:, k * P:(k + 1) * P], ident)
                last.then_inc(s_pb, 1)
                act.wait_ge(s_pb, at(i, weigh, 1, C + 1))
                act.wait_ge(s_out, at(i, weigh, 1, C - 1))
                act.copy(pw[wp], ps[:, PB_ + wp, :]).then_inc(s_cp, 1)

        for q in range(-4, 0):
            slot3(None, q, None)
        act.wait_ge(s_out, C + 1)
        stage3(None, RINGB)
        gather3(None, RINGB)
        for first_it, end_it, loaded in ((0, EARLY, ld_q), (EARLY, ITERSB, ld_a)):
            need(dve, loaded.mark)
            with nc.Fori(first_it, end_it) as i:
                for q in range(RINGB):
                    if q % 3 == 0:
                        _, offs = nc.values_load_multi_w_load_instructions(
                            winB[0:1, bass.ds(at(i, q, QUAD), 3 * QUAD)], engines=[ENG.DVE], min_val=0,
                            max_val=(BB - 1) * ACC3,
                            skip_runtime_bounds_check_because="b_s counts the windows that have started")
                    slot3(i, q, offs[q % 3 * QUAD:(q % 3 + 1) * QUAD])
                    act.wait_ge(s_out, at(i, q + 1, 1, C + 1))
                    stage3(i, q + 1 + RINGB)
                    gather3(i, q + 1 + RINGB)
        quads = RINGB * ITERSB
        for q in range(RINGB):
            need(dve, (s_g[q], base_g[q] + 64 * (ITERSB + 1 + (q == 0))))
        need(dve, (s_add[-1], C + quads), (s_pt, C + quads + 4), (s_pb, C + quads + 2),
             (s_ex, C + quads + 3), (s_out, C + quads + 1), (s_cp, C + quads + 2), (s_idx, b_idx + quads + RINGB + 1))

        zr = flatA[:, 0:BB]
        m = V.did(dve.tensor_scalar(zr, acc3[:, :, D], float(HEADS), None, ALU.mult))
        need(dve, m)
        m = V.did(dve.reciprocal(zr, zr))
        need(dve, m)
        turned_w = [flatA[:, 256 + 512 * k:768 + 512 * k] for k in range(2)]
        WPT = P // WB
        gat = hT[:, 0:NP].rearrange("p (t d) -> p t d", d=D)
        need(act, m)
        need(pool, m)
        st_out = Load("st_out")
        scaled, w_turned, w_free, gat_done, drawn, dv, nm, shifted = ({} for _ in range(8))

        def scale_sums(g, lo, hi):
            s4 = slice(WPT * lo, WPT * hi)
            scaled[g] = V.did(dve.tensor_tensor(
                out=acc3[:, s4, 0:D], in0=acc3[:, s4, 0:D],
                in1=zr[:, s4].unsqueeze(2).to_broadcast([P, WPT * (hi - lo), D]), op=ALU.mult))

        def turn_windows(t):
            if t >= 2:
                need(pe, w_turned[t - 2])
            for w in range(WPT):
                last = pe.transpose(ps[:, t % 2, w * P:(w + 1) * P], acc3[:, t * WPT + w, 0:D], ident)
            need(act, T.did(last))
            if t >= 2:
                need(act, w_free[t - 2])
            w_turned[t] = A.did(act.copy(
                turned_w[t % 2].rearrange("p (h w n) -> p w h n", h=HEADS, w=WPT),
                ps[:, t % 2, :].rearrange("p (w h n) -> p w h n", w=WPT, h=HEADS)))

        def heads(g, lo, hi):
            need(pe, scaled[g])
            if g >= 2:
                need(pe, drawn[g - 2])
            bank = 4 + g % 2
            for t in range(lo, hi + 1):
                if t < hi:
                    turn_windows(t)
                if t > lo:
                    u = t - 1
                    o = ps[:, bank, (u - lo) * D:(u - lo + 1) * D]
                    need(pe, w_turned[u])
                    for h in range(HEADS):
                        last = pe.matmul(o, turned_w[u % 2][:, h * P:(h + 1) * P], W3[:, h * D:(h + 1) * D],
                                         start=(h == 0), stop=(h == HEADS - 1))
                    w_free[u] = T.did(last)
            gat_done[g] = w_free[hi - 1]

        def gat_of(t):
            return gat[:, t, :]

        def draw(g, lo, hi):
            drawn[g] = with_bias(dve, V, rows(gat, lo, hi), banked(4 + g % 2, hi - lo), BIAS3, hi - lo, gat_done[g])

        def measure3(g, lo, hi):
            dv[g] = deviation(lo, hi, statistics(gat_of, lo, hi, drawn[g]))

        def norm3(g, lo, hi):
            need(dve, dv[g])
            need(dve, V.did(dve.reciprocal(dev[:, 1, lo:hi], dev[:, 0, lo:hi])))
            need(act, V.did(dve.scalar_tensor_tensor(out=rn[:, 0, lo:hi], in0=meanvar[:, lo:hi, 0], scalar=-1.0,
                                                     in1=dev[:, 1, lo:hi], op0=ALU.mult, op1=ALU.mult)))
            for t in range(lo, hi):
                nm[g] = A.did(act.activation(gat_of(t), gat_of(t), ACT.Identity, bias=rn[:, 0, t:t + 1],
                                             scale=dev[:, 1, t:t + 1]))

        def affine(g, lo, hi):
            m = nm[g]
            for vec, op in ((GAMMA, ALU.mult), (BETA, ALU.add)):
                need(pool, m)
                m = G.did(pool.tensor_tensor(out=rows(gat, lo, hi), in0=rows(gat, lo, hi),
                                             in1=vec.unsqueeze(1).to_broadcast([P, hi - lo, D]), op=op))
            shifted[g] = m

        def result(g, lo, hi):
            need(dve, shifted[g])
            m = V.did(dve.scalar_tensor_tensor(out=rows(x_n, lo, hi), in0=rows(gat, lo, hi), scalar=0.0,
                                               in1=rows(x_n, lo, hi), op0=ALU.max, op1=ALU.add))
            need(sp, m)
            full = min(hi, NT - 1)
            if full > lo:
                st_out.add(sp.dma_start(out[lo * P:full * P, :].rearrange("(t p) d -> p t d", p=P),
                                        rows(x_n, lo, full)))
            if hi == NT:
                st_out.add(sp.dma_start(out[(NT - 1) * P:N, :], x_n[0:LAST, NT - 1, :]))

        pipeline(scale_sums, heads, draw, measure3, norm3, affine, result)
        need(sp, st_out.mark)


def kernel(**inputs):
    import concourse.bacc as bacc
    from concourse.bass_utils import run_bass_kernel_spmd

    def arr(name):
        return np.asarray(inputs[name])

    pad = ROWS * P - E
    src = np.concatenate([arr("src"), np.zeros(pad, np.int32)]).reshape(ROWS, P)
    dst = np.concatenate([arr("dst"), np.full(pad, 1 << 20, np.int32)]).reshape(ROWS, P)
    arrays = {
        "x": arr("x"),
        "edges": np.concatenate([src, dst], axis=1),
        "lasts": dst[:, P - 1].reshape(1, ROWS),
        "weights": np.concatenate([arr("edge_weight"), np.zeros(pad, np.float32)]).reshape(ROWS, P),
        "edge_attrT": np.concatenate([arr("edge_attr_128").T, np.zeros((P, ECOLS - E), np.float32)], axis=1),
        "consts": const_table(), "steps": np.arange(TABB, dtype=np.float32).reshape(1, TABB),
        "w0": arr("L0_gnn_weight"), "w1": arr("L1_gnn_W1"), "w2": arr("L1_gnn_W2"),
        "wnT": arr("L2_gnn_W_node").T, "we1T": arr("L2_gnn_W_e1").T, "we2T": arr("L2_gnn_W_e2").T,
        "wf1T": arr("L2_gnn_W_fc1").T, "wf2T": arr("L2_gnn_W_fc2").T,
        "w3": arr("L3_gnn_W"), "w3T": arr("L3_gnn_W").T,
        "att_srcT": arr("L3_gnn_att_src").T, "att_dstT": arr("L3_gnn_att_dst").T,
        "b0": arr("L0_gnn_b").reshape(1, D), "b1a": arr("L1_gnn_b1"), "b1b": arr("L1_gnn_b2"),
        "bn": arr("L2_gnn_b_node").reshape(1, D), "bf2": arr("L2_gnn_b_fc2").reshape(1, D),
        "be2": arr("L2_gnn_b_e2").reshape(1, D),
        "be1": arr("L2_gnn_b_e1").reshape(D, 1), "bf1": arr("L2_gnn_b_fc1").reshape(D, 1),
        "bias3": arr("L3_gnn_bias").reshape(1, D), "gamma3": arr("L3_gnn_ln_gamma").reshape(1, D),
        "beta3": arr("L3_gnn_ln_beta").reshape(1, D),
    }
    arrays = {"in_" + k: np.ascontiguousarray(v) for k, v in arrays.items()}
    nc = bacc.Bacc("TRN2", target_bir_lowering=False, num_devices=1)
    aps = {k[3:]: nc.dram_tensor(k, v.shape, mybir.dt.from_np(v.dtype), kind="ExternalInput").ap()
           for k, v in arrays.items()}
    out = nc.dram_tensor("out", (N, D), F32, kind="ExternalOutput").ap()
    build(nc, aps, out)
    r = run_bass_kernel_spmd(nc, [arrays], core_ids=[0])
    return r.results[0]["out"]
```
